# Optimizing a Trainium2 kernel written in Bass

```python
import numpy as np
import jax
import jax.numpy as jnp

def _softmax(x, axis=-1):
    return jax.nn.softmax(x, axis=axis)

def _gelu(x):
    return jax.nn.gelu(x, approximate=True)

def _silu(x):
    return jax.nn.silu(x)

def _sigmoid(x):
    return jax.nn.sigmoid(x)

def _layernorm(x, axis=-1, eps=1e-05):
    m = jnp.mean(x, axis=axis, keepdims=True)
    v = jnp.var(x, axis=axis, keepdims=True)
    return (x - m) / jnp.sqrt(v + eps)

def _scatter_add(tgt, idx, src, axis=0):
    return tgt.at[idx].add(src)

def _segment_sum(src, seg, n):
    return jax.ops.segment_sum(src, seg, n)
kernel_name = 'mk_gnn_ffn_d2_gnn_r8_4d6b20'

def setup_inputs(seed: int=0):
    np.random.seed(seed)
    _w = jnp.asarray

    def _rec_inputs():
        import jax
        import jax.numpy as jnp
        _gk = jax.random.key(seed)
        x = -0.0002117 + 1 * jax.random.normal(jax.random.fold_in(_gk, 1), (1250, 512), jnp.float32)
        _s = jax.random.randint(jax.random.fold_in(_gk, 2), (10000,), 0, 1250, jnp.int32)
        _d = jax.random.randint(jax.random.fold_in(_gk, 3), (10000,), 0, 1250, jnp.int32)
        _loop = jnp.arange(1250, dtype=jnp.int32)
        src = jnp.concatenate([_s, _d, _loop])
        dst = jnp.concatenate([_d, _s, _loop])
        _o = jnp.argsort(dst, stable=True)
        src = src[_o]
        dst = dst[_o]
        return (x, src, dst)
    x, src, dst = _rec_inputs()

    def _L0_gnn_setup():
        import jax, jax.numpy as jnp
        import numpy as np
        N = 6250
        E = 100000
        D = 512

        def _gcn_conv(x, edge_index, W, b):
            n = x.shape[0]
            xw = x @ W.T
            loop = jnp.arange(n, dtype=edge_index.dtype)
            row = jnp.concatenate([edge_index[0], loop])
            col = jnp.concatenate([edge_index[1], loop])
            deg = jax.ops.segment_sum(jnp.ones_like(row, dtype=xw.dtype), col, num_segments=n)
            dinv = jnp.where(deg > 0, jax.lax.rsqrt(deg), 0.0)
            norm = dinv[row] * dinv[col]
            msgs = norm[:, None] * xw[row]
            out = jax.ops.segment_sum(msgs, col, num_segments=n)
            return out + b

        def _batch_norm(h, gamma, beta, eps=1e-05):
            mean = jnp.mean(h, axis=0)
            var = jnp.var(h, axis=0)
            return (h - mean) * jax.lax.rsqrt(var + eps) * gamma + beta
        key = jax.random.key(seed)
        k1, k2, k3, k4, k5, k6 = jax.random.split(key, 6)
        x = jax.random.normal(k1, (N, D), dtype=jnp.float32)
        edge_index = jax.random.randint(k2, (2, E), 0, N, dtype=jnp.int64)
        W = jax.random.normal(k3, (D, D), dtype=jnp.float32) * (1.0 / np.sqrt(D))
        b = jnp.zeros((D,), dtype=jnp.float32)
        gamma = jnp.ones((D,), dtype=jnp.float32)
        beta = jnp.zeros((D,), dtype=jnp.float32)
        return {'x': x, 'edge_index': edge_index, 'W': W, 'b': b, 'gamma': gamma, 'beta': beta}
    _L0_gnn_all = _L0_gnn_setup()
    _L0_gnn_in = {k: v for k, v in _L0_gnn_all.items() if k in ('W', 'b', 'gamma', 'beta')}
    del _L0_gnn_all

    def _L0_ffn_setup():
        import jax, jax.numpy as jnp
        import numpy as np
        from jax import lax
        N_HEADS = 8
        D_KEYS = 128
        HALF = D_KEYS // 2
        N_KEYS = 256
        TOP_K = 8
        D_MODEL = 512

        def _forward(queries, Wq, bq, keys, w_down, w_up):
            N, T, D = queries.shape
            x = queries.reshape(-1, D)
            q = (x @ Wq + bq).reshape(-1, N_HEADS, D_KEYS)
            q1, q2 = (q[..., :HALF], q[..., HALF:])
            s1 = jnp.einsum('bhc,hnc->bhn', q1, keys[:, 0])
            s2 = jnp.einsum('bhc,hnc->bhn', q2, keys[:, 1])
            s1t, i1 = lax.top_k(s1, TOP_K)
            s2t, i2 = lax.top_k(s2, TOP_K)
            all_scores = (s1t[..., :, None] + s2t[..., None, :]).reshape(-1, N_HEADS, TOP_K * TOP_K)
            all_idx = (i1[..., :, None] * N_KEYS + i2[..., None, :]).reshape(-1, N_HEADS, TOP_K * TOP_K)
            scores, best = lax.top_k(all_scores, TOP_K)
            indices = jnp.take_along_axis(all_idx, best, axis=-1)
            w_d = w_down[indices]
            w_u = w_up[indices]
            inner = jnp.einsum('bd,bhkd->bhk', x, w_d)
            vals = jax.nn.relu(inner) * jax.nn.softmax(scores, axis=-1)
            out = jnp.einsum('bhk,bhkd->bd', vals, w_u)
            return out.reshape(N, T, D)
        key = jax.random.key(seed)
        ks = jax.random.split(key, 6)
        N, T = (2, 1024)
        queries = jax.random.normal(ks[0], (N, T, D_MODEL), dtype=jnp.float32)
        Wq = jax.random.normal(ks[1], (D_MODEL, N_HEADS * D_KEYS), dtype=jnp.float32) / np.sqrt(D_MODEL)
        bq = jnp.zeros((N_HEADS * D_KEYS,), dtype=jnp.float32)
        bound = 1.0 / np.sqrt(HALF)
        keys = jax.random.uniform(ks[2], (N_HEADS, 2, N_KEYS, HALF), dtype=jnp.float32, minval=-bound, maxval=bound)
        w_down = jax.random.normal(ks[3], (N_KEYS * N_KEYS, D_MODEL), dtype=jnp.float32) * 0.02
        w_up = jax.random.normal(ks[4], (N_KEYS * N_KEYS, D_MODEL), dtype=jnp.float32) * 0.02
        return {'queries': queries, 'Wq': Wq, 'bq': bq, 'keys': keys, 'w_down': w_down, 'w_up': w_up}
    _L0_ffn_all = _L0_ffn_setup()
    _L0_ffn_in = {k: v for k, v in _L0_ffn_all.items() if k in ('Wq', 'bq', 'keys', 'w_down', 'w_up')}
    del _L0_ffn_all

    def _L1_gnn_setup():
        import jax, jax.numpy as jnp
        import numpy as np
        N_NODES = 6250
        N_EDGES = 100000
        D = 512
        key = jax.random.key(seed)
        k1, k2, k3, k4 = jax.random.split(key, 4)
        x = jax.random.normal(k1, (N_NODES, D), dtype=jnp.float32)
        W = jax.random.normal(k2, (D, D), dtype=jnp.float32) * (1.0 / np.sqrt(D))
        b = jnp.zeros((D,), dtype=jnp.float32)
        src = jax.random.randint(k3, (N_EDGES,), 0, N_NODES, dtype=jnp.int32)
        dst = jax.random.randint(k4, (N_EDGES,), 0, N_NODES, dtype=jnp.int32)
        return {'x': x, 'W': W, 'b': b, 'src': src, 'dst': dst}
    _L1_gnn_all = _L1_gnn_setup()
    _L1_gnn_in = {k: v for k, v in _L1_gnn_all.items() if k in ('W', 'b')}
    del _L1_gnn_all

    def _L1_ffn_setup():
        import jax, jax.numpy as jnp
        import numpy as np
        BINS = jnp.array([-1.5, -1.0, -0.5, 0.0, 0.5, 1.0, 1.5], dtype=jnp.float32)
        N_BINS = BINS.shape[0] + 1
        INDEX = 0
        key = jax.random.key(seed)
        k1, k2 = jax.random.split(key)
        x = jax.random.normal(k1, (8, 512, 512), dtype=jnp.float32)
        W = jax.random.normal(k2, (N_BINS, 512, 512), dtype=jnp.float32) * 0.02
        return {'x': x, 'W': W}
    _L1_ffn_all = _L1_ffn_setup()
    _L1_ffn_in = {k: v for k, v in _L1_ffn_all.items() if k in ('W',)}
    del _L1_ffn_all
    return {'x': x, 'src': src, 'dst': dst, 'L0_gnn_W': _L0_gnn_in['W'], 'L0_gnn_b': _L0_gnn_in['b'], 'L0_gnn_gamma': _L0_gnn_in['gamma'], 'L0_gnn_beta': _L0_gnn_in['beta'], 'L0_ffn_Wq': _L0_ffn_in['Wq'], 'L0_ffn_bq': _L0_ffn_in['bq'], 'L0_ffn_keys': _L0_ffn_in['keys'], 'L0_ffn_w_down': _L0_ffn_in['w_down'], 'L0_ffn_w_up': _L0_ffn_in['w_up'], 'L1_gnn_W': _L1_gnn_in['W'], 'L1_gnn_b': _L1_gnn_in['b'], 'L1_ffn_W': _L1_ffn_in['W']}

def reference(x, src, dst, L0_gnn_W, L0_gnn_b, L0_gnn_gamma, L0_gnn_beta, L0_ffn_Wq, L0_ffn_bq, L0_ffn_keys, L0_ffn_w_down, L0_ffn_w_up, L1_gnn_W, L1_gnn_b, L1_ffn_W):
    import jax
    import jax.numpy as jnp

    def _L0_gnn_ref(x, edge_index, W, b, gamma, beta):
        import jax, jax.numpy as jnp
        import numpy as np
        N = 6250
        E = 100000
        D = 512

        def _gcn_conv(x, edge_index, W, b):
            n = x.shape[0]
            xw = x @ W.T
            loop = jnp.arange(n, dtype=edge_index.dtype)
            row = jnp.concatenate([edge_index[0], loop])
            col = jnp.concatenate([edge_index[1], loop])
            deg = jax.ops.segment_sum(jnp.ones_like(row, dtype=xw.dtype), col, num_segments=n)
            dinv = jnp.where(deg > 0, jax.lax.rsqrt(deg), 0.0)
            norm = dinv[row] * dinv[col]
            msgs = norm[:, None] * xw[row]
            out = jax.ops.segment_sum(msgs, col, num_segments=n)
            return out + b

        def _batch_norm(h, gamma, beta, eps=1e-05):
            mean = jnp.mean(h, axis=0)
            var = jnp.var(h, axis=0)
            return (h - mean) * jax.lax.rsqrt(var + eps) * gamma + beta
        identity = x
        h = _gcn_conv(x, edge_index, W, b)
        h = _batch_norm(h, gamma, beta)
        h = jax.nn.gelu(h, approximate=False)
        return h + identity

    def _L0_ffn_ref(queries, Wq, bq, keys, w_down, w_up):
        import jax, jax.numpy as jnp
        import numpy as np
        from jax import lax
        N_HEADS = 8
        D_KEYS = 128
        HALF = D_KEYS // 2
        N_KEYS = 256
        TOP_K = 8
        D_MODEL = 512

        def _forward(queries, Wq, bq, keys, w_down, w_up):
            N, T, D = queries.shape
            x = queries.reshape(-1, D)
            q = (x @ Wq + bq).reshape(-1, N_HEADS, D_KEYS)
            q1, q2 = (q[..., :HALF], q[..., HALF:])
            s1 = jnp.einsum('bhc,hnc->bhn', q1, keys[:, 0])
            s2 = jnp.einsum('bhc,hnc->bhn', q2, keys[:, 1])
            s1t, i1 = lax.top_k(s1, TOP_K)
            s2t, i2 = lax.top_k(s2, TOP_K)
            all_scores = (s1t[..., :, None] + s2t[..., None, :]).reshape(-1, N_HEADS, TOP_K * TOP_K)
            all_idx = (i1[..., :, None] * N_KEYS + i2[..., None, :]).reshape(-1, N_HEADS, TOP_K * TOP_K)
            scores, best = lax.top_k(all_scores, TOP_K)
            indices = jnp.take_along_axis(all_idx, best, axis=-1)
            w_d = w_down[indices]
            w_u = w_up[indices]
            inner = jnp.einsum('bd,bhkd->bhk', x, w_d)
            vals = jax.nn.relu(inner) * jax.nn.softmax(scores, axis=-1)
            out = jnp.einsum('bhk,bhkd->bd', vals, w_u)
            return out.reshape(N, T, D)
        return _forward(queries, Wq, bq, keys, w_down, w_up)

    def _L1_gnn_ref(x, W, b, src, dst):
        import jax, jax.numpy as jnp
        import numpy as np
        N_NODES = 6250
        N_EDGES = 100000
        D = 512
        N = x.shape[0]
        ones = jnp.ones(src.shape[0], dtype=x.dtype)
        deg_out = jnp.clip(jax.ops.segment_sum(ones, src, num_segments=N), 1.0)
        deg_in = jnp.clip(jax.ops.segment_sum(ones, dst, num_segments=N), 1.0)
        h = x * (deg_out ** (-0.5))[:, None]
        agg = jax.ops.segment_sum(h[src], dst, num_segments=N)
        agg = agg * (deg_in ** (-0.5))[:, None]
        return agg @ W + b

    def _L1_ffn_ref(x, W):
        import jax, jax.numpy as jnp
        import numpy as np
        BINS = jnp.array([-1.5, -1.0, -0.5, 0.0, 0.5, 1.0, 1.5], dtype=jnp.float32)
        N_BINS = BINS.shape[0] + 1
        INDEX = 0
        y = x[..., INDEX]
        mem = jnp.sum(y[..., None] > BINS, axis=-1)
        B, T, D = x.shape
        xf = x.reshape(B * T, D)
        memf = mem.reshape(B * T)
        out = jnp.zeros((B * T, W.shape[-1]), dtype=x.dtype)
        for k in range(N_BINS):
            sel = (memf == k)[:, None].astype(x.dtype)
            out = out + sel * (xf @ W[k])
        return out.reshape(B, T, W.shape[-1])
    edge_index = jnp.stack([src, dst])
    x = x + _L0_gnn_ref(_layernorm(x, axis=-1), edge_index, L0_gnn_W, L0_gnn_b, L0_gnn_gamma, L0_gnn_beta)
    x = x + _L0_ffn_ref(_layernorm(x, axis=-1)[None], L0_ffn_Wq, L0_ffn_bq, L0_ffn_keys, L0_ffn_w_down, L0_ffn_w_up)[0]
    x = x + _L1_gnn_ref(_layernorm(x, axis=-1), L1_gnn_W, L1_gnn_b, src, dst)
    x = x + _L1_ffn_ref(_layernorm(x, axis=-1)[None], L1_ffn_W)[0]
    return x

_drawn_inputs = setup_inputs


def setup_inputs(seed=0):
    import zlib

    import numpy as np

    out = dict(_drawn_inputs(seed))
    spreads = {'L0_gnn_b': (0.0, 0.8),
     'L0_gnn_gamma': (1.0, 0.2),
     'L0_gnn_beta': (0.0, 0.1),
     'L0_ffn_bq': (0.0, 0.8),
     'L1_gnn_b': (0.0, 0.1)}
    factors = {'L0_ffn_Wq': 4.656, 'L0_ffn_keys': 4.636, 'L0_ffn_w_down': 4.707, 'L0_ffn_w_up': 4.154}
    for name, (base, spread) in spreads.items():
        noise = np.random.default_rng([zlib.crc32(name.encode()), seed]).standard_normal(out[name].shape)
        drawn = base * np.exp(spread * noise) if base else spread * noise
        out[name] = jnp.asarray(drawn.astype(out[name].dtype))
    for name, factor in factors.items():
        out[name] = (out[name] * factor).astype(out[name].dtype)
    return out
```

```python
from contextlib import ExitStack

import numpy as np
import concourse.bass as bass
from concourse import mybir

F32 = mybir.dt.float32
F16 = mybir.dt.float16
I32 = mybir.dt.int32
U32 = mybir.dt.uint32
ALU = mybir.AluOpType
ACT = mybir.ActivationFunctionType
AX = mybir.AxisListType

P = 128
N = 1250
D = 512
E = 21250
NT = -(-N // P)
NPAD = NT * P
LAST = N - (NT - 1) * P
FT = D // P
H = 8
NK = 256
HK = H * 8
EPS = 1e-5
BPS = 4
SPAN = BPS * P
NS = -(-E // SPAN)
TAIL = E - (NS - 1) * SPAN
NO_NODE = 4096
FAR = 1000.0
CHUNKS = [(0, 512), (512, 512), (1024, N - 1024)]
GS = 4
NG = HK // GS
RING = 4
BINS = 8


class Net:
    pass


def lay_out(nc, ctx, k):
    def sb(name, cols, dt=F32, rows=P):
        return ctx.enter_context(nc.sbuf_tensor(name, [rows, cols], dt))

    k.AT = sb("AT", NT * NPAD)
    k.x = sb("x", NT * D)
    k.big = sb("big", 16 * 1024)
    k.qk = sb("qk", 4096 + 2048)
    k.outT = sb("outT", FT * NPAD)
    k.y = sb("y", 2 * D)
    k.yT = sb("yT", D)
    k.qT = sb("qT", H * P)
    k.gt = sb("gt", D)
    k.diag = sb("diag", 2 * GS * P)
    k.b1 = k.gt
    k.h0 = k.big[:, 0:5120]
    k.ei = k.big[0:NS, 0:2 * SPAN].bitcast(I32)
    k.ef = k.big[0:NS, 2 * SPAN:4 * SPAN]
    k.aggT = k.big[:, 5120:10240]
    k.stage = k.big[:, 10240:12800]
    k.w0 = k.big[:, 12800:14848]
    k.dinvB = k.big[:, 14848:16128]
    k.zero = k.big[:, 2048:2304].bitcast(F16)
    k.dstp = k.big[:, 4096:4096 + BPS * NS]
    k.srcp = k.big[:, 4096 + BPS * NS:4096 + 2 * BPS * NS]
    k.iota = k.big[:, 4440:4440 + NPAD // 2].bitcast(F16)
    k.ones = k.big[:, 16128:16256]
    k.iotai = k.big[:, 5120:5120 + NPAD].bitcast(I32)
    oh = k.outT[:, 0:BPS * (NPAD + P) // 2].bitcast(F16)
    k.ohs = [oh[:, b * NPAD:(b + 1) * NPAD] for b in range(BPS)]
    k.ohd = [oh[:, BPS * NPAD + b * P:BPS * NPAD + (b + 1) * P] for b in range(BPS)]
    k.dg = k.outT[:, 0:NT * P]
    k.wq = k.qk[:, 0:4096]
    k.keys = k.qk[:, 4096:6144]
    k.h1 = k.outT[:, 0:NT * D]
    k.agg1 = k.qk[:, 0:FT * NPAD]
    k.w1 = k.big[:, 7 * 2048:8 * 2048]
    k.we = [k.big[:, b * 2048:(b + 1) * 2048] for b in range(7)] + [k.AT[:, 0:2048]]
    k.ident = sb("ident", P)
    k.eps = sb("eps", 1)
    k.thr = sb("thr", NT, rows=NS)
    k.thri = sb("thri", NT, I32, rows=NS)
    k.qcol = sb("qcol", 2, rows=NS)
    k.qcoli = sb("qcoli", 1, I32, rows=NS)
    k.lt = sb("lt", 2 * NT, rows=NT)
    k.iota8 = sb("iota8", 8)
    k.iota8i = sb("iota8i", 8, I32)
    k.bins = sb("bins", BINS - 1)
    k.par = sb("par", 4 * FT + H)
    k.mm = sb("mm", 2, rows=NS)
    k.ov = k.big[0:NS, 2304:2304 + 4 * NT]
    k.lh = sb("lh", 4, rows=NT)
    k.row = sb("row", 3 * NT, rows=1)
    k.bnd = sb("bnd", 3 * NT, I32, rows=1)
    k.st = sb("st", 6 * NT)
    k.mv = sb("mv", 2 * NT)
    k.rs = sb("rs", 2 * NT)
    k.pq = sb("pq", 2 * NT)
    k.degin = sb("degin", NT)
    k.deg = sb("deg", 3 * NT)
    k.dsq = sb("dsq", 3 * NT)
    k.dri = sb("dri", 3 * NT)
    k.comb = sb("comb", NT)
    k.bst = sb("bst", FT * 3 * 6)
    k.bmv = sb("bmv", 2 * FT)
    k.bsd = sb("bsd", FT)
    k.bsc = sb("bsc", 2 * FT)
    k.tst = sb("tst", 6)
    k.tmv = sb("tmv", 2)
    k.tsd = sb("tsd", 2)
    k.top = sb("top", 2 * HK)
    k.topi = sb("topi", 2 * HK, U32)
    k.topf = sb("topf", 2 * HK)
    k.best = sb("best", HK)
    k.pos = sb("pos", HK, U32)
    k.posab = sb("posab", 2 * HK, U32)
    k.posf = sb("posf", 2 * HK)
    k.pick = sb("pick", 2 * H * 64)
    k.all = k.pick[:, 0:H * 64]
    k.iab = k.posf
    k.idx = [sb(f"idx{b}", HK, I32) for b in range(2)]
    k.sm = sb("sm", HK)
    k.ex = k.sm
    k.ssum = sb("ssum", 2 * H)
    k.prob = sb("prob", 2 * HK)
    k.inner = sb("inner", HK)
    k.val = sb("val", HK)
    k.gtb = sb("gtb", BINS - 1)
    k.mem = sb("mem", 1)
    k.sel = sb("sel", BINS)

    def ps(name, cols, dt=F32):
        return ctx.enter_context(nc.psum_tensor(name, [P, cols], dt))

    k.acc = [ps(f"acc{s}", 3 * 512) for s in range(2)]
    k.tr = [ps(f"tr{s}", 512) for s in range(2)]
    banks = [k.acc[s][:, b * 512:(b + 1) * 512] for s in range(2) for b in range(3)]
    k.TK = k.YT = banks[0]
    k.Q = banks[1]
    k.S = [banks[2:4], banks[4:6]]
    k.O = [k.tr[0][:, :], k.tr[1][:, :]]




def program(nc, x_d, src_d, dst_d, w0t_d, par_d, wq_d, keys_d, wdu_d, w1_d, b1_d, we_d, out_d):
    k = Net()
    with ExitStack() as ctx:
        k.nc = nc
        lay_out(nc, ctx, k)

        def sem(name):
            return ctx.enter_context(nc.semaphore(name))

        k.ring_free = sem("ring_free")
        k.s_seen = sem("s_seen")
        k.consts = sem("consts")
        k.edges_pre = sem("edges_pre")
        k.xpad = sem("xpad")
        k.edges_in = sem("edges_in")
        k.x_in = sem("x_in")
        k.w_in = sem("w_in")
        k.par_in = sem("par_in")
        k.wq_in = sem("wq_in")
        k.keys_in = sem("keys_in")
        k.b1_in = sem("b1_in")
        k.edge_f = sem("edge_f")
        k.ov_done = sem("ov_done")
        k.stats0 = sem("stats0")
        k.sd0_ready = sem("sd0_ready")
        k.edgeT_ready = sem("edgeT_ready")
        k.edgeT_done = sem("edgeT_done")
        k.lowT_ready = sem("lowT_ready")
        k.lh_ready = sem("lh_ready")
        k.row_ready = sem("row_ready")
        k.bounds_ready = sem("bounds_ready")
        k.oh_ready = sem("oh_ready")
        k.oh_used = sem("oh_used")
        k.acc_ready = sem("acc_ready")
        k.stage_ready = sem("stage_ready")
        k.trp_ready = sem("trp_ready")
        k.at_done = sem("at_done")
        k.degs_ready = sem("degs_ready")
        k.degsq_ready = sem("degsq_ready")
        k.dego_ready = sem("dego_ready")
        k.degosq_ready = sem("degosq_ready")
        k.h0_ready = sem("h0_ready")
        k.dg_ready = sem("dg_ready")
        k.dinvB_psum = sem("dinvB_psum")
        k.dinvB_ready = sem("dinvB_ready")
        k.agg_ready = sem("agg_ready")
        k.aggT_done = sem("aggT_done")
        k.out_ready = sem("out_ready")
        k.outT_done = sem("outT_done")
        k.bnvar_ready = sem("bnvar_ready")
        k.bnsd_ready = sem("bnsd_ready")
        k.bn_ready = sem("bn_ready")
        k.gelu_done = sem("gelu_done")
        k.tk_ready = sem("tk_ready")
        k.x1_done = sem("x1_done")
        k.var_ready = sem("var_ready")
        k.sd_ready = sem("sd_ready")
        k.y_ready = sem("y_ready")
        k.yt_ready = sem("yt_ready")
        k.yT_done = sem("yT_done")
        k.q_ready = sem("q_ready")
        k.qT_done = sem("qT_done")
        k.s_ready = sem("s_ready")
        k.topk_done = sem("topk_done")
        k.idx_ready = sem("idx_ready")
        k.exp_in = sem("exp_in")
        k.exp_done = sem("exp_done")
        k.prob_ready = sem("prob_ready")
        k.val_ready = sem("val_ready")
        k.diag_ready = sem("diag_ready")
        k.grp_done = sem("grp_done")
        k.x2_done = sem("x2_done")
        k.stats1 = sem("stats1")
        k.sd1_ready = sem("sd1_ready")
        k.h1_ready = sem("h1_ready")
        k.agg1_ready = sem("agg1_ready")
        k.agg1_done = sem("agg1_done")
        k.g1_ready = sem("g1_ready")
        k.x3_done = sem("x3_done")
        k.var4_ready = sem("var4_ready")
        k.sd4_ready = sem("sd4_ready")
        k.z_ready = sem("z_ready")
        k.zt_ready = sem("zt_ready")
        k.zT_done = sem("zT_done")
        k.e_ready = sem("e_ready")
        k.e_used = sem("e_used")
        k.w1_in = sem("w1_in")
        k.we_in = sem("we_in")
        k.we7_in = sem("we7_in")
        k.out_done = sem("out_done")
        k.landed = [ctx.enter_context(nc.semaphore(f"landed{r}")) for r in range(RING)]
        k.x_d, k.src_d, k.dst_d, k.w0t_d, k.par_d, k.wq_d = x_d, src_d, dst_d, w0t_d, par_d, wq_d
        k.keys_d, k.wdu_d, k.w1_d, k.b1_d, k.we_d, k.out_d = keys_d, wdu_d, w1_d, b1_d, we_d, out_d
        block = ctx.enter_context(nc.Block())

        @block.sync
        def _(sp):
            sync_program(sp, k)

        @block.gpsimd
        def _(pool):
            pool_program(pool, k)

        @block.scalar
        def _(act):
            act_program(act, k)

        @block.vector
        def _(dve):
            dve_program(dve, k)

        @block.tensor
        def _(pe):
            pe_program(pe, k)


def sync_program(sp, k):
    sp.wait_ge(k.edges_pre, 1)
    full = (NS - 1) * SPAN
    for c, d in enumerate((k.dst_d, k.src_d)):
        cols = slice(c * SPAN, (c + 1) * SPAN)
        sp.dma_start(k.ei[0:NS - 1, cols], d[0:full].rearrange("(q n) -> q n", n=SPAN)).then_inc(k.edges_in, 16)
        sp.dma_start(k.ei[NS - 1:NS, c * SPAN:c * SPAN + TAIL],
                     d[full:E].rearrange("(q n) -> q n", q=1)).then_inc(k.edges_in, 16)
    sp.wait_ge(k.xpad, 1)
    sp.dma_start(k.x[:, 0:(NT - 1) * D].rearrange("p (t d) -> p t d", d=D),
                 k.x_d[0:(NT - 1) * P, :].rearrange("(t p) d -> p t d", p=P)).then_inc(k.x_in, 16)
    sp.dma_start(k.x[0:LAST, (NT - 1) * D:NT * D], k.x_d[(NT - 1) * P:N, :]).then_inc(k.x_in, 16)
    sp.dma_start(k.w0.rearrange("p (f n) -> p f n", n=D),
                 k.w0t_d.rearrange("(f p) n -> p f n", p=P)).then_inc(k.w_in, 16)
    sp.dma_start(k.par[:, :], k.par_d).then_inc(k.par_in, 16)
    sp.dma_start(k.wq.rearrange("p (f n) -> p f n", n=H * P),
                 k.wq_d.rearrange("(f p) n -> p f n", p=P)).then_inc(k.wq_in, 16)
    sp.dma_start(k.keys, k.keys_d).then_inc(k.keys_in, 16)
    sp.wait_ge(k.grp_done, NT * NG + RING)
    sp.dma_start(k.b1[:, :], k.b1_d.partition_broadcast(P)).then_inc(k.b1_in, 16)
    sp.dma_start(k.w1.rearrange("p (f n) -> p f n", n=D),
                 k.w1_d.rearrange("(f p) n -> p f n", p=P)).then_inc(k.w1_in, 16)
    for b in range(BINS - 1):
        sp.dma_start(k.we[b].rearrange("p (f n) -> p f n", n=D),
                     k.we_d[b].rearrange("(f p) n -> p f n", p=P)).then_inc(k.we_in, 16)
    sp.wait_ge(k.agg1_ready, FT)
    sp.dma_start(k.we[BINS - 1].rearrange("p (f n) -> p f n", n=D),
                 k.we_d[BINS - 1].rearrange("(f p) n -> p f n", p=P)).then_inc(k.we7_in, 16)
    with sp.Fori(0, NT - 1) as t:
        sp.wait_ge(k.e_used, (t + 1) * BINS)
        sp.dma_start(k.out_d[bass.ds(t * P, P), :], k.x[:, bass.ds(t * D, D)]).then_inc(k.out_done, 16)
    sp.wait_ge(k.e_used, NT * BINS)
    sp.dma_start(k.out_d[(NT - 1) * P:N, :], k.x[0:LAST, (NT - 1) * D:NT * D]).then_inc(k.out_done, 16)
    sp.wait_ge(k.out_done, 16 * NT)


def pool_program(pool, k):
    pool.memset(k.ei, NO_NODE).then_inc(k.edges_pre, 1)
    pool.memset(k.x[:, (NT - 1) * D:NT * D], 0.0).then_inc(k.xpad, 1)
    pool.memset(k.ident[:, :], 0.0)
    pool.memset(k.lt[:, :], 0.0)
    pool.memset(k.ones, 1.0)
    pool.memset(k.zero, 0.0)
    pool.memset(k.eps[:, :], EPS)
    pool.memset(k.stage, 0.0)
    pool.iota(k.iotai, pattern=[[1, NPAD]], base=0, channel_multiplier=0)
    pool.iota(k.thri[:, :], pattern=[[P, NT]], base=0, channel_multiplier=0)
    pool.iota(k.qcoli[:, :], pattern=[[0, 1]], base=0, channel_multiplier=1)
    pool.iota(k.iota8i[:, :], pattern=[[1, 8]], base=0, channel_multiplier=0)
    pool.drain()
    pool.affine_select(out=k.ident[:, :], in_=k.ident[:, :], compare_op=ALU.not_equal, fill=1.0, base=0,
                       pattern=[[-1, P]], channel_multiplier=1)
    pool.affine_select(out=k.lt[:, 0:NT], in_=k.lt[:, 0:NT], compare_op=ALU.is_ge, fill=1.0, base=0,
                       pattern=[[-1, NT]], channel_multiplier=1)
    pool.affine_select(out=k.lt[:, NT:2 * NT], in_=k.lt[:, NT:2 * NT], compare_op=ALU.is_gt, fill=1.0, base=0,
                       pattern=[[-1, NT]], channel_multiplier=1)
    pool.tensor_copy(k.iota, k.iotai)
    pool.tensor_copy(k.thr[:, :], k.thri[:, :])
    pool.tensor_copy(k.iota8[:, :], k.iota8i[:, :])
    pool.drain()
    pool.tensor_scalar(k.qcol[:, 0:1], k.qcoli[:, :], -FAR, None, ALU.add)
    pool.tensor_scalar(k.qcol[:, 1:2], k.qcoli[:, :], 1.0, None, ALU.add)
    pool.tensor_scalar(k.bins[:, :], k.iota8[:, 0:BINS - 1], 0.5, -1.5, ALU.mult, ALU.add)
    pool.drain().then_inc(k.consts, 1)

    def gather_tile(i, par):
        pool.wait_ge(k.idx_ready, i + 1)
        for g in range(NG):
            r = g % RING
            pool.wait_ge(k.val_ready, i * NG + g + 1)
            pool.wait_ge(k.grp_done, i * NG + g + 1)
            pool.sem_inc(k.ring_free, 1)
            for s in range(GS):
                j = g * GS + s
                slot = r * GS + s
                pool.indirect_dma_start(
                    out=k.big[:, slot * 2 * D:(slot + 1) * 2 * D], out_offset=None, in_=k.wdu_d,
                    in_offset=bass.IndirectOffsetOnAxis(ap=k.idx[par][:, j:j + 1], axis=0),
                ).then_inc(k.landed[r], 16)

    with pool.Fori(0, NT // 2) as pair:
        gather_tile(pair * 2, 0)
        gather_tile(pair * 2 + 1, 1)


def act_program(act, k):
    copy = ACT.Copy
    act.wait_ge(k.consts, 1)
    act.wait_ge(k.edgeT_ready, 1)
    act.activation(k.dstp, k.tr[0][:, 0:BPS * NS], copy)
    act.activation(k.srcp, k.tr[1][:, 0:BPS * NS], copy).then_inc(k.edgeT_done, 1)
    act.wait_ge(k.row_ready, 1)
    act.activation(k.row[:, :], k.tr[0][0:1, 0:3 * NT], copy).then_inc(k.lh_ready, 1)
    act.wait_ge(k.stats0, 1)
    act.activation(k.rs[:, 0:NT], k.mv[:, NT:2 * NT], ACT.Sqrt, bias=k.eps[:, :]).then_inc(k.sd0_ready, 1)

    def count_rows(t, s):
        act.wait_ge(k.acc_ready, t + 1)
        act.wait_ge(k.trp_ready, t * 3 - 3)
        act.activation(k.stage[:, s * NPAD:s * NPAD + N], k.acc[s][:, 0:N], copy,
                       accum_out=k.degin[:, bass.ds(t, 1)]).then_inc(k.stage_ready, 1)

    def count_cols(t, s):
        at = k.AT[:, :].rearrange("p (j c) -> p j c", c=NPAD)
        for b, j0 in enumerate((0, 4, 8)):
            n = min(4, NT - j0)
            act.wait_ge(k.trp_ready, t * 3 + b + 1)
            act.activation(at[:, j0:j0 + n, bass.ds(t * P, P)],
                           k.tr[(s + b) % 2][:, 0:n * P].rearrange("p (j c) -> p j c", c=P),
                           copy).then_inc(k.at_done, 1)

    act.wait_ge(k.acc_ready, 1)
    act.activation(k.stage[:, 0:N], k.acc[0][:, 0:N], copy, accum_out=k.degin[:, 0:1]).then_inc(k.stage_ready, 1)
    act.wait_ge(k.acc_ready, 2)
    act.activation(k.stage[:, NPAD:NPAD + N], k.acc[1][:, 0:N], copy,
                   accum_out=k.degin[:, 1:2]).then_inc(k.stage_ready, 1)
    count_cols(0, 0)
    with act.Fori(1, NT // 2) as h:
        count_rows(2 * h, 0)
        count_cols(2 * h - 1, 1)
        count_rows(2 * h + 1, 1)
        count_cols(2 * h, 0)
    count_cols(NT - 1, 1)

    act.wait_ge(k.degs_ready, 1)
    act.activation(k.dsq[:, 0:2 * NT], k.deg[:, 0:2 * NT], ACT.Sqrt).then_inc(k.degsq_ready, 1)
    act.wait_ge(k.dinvB_psum, 1)
    act.activation(k.dinvB[:, 0:512], k.tr[0][:, :], copy)
    act.activation(k.dinvB[:, 512:1024], k.tr[1][:, :], copy).then_inc(k.dinvB_ready, 1)
    act.wait_ge(k.dinvB_psum, 2)
    act.activation(k.dinvB[:, 1024:NPAD], k.tr[0][:, 0:NPAD - 1024], copy).then_inc(k.dinvB_ready, 1)
    act.wait_ge(k.dego_ready, 1)
    act.activation(k.dsq[:, 2 * NT:3 * NT], k.deg[:, 2 * NT:3 * NT], ACT.Sqrt).then_inc(k.degosq_ready, 1)
    act.wait_ge(k.par_in, 16)
    for o in range(FT):
        act.wait_ge(k.out_ready, o + 1)
        act.activation(k.outT[:, o * NPAD:o * NPAD + N], k.acc[o % 2][:, 0:N], ACT.Identity,
                       bias=k.par[:, o:o + 1]).then_inc(k.outT_done, 1)
    act.wait_ge(k.bnvar_ready, 1)
    act.activation(k.bsd[:, :], k.bmv[:, FT:2 * FT], ACT.Sqrt, bias=k.eps[:, :]).then_inc(k.bnsd_ready, 1)
    act.wait_ge(k.bn_ready, 1)

    def gelu(i):
        act.wait_ge(k.tk_ready, i)
        for o in range(FT):
            ins = act.activation(k.gt[:, o * P:(o + 1) * P], k.outT[:, bass.ds(i * P + o * NPAD, P)], ACT.Gelu,
                                 bias=k.bsc[:, FT + o:FT + o + 1], scale=k.bsc[:, o:o + 1])
        ins.then_inc(k.gelu_done, 1)

    def root(i):
        act.wait_ge(k.var_ready, i + 1)
        act.activation(k.tsd[:, 0:1], k.tmv[:, 1:2], ACT.Sqrt, bias=k.eps[:, :]).then_inc(k.sd_ready, 1)

    def copy_yT(i):
        act.wait_ge(k.yt_ready, i + 1)
        act.activation(k.yT[:, :], k.YT, copy).then_inc(k.yT_done, 1)

    def copy_q(i, half):
        act.wait_ge(k.q_ready, 2 * i + half + 1)
        if half == 0:
            act.wait_ge(k.s_ready, i * H)
        for b in range(4):
            h = 4 * half + b
            act.activation(k.qT[:, h * P:(h + 1) * P], k.Q[:, b * P:(b + 1) * P], ACT.Identity,
                           bias=k.par[:, 4 * FT + h:4 * FT + h + 1]).then_inc(k.qT_done, 1)

    def exps(i):
        act.wait_ge(k.exp_in, i + 1)
        act.activation(k.ex[:, :], k.sm[:, :], ACT.Exp).then_inc(k.exp_done, 1)

    pieces = {0: gelu, 3: root, 5: copy_yT, 6: lambda i: copy_q(i, 0), 7: lambda i: copy_q(i, 1), 13: exps}

    def search(i):
        for g in sorted(pieces):
            pieces[g](i)

    def tile(i, par, ahead):
        for g in range(NG):
            if ahead and g in pieces:
                pieces[g](i + 1)
            act.wait_ge(k.val_ready, i * NG + g + 1 + RING)
            act.wait_ge(k.grp_done, i * NG + g - 1 + RING)
            for s in range(GS):
                j = g * GS + s
                ins = act.activation(k.diag[:, ((g % 2) * GS + s) * P:((g % 2) * GS + s + 1) * P], k.ident[:, :],
                                     copy, scale=k.val[:, j:j + 1])
            ins.then_inc(k.diag_ready, 1)

    search(0)
    with act.Fori(0, NT // 2 - 1) as pair:
        tile(pair * 2, 0, True)
        tile(pair * 2 + 1, 1, True)
    tile(NT - 2, 0, True)
    tile(NT - 1, 1, False)

    act.wait_ge(k.stats1, 1)
    act.activation(k.rs[:, 0:NT], k.mv[:, NT:2 * NT], ACT.Sqrt, bias=k.eps[:, :]).then_inc(k.sd1_ready, 1)
    for f in range(FT):
        act.wait_ge(k.agg1_ready, f + 1)
        act.activation(k.agg1[:, f * NPAD:f * NPAD + N], k.acc[f % 2][:, 0:N], copy).then_inc(k.agg1_done, 1)
    with act.Fori(0, NT) as i:
        act.wait_ge(k.var4_ready, i + 1)
        act.activation(k.tsd[:, 0:1], k.tmv[:, 1:2], ACT.Sqrt, bias=k.eps[:, :]).then_inc(k.sd4_ready, 1)
        act.wait_ge(k.zt_ready, i + 1)
        act.activation(k.yT[:, :], k.YT, copy).then_inc(k.zT_done, 1)


def dve_program(dve, k):
    def stats(tile, t):
        dve.bn_stats(k.st[:, 6 * t:6 * t + 6], tile)

    dve.wait_ge(k.edges_in, 64)
    dve.tensor_copy(k.ef, k.ei).then_inc(k.edge_f, 1)
    dve.drain()
    dve.tensor_reduce(k.mm[:, 0:1], k.ef[:, 0:SPAN], AX.X, ALU.min)
    dve.tensor_reduce(k.mm[:, 1:2], k.ef[:, 0:SPAN], AX.X, ALU.max)
    dve.wait_ge(k.consts, 1)
    dve.drain()
    a, b = k.ov[:, 0:NT], k.ov[:, NT:2 * NT]
    low, high = k.ov[:, 2 * NT:3 * NT], k.ov[:, 3 * NT:4 * NT]
    dve.tensor_scalar(a, k.thr[:, :], k.mm[:, 1:2], None, ALU.is_le)
    dve.tensor_scalar(b, k.thr[:, :], float(P), k.mm[:, 0:1], ALU.add, ALU.is_gt)
    dve.drain()
    dve.tensor_tensor(a, a, b, ALU.mult)
    dve.drain()
    dve.tensor_scalar(low, a, k.qcol[:, 0:1], FAR, ALU.mult, ALU.add)
    dve.tensor_scalar(high, a, k.qcol[:, 1:2], None, ALU.mult)
    dve.drain().then_inc(k.ov_done, 1)
    dve.wait_ge(k.lowT_ready, 1)
    lo, hi, ln, pos = (k.lh[:, c:c + 1] for c in range(4))
    dve.tensor_reduce(lo, k.acc[0][0:NT, 0:NS], AX.X, ALU.min)
    dve.tensor_reduce(hi, k.acc[0][0:NT, NS:2 * NS], AX.X, ALU.max)
    dve.drain()
    dve.tensor_scalar(pos, hi, 0.0, None, ALU.is_gt)
    dve.tensor_scalar(hi, hi, 1.0, None, ALU.max)
    dve.drain()
    dve.tensor_tensor(lo, lo, pos, ALU.mult)
    dve.drain()
    dve.tensor_tensor(ln, hi, lo, ALU.subtract)
    dve.drain().then_inc(k.bounds_ready, 1)
    dve.wait_ge(k.lh_ready, 1)
    dve.tensor_copy(k.bnd[:, 0:2 * NT], k.row[:, NT:3 * NT])
    dve.tensor_tensor(k.bnd[:, 2 * NT:3 * NT], k.row[:, 0:NT], k.row[:, NT:2 * NT], ALU.subtract)
    dve.drain().then_inc(k.bounds_ready, 1)
    dve.wait_ge(k.x_in, 32)
    for t in range(NT):
        stats(k.x[:, t * D:(t + 1) * D], t)
    dve.drain()
    mv = k.mv[:, :].rearrange("p (c t) -> p t c", c=2)
    for t in range(NT):
        dve.bn_aggr(mv[:, t, :], k.st[:, 6 * t:6 * t + 6])
    dve.drain().then_inc(k.stats0, 1)
    dve.wait_ge(k.edgeT_done, 1)
    with dve.Fori(0, NT) as t:
        first = dve.value_load(k.bnd[0:1, bass.ds(t, 1)], min_val=0, max_val=NS * NT)
        end = dve.value_load(k.bnd[0:1, bass.ds(t + NT, 1)], min_val=1, max_val=NS * NT + 1)
        shift = dve.value_load(k.bnd[0:1, bass.ds(t + 2 * NT, 1)], min_val=-NS * NT, max_val=NS)
        with dve.Fori(first, end) as n:
            q = k.nc.s_assert_within(dve.snap(n + shift), 0, NS - 1,
                                       skip_runtime_bounds_check_because="first <= n < end, so lo <= q < hi <= NS")
            for c in range(BPS):
                dve.wait_ge(k.oh_used, n * BPS + c + 1)
                dve.tensor_scalar(k.ohs[c][:, 0:N], k.iota[:, 0:N], k.srcp[:, bass.ds(q + c * NS, 1)], None,
                                  ALU.is_equal).then_inc(k.oh_ready, 1)
                dve.tensor_scalar(k.ohd[c], k.iota[:, bass.ds(t * P, P)], k.dstp[:, bass.ds(q + c * NS, 1)], None,
                                  ALU.is_equal).then_inc(k.oh_ready, 1)

    dve.wait_ge(k.stage_ready, NT)
    dve.tensor_scalar(k.deg[:, 0:NT], k.degin[:, :], 1.0, None, ALU.add)
    dve.tensor_scalar(k.deg[:, NT:2 * NT], k.degin[:, :], 1.0, None, ALU.max)
    dve.drain().then_inc(k.degs_ready, 1)
    dve.wait_ge(k.sd0_ready, 1)
    dve.reciprocal(k.rs[:, NT:2 * NT], k.rs[:, 0:NT])
    dve.wait_ge(k.degsq_ready, 1)
    dve.reciprocal(k.dri[:, 0:2 * NT], k.dsq[:, 0:2 * NT])
    dve.drain()
    dve.tensor_tensor(k.comb[:, :], k.rs[:, NT:2 * NT], k.dri[:, 0:NT], ALU.mult)
    dve.tensor_scalar(k.pq[:, 0:NT], k.rs[:, NT:2 * NT], 1.0, None, ALU.add)
    dve.tensor_tensor(k.pq[:, NT:2 * NT], k.rs[:, NT:2 * NT], k.mv[:, 0:NT], ALU.mult)
    dve.wait_ge(k.at_done, 3 * NT)
    dve.drain()
    for t in range(NT):
        diag = k.AT[:, t * NPAD + t * P:t * NPAD + (t + 1) * P]
        dve.tensor_tensor(diag, diag, k.ident[:, :], ALU.add)
        dve.tensor_scalar(k.h0[:, t * D:(t + 1) * D], k.x[:, t * D:(t + 1) * D], k.mv[:, t:t + 1],
                          k.comb[:, t:t + 1], ALU.subtract, ALU.mult)
        dve.drain().then_inc(k.h0_ready, 1)
    for t in range(NT):
        dve.tensor_scalar(k.dg[:, t * P:(t + 1) * P], k.ident[:, :], k.dri[:, t:t + 1], None, ALU.mult)
    dve.drain().then_inc(k.dg_ready, 1)
    dve.tensor_reduce(k.degin[:, :], k.AT[:, :].rearrange("p (j c) -> p j c", c=NPAD), AX.X, ALU.add)
    dve.drain()
    dve.tensor_scalar(k.deg[:, 2 * NT:3 * NT], k.degin[:, :], -1.0, 1.0, ALU.add, ALU.max)
    dve.drain().then_inc(k.dego_ready, 1)
    for t in range(NT):
        tile = k.x[:, t * D:(t + 1) * D]
        dve.tensor_scalar(tile, tile, k.pq[:, t:t + 1], k.pq[:, NT + t:NT + t + 1], ALU.mult, ALU.subtract)
    dve.wait_ge(k.degosq_ready, 1)
    dve.reciprocal(k.dri[:, 2 * NT:3 * NT], k.dsq[:, 2 * NT:3 * NT])
    dve.wait_ge(k.dinvB_ready, 2)
    for f in range(FT):
        dve.wait_ge(k.agg_ready, f + 1)
        dve.tensor_tensor(k.aggT[:, f * NPAD:f * NPAD + N], k.acc[f % 2][:, 0:N], k.dinvB[:, 0:N],
                          ALU.mult).then_inc(k.aggT_done, 1)
    dve.memset(k.outT[:, :].rearrange("p (o c) -> p o c", c=NPAD)[:, :, N:NPAD], 0.0)
    bmv = k.bmv[:, :].rearrange("p (c o) -> p o c", c=2)
    for o in range(FT):
        dve.wait_ge(k.outT_done, o + 1)
        for c, (c0, n) in enumerate(CHUNKS):
            dve.bn_stats(k.bst[:, (o * 3 + c) * 6:(o * 3 + c + 1) * 6], k.outT[:, o * NPAD + c0:o * NPAD + c0 + n])
        dve.drain()
        dve.bn_aggr(bmv[:, o, :], k.bst[:, o * 18:(o + 1) * 18])
    dve.drain().then_inc(k.bnvar_ready, 1)
    dve.wait_ge(k.bnsd_ready, 1)
    dve.reciprocal(k.bsd[:, :], k.bsd[:, :])
    dve.wait_ge(k.par_in, 16)
    dve.drain()
    dve.tensor_tensor(k.bsc[:, 0:FT], k.bsd[:, :], k.par[:, FT:2 * FT], ALU.mult)
    dve.drain()
    dve.tensor_tensor(k.bsc[:, FT:2 * FT], k.bsc[:, 0:FT], k.bmv[:, 0:FT], ALU.mult)
    dve.drain()
    dve.tensor_tensor(k.bsc[:, FT:2 * FT], k.par[:, 2 * FT:3 * FT], k.bsc[:, FT:2 * FT], ALU.subtract)
    dve.drain().then_inc(k.bn_ready, 1)

    def first_norm(i, par):
        dve.wait_ge(k.tk_ready, i + 1)
        tile = k.x[:, bass.ds(i * D, D)]
        dve.tensor_tensor(tile, tile, k.TK, ALU.add).then_inc(k.x1_done, 1)
        dve.drain()
        dve.bn_stats(k.tst[:, :], tile)
        dve.drain()
        dve.bn_aggr(k.tmv[:, :], k.tst[:, :]).then_inc(k.var_ready, 1)

    def normed(i, par):
        dve.wait_ge(k.sd_ready, i + 1)
        dve.reciprocal(k.tsd[:, 1:2], k.tsd[:, 0:1])
        dve.drain()
        dve.tensor_scalar(k.y[:, par * D:(par + 1) * D], k.x[:, bass.ds(i * D, D)], k.tmv[:, 0:1], k.tsd[:, 1:2],
                          ALU.subtract, ALU.mult).then_inc(k.y_ready, 1)

    def top_heads(i, h0):
        for h in (h0, h0 + 1):
            dve.wait_ge(k.s_ready, i * H + h + 1)
            dve.sem_inc(k.s_seen, 1)
            for c in range(2):
                dve.max(k.top[:, c * HK + h * 8:c * HK + h * 8 + 8], k.S[h % 2][c][:, 0:NK])
            dve.drain()
            for c in range(2):
                ins = dve.max_index(k.topi[:, c * HK + h * 8:c * HK + h * 8 + 8],
                                    k.top[:, c * HK + h * 8:c * HK + h * 8 + 8], k.S[h % 2][c][:, 0:NK])
            dve.drain().then_inc(k.topk_done, 1)

    def pairs(i, par):
        shape = [P, H, 8, 8]
        t1 = k.top[:, 0:HK].rearrange("p (h a) -> p h a", h=H).unsqueeze(3).to_broadcast(shape)
        t2 = k.top[:, HK:2 * HK].rearrange("p (h b) -> p h b", h=H).unsqueeze(2).to_broadcast(shape)
        dve.tensor_tensor(k.all.rearrange("p (h a b) -> p h a b", h=H, a=8), t1, t2, ALU.add)
        dve.tensor_copy(k.topf[:, :], k.topi[:, :])
        dve.drain()
        for h in range(H):
            dve.max(k.best[:, h * 8:h * 8 + 8], k.all[:, h * 64:(h + 1) * 64])
        dve.drain()
        for h in range(H):
            dve.max_index(k.pos[:, h * 8:h * 8 + 8], k.best[:, h * 8:h * 8 + 8], k.all[:, h * 64:(h + 1) * 64])
        dve.drain()
        dve.tensor_scalar(k.posab[:, 0:HK], k.pos[:, :], 3, None, ALU.logical_shift_right)
        dve.tensor_scalar(k.posab[:, HK:2 * HK], k.pos[:, :], 7, None, ALU.bitwise_and)
        dve.drain()
        dve.tensor_copy(k.posf[:, :], k.posab[:, :])
        dve.drain()
        pick3 = k.pick[:, :].rearrange("p (j a) -> p j a", a=8)
        dve.tensor_tensor(pick3, k.posf[:, :].unsqueeze(2).to_broadcast([P, 2 * HK, 8]),
                          k.iota8[:, :].unsqueeze(1).to_broadcast([P, 2 * HK, 8]), ALU.is_equal)
        dve.drain()
        pick4 = k.pick[:, :].rearrange("p (h j a) -> p h j a", h=2 * H, a=8)
        dve.tensor_tensor(pick4, pick4, k.topf[:, :].rearrange("p (h a) -> p h a", a=8).unsqueeze(2)
                          .to_broadcast([P, 2 * H, 8, 8]), ALU.mult)
        dve.drain()
        dve.tensor_reduce(k.iab[:, :], pick3, AX.X, ALU.add)
        dve.drain()
        dve.scalar_tensor_tensor(k.idx[par][:, :], k.iab[:, 0:HK], float(NK), k.iab[:, HK:2 * HK],
                                 ALU.mult, ALU.add).then_inc(k.idx_ready, 1)
        best = k.best[:, :].rearrange("p (h a) -> p h a", a=8)
        dve.tensor_tensor(k.sm[:, :].rearrange("p (h a) -> p h a", a=8), best,
                          best[:, :, 0:1].to_broadcast([P, H, 8]), ALU.subtract).then_inc(k.exp_in, 1)

    def softmax(i, par):
        dve.wait_ge(k.exp_done, i + 1)
        ex = k.ex[:, :].rearrange("p (h a) -> p h a", a=8)
        dve.tensor_reduce(k.ssum[:, 0:H], ex, AX.X, ALU.add)
        dve.drain()
        dve.reciprocal(k.ssum[:, H:2 * H], k.ssum[:, 0:H])
        dve.drain()
        dve.tensor_tensor(k.prob[:, par * HK:(par + 1) * HK].rearrange("p (h a) -> p h a", a=8), ex,
                          k.ssum[:, H:2 * H].unsqueeze(2).to_broadcast([P, H, 8]), ALU.mult)

    pieces = {2: first_norm, 4: normed, 8: lambda i, p: top_heads(i, 0), 9: lambda i, p: top_heads(i, 2),
              10: lambda i, p: top_heads(i, 4), 11: lambda i, p: top_heads(i, 6), 12: pairs, 15: softmax}

    def search(i, par):
        for g in sorted(pieces):
            pieces[g](i, par)

    def tile(i, par, ahead):
        for g in range(NG):
            if ahead and g in pieces:
                pieces[g](i + 1, 1 - par)
            r = g % RING
            use = i * (NG // RING) + g // RING
            dve.wait_ge(k.landed[r], use * (16 * GS) + 16 * GS)
            for s in range(GS):
                slot = (r * GS + s) * 2 * D
                dve.tensor_tensor_reduce(out=k.big[:, slot:slot + D], in0=k.big[:, slot:slot + D],
                                         in1=k.y[:, par * D:(par + 1) * D], scale=1.0, scalar=0.0,
                                         op0=ALU.mult, op1=ALU.add,
                                         accum_out=k.inner[:, g * GS + s:g * GS + s + 1])
            dve.drain()
            dve.scalar_tensor_tensor(k.val[:, g * GS:(g + 1) * GS], k.inner[:, g * GS:(g + 1) * GS], 0.0,
                                     k.prob[:, par * HK + g * GS:par * HK + (g + 1) * GS],
                                     ALU.max, ALU.mult).then_inc(k.val_ready, 1)
        dve.wait_ge(k.grp_done, i * NG + NG + RING)
        t = k.x[:, bass.ds(i * D, D)]
        dve.tensor_tensor(t, t, k.O[par], ALU.add).then_inc(k.x2_done, 1)

    dve.sem_inc(k.val_ready, RING)
    search(0, 0)
    dve.drain()
    with dve.Fori(0, NT // 2 - 1) as pair:
        tile(pair * 2, 0, True)
        tile(pair * 2 + 1, 1, True)
    tile(NT - 2, 0, True)
    tile(NT - 1, 1, False)

    dve.drain()
    for t in range(NT):
        stats(k.x[:, t * D:(t + 1) * D], t)
    dve.drain()
    for t in range(NT):
        dve.bn_aggr(mv[:, t, :], k.st[:, 6 * t:6 * t + 6])
    dve.drain().then_inc(k.stats1, 1)
    for t in range(NT):
        diag = k.AT[:, t * NPAD + t * P:t * NPAD + (t + 1) * P]
        dve.tensor_tensor(diag, diag, k.ident[:, :], ALU.subtract)
    dve.wait_ge(k.sd1_ready, 1)
    dve.reciprocal(k.rs[:, NT:2 * NT], k.rs[:, 0:NT])
    dve.drain()
    dve.tensor_tensor(k.comb[:, :], k.rs[:, NT:2 * NT], k.dri[:, 2 * NT:3 * NT], ALU.mult)
    dve.drain()
    for t in range(NT):
        dve.tensor_scalar(k.h1[:, t * D:(t + 1) * D], k.x[:, t * D:(t + 1) * D], k.mv[:, t:t + 1],
                          k.comb[:, t:t + 1], ALU.subtract, ALU.mult).then_inc(k.h1_ready, 1)
    dve.memset(k.agg1.rearrange("p (o c) -> p o c", c=NPAD)[:, :, N:NPAD], 0.0).then_inc(k.h1_ready, 1)
    dve.wait_ge(k.b1_in, 16)
    for t in range(NT):
        tile_ = k.x[:, t * D:(t + 1) * D]
        dve.tensor_tensor(tile_, tile_, k.b1[:, :], ALU.add)
    dve.drain()
    for t in range(NT):
        dve.wait_ge(k.g1_ready, t + 1)
        tile_ = k.x[:, t * D:(t + 1) * D]
        dve.scalar_tensor_tensor(tile_, k.tr[t % 2][:, :], k.dri[:, NT + t:NT + t + 1], tile_,
                                 ALU.mult, ALU.add).then_inc(k.x3_done, 1)
    dve.drain()
    with dve.Fori(0, NT) as i:
        tile_ = k.x[:, bass.ds(i * D, D)]
        dve.bn_stats(k.tst[:, :], tile_)
        dve.drain()
        dve.bn_aggr(k.tmv[:, :], k.tst[:, :]).then_inc(k.var4_ready, 1)
        dve.wait_ge(k.sd4_ready, i + 1)
        dve.reciprocal(k.tsd[:, 1:2], k.tsd[:, 0:1])
        dve.drain()
        dve.tensor_scalar(k.y[:, 0:D], tile_, k.tmv[:, 0:1], k.tsd[:, 1:2],
                          ALU.subtract, ALU.mult).then_inc(k.z_ready, 1)
        dve.drain()
        dve.tensor_scalar(k.gtb[:, :], k.bins[:, :], k.y[:, 0:1], None, ALU.is_lt)
        dve.drain()
        dve.tensor_reduce(k.mem[:, :], k.gtb[:, :], AX.X, ALU.add)
        dve.drain()
        dve.tensor_scalar(k.sel[:, :], k.iota8[:, :], k.mem[:, :], None, ALU.is_equal)
        for b in range(BINS):
            dve.drain()
            dve.wait_ge(k.e_ready, i * BINS + b + 1)
            dve.scalar_tensor_tensor(tile_, k.tr[b % 2][:, :], k.sel[:, b:b + 1], tile_,
                                     ALU.mult, ALU.add).then_inc(k.e_used, 1)
        dve.drain()


def pe_program(pe, k):
    ident = k.ident[:, :]
    pe.wait_ge(k.consts, 1)
    pe.wait_ge(k.edge_f, 1)
    for c in range(2):
        for b in range(BPS):
            ins = pe.transpose(k.tr[c][:, b * NS:(b + 1) * NS], k.ef[:, c * SPAN + b * P:c * SPAN + (b + 1) * P],
                               k.ident[0:NS, 0:NS])
    ins.then_inc(k.edgeT_ready, 1)
    pe.wait_ge(k.ov_done, 1)
    for c in range(2):
        ins = pe.transpose(k.acc[0][0:NT, c * NS:(c + 1) * NS], k.ov[:, (2 + c) * NT:(3 + c) * NT],
                           k.ident[0:NS, 0:NS])
    ins.then_inc(k.lowT_ready, 1)
    pe.wait_ge(k.bounds_ready, 1)
    pe.wait_ge(k.edgeT_done, 1)
    pe.matmul(k.tr[0][0:1, 0:NT], k.lh[:, 0:1], k.ident[0:NT, 0:NT], start=True, stop=True)
    pe.matmul(k.tr[0][0:1, NT:3 * NT], k.lh[:, 2:3], k.lt[:, :], start=True, stop=True).then_inc(k.row_ready, 1)
    pe.wait_ge(k.bounds_ready, 2)
    pe.sem_inc(k.oh_used, BPS)

    def counts(t, s):
        first = pe.value_load(k.bnd[0:1, bass.ds(t, 1)], min_val=0, max_val=NS * NT)
        end = pe.value_load(k.bnd[0:1, bass.ds(t + NT, 1)], min_val=1, max_val=NS * NT + 1)
        for c0, n in CHUNKS:
            pe.matmul(k.acc[s][:, c0:c0 + n], k.zero[:, 0:P], k.zero[:, 0:n], start=True, stop=False)
        with pe.Fori(first, end) as n_step:
            for b in range(BPS):
                pe.wait_ge(k.oh_ready, n_step * (2 * BPS) + 2 * b + 2)
                for c0, n in CHUNKS:
                    ins = pe.matmul(k.acc[s][:, c0:c0 + n], k.ohd[b], k.ohs[b][:, c0:c0 + n], start=False, stop=False)
                ins.then_inc(k.oh_used, 1)
        for c0, n in CHUNKS:
            ins = pe.matmul(k.acc[s][:, c0:c0 + n], k.zero[:, 0:P], k.zero[:, 0:n], start=False, stop=True)
        ins.then_inc(k.acc_ready, 1)

    def flip(t, s):
        pe.wait_ge(k.stage_ready, t + 1)
        for b, j0 in enumerate((0, 4, 8)):
            pe.wait_ge(k.at_done, t * 3 + b - 1 if not isinstance(t, int) else max(t * 3 + b - 1, 0))
            for j in range(j0, min(j0 + 4, NT)):
                ins = pe.transpose(k.tr[(s + b) % 2][:, (j - j0) * P:(j - j0 + 1) * P],
                                   k.stage[:, s * NPAD + j * P:s * NPAD + (j + 1) * P], ident)
            ins.then_inc(k.trp_ready, 1)

    counts(0, 0)
    counts(1, 1)
    flip(0, 0)
    with pe.Fori(1, NT // 2) as h:
        pe.wait_ge(k.stage_ready, 2 * h - 1)
        counts(2 * h, 0)
        flip(2 * h - 1, 1)
        counts(2 * h + 1, 1)
        flip(2 * h, 0)
    flip(NT - 1, 1)

    def aggregate(h, f, s, ready, at=None):
        for t in range(NT):
            if f == 0:
                pe.wait_ge(ready, t + 1)
            for c0, n in CHUNKS:
                ins = pe.matmul(k.acc[s][:, c0:c0 + n], h[:, t * D + f * P:t * D + (f + 1) * P],
                                k.AT[:, t * NPAD + c0:t * NPAD + c0 + n], start=(t == 0), stop=(t == NT - 1))
        return ins

    aggregate(k.h0, 0, 0, k.h0_ready).then_inc(k.agg_ready, 1)
    pe.wait_ge(k.dg_ready, 1)
    for t in range(8):
        ins = pe.matmul(k.tr[t // 4][:, (t % 4) * P:(t % 4 + 1) * P], k.ones, k.dg[:, t * P:(t + 1) * P],
                        start=True, stop=True)
    ins.then_inc(k.dinvB_psum, 1)
    pe.wait_ge(k.dinvB_ready, 1)
    for t in range(8, NT):
        ins = pe.matmul(k.tr[0][:, (t - 8) * P:(t - 7) * P], k.ones, k.dg[:, t * P:(t + 1) * P],
                        start=True, stop=True)
    ins.then_inc(k.dinvB_psum, 1)
    for f in range(1, FT):
        if f >= 2:
            pe.wait_ge(k.aggT_done, f - 1)
        aggregate(k.h0, f, f % 2, k.h0_ready).then_inc(k.agg_ready, 1)
    pe.wait_ge(k.w_in, 16)
    for o in range(FT):
        pe.wait_ge(k.aggT_done, FT - 1 if o == 0 else FT)
        if o >= 2:
            pe.wait_ge(k.outT_done, o - 1)
        for f in range(FT):
            if f == FT - 1:
                pe.wait_ge(k.aggT_done, FT)
            for c0, n in CHUNKS:
                ins = pe.matmul(k.acc[o % 2][:, c0:c0 + n], k.w0[:, f * D + o * P:f * D + (o + 1) * P],
                                k.aggT[:, f * NPAD + c0:f * NPAD + c0 + n], start=(f == 0), stop=(f == FT - 1))
        ins.then_inc(k.out_ready, 1)

    def flip_gelu(i):
        pe.wait_ge(k.gelu_done, i + 1)
        pe.wait_ge(k.yT_done, i)
        for o in range(FT):
            ins = pe.transpose(k.TK[:, o * P:(o + 1) * P], k.gt[:, o * P:(o + 1) * P], ident)
        ins.then_inc(k.tk_ready, 1)

    def flip_y(i, par):
        pe.wait_ge(k.y_ready, i + 1)
        for f in range(FT):
            c = par * D + f * P
            ins = pe.transpose(k.YT[:, f * P:(f + 1) * P], k.y[:, c:c + P], ident)
        ins.then_inc(k.yt_ready, 1)

    def queries(i, half):
        pe.wait_ge(k.yT_done, i + 1)
        pe.wait_ge(k.qT_done, i * H + 4 * half)
        for b in range(4):
            h = 4 * half + b
            for f in range(FT):
                ins = pe.matmul(k.Q[:, b * P:(b + 1) * P], k.wq[:, f * H * P + h * P:f * H * P + (h + 1) * P],
                                k.yT[:, f * P:(f + 1) * P], start=(f == 0), stop=(f == FT - 1))
        ins.then_inc(k.q_ready, 1)

    def scores(i, h0):
        for h in (h0, h0 + 1):
            pe.wait_ge(k.qT_done, i * H + h + 1)
            if h >= 2:
                pe.wait_ge(k.topk_done, i * H + h - 1)
            else:
                pe.wait_ge(k.topk_done, i * H)
            for c in range(2):
                half = slice(64 * c, 64 * c + 64)
                ins = pe.matmul(k.S[h % 2][c][:, 0:NK], k.qT[half, h * P:(h + 1) * P],
                                k.keys[half, h * NK:(h + 1) * NK], start=True, stop=True)
            ins.then_inc(k.s_ready, 1)

    pieces = {1: lambda i, p: flip_gelu(i), 4: flip_y, 5: lambda i, p: queries(i, 0), 6: lambda i, p: queries(i, 1),
              7: lambda i, p: scores(i, 0), 8: lambda i, p: scores(i, 2), 9: lambda i, p: scores(i, 4),
              10: lambda i, p: scores(i, 6)}

    def search(i, par):
        for g in sorted(pieces):
            pieces[g](i, par)

    def tile(i, par, ahead):
        for g in range(NG):
            if ahead and g in pieces:
                pieces[g](i + 1, 1 - par)
            pe.wait_ge(k.diag_ready, i * NG + g + 1)
            for s in range(GS):
                slot = ((g % RING) * GS + s) * 2 * D + D
                c = ((g % 2) * GS + s) * P
                ins = pe.matmul(k.O[par], k.diag[:, c:c + P], k.big[:, slot:slot + D],
                                start=(g == 0 and s == 0), stop=(g == NG - 1 and s == GS - 1))
            ins.then_inc(k.grp_done, 1)

    pe.wait_ge(k.wq_in, 16)
    pe.wait_ge(k.keys_in, 16)
    pe.sem_inc(k.grp_done, RING)
    search(0, 0)
    with pe.Fori(0, NT // 2 - 1) as pair:
        tile(pair * 2, 0, True)
        tile(pair * 2 + 1, 1, True)
    tile(NT - 2, 0, True)
    tile(NT - 1, 1, False)

    for f in range(FT):
        if f >= 2:
            pe.wait_ge(k.agg1_done, f - 1)
        aggregate(k.h1, f, f % 2, k.h1_ready).then_inc(k.agg1_ready, 1)
    pe.wait_ge(k.h1_ready, NT + 1)
    pe.wait_ge(k.agg1_done, FT)
    pe.wait_ge(k.x2_done, NT)
    pe.wait_ge(k.w1_in, 16)
    for t in range(NT):
        if t >= 2:
            pe.wait_ge(k.x3_done, t - 1)
        for f in range(FT):
            ins = pe.matmul(k.tr[t % 2][:, :], k.agg1[:, f * NPAD + t * P:f * NPAD + (t + 1) * P],
                            k.w1[:, f * D:(f + 1) * D], start=(f == 0), stop=(f == FT - 1))
        ins.then_inc(k.g1_ready, 1)
    pe.wait_ge(k.we_in, 16 * (BINS - 1))
    pe.wait_ge(k.we7_in, 16)
    pe.wait_ge(k.x3_done, NT)
    with pe.Fori(0, NT) as i:
        pe.wait_ge(k.z_ready, i + 1)
        for f in range(FT):
            ins = pe.transpose(k.YT[:, f * P:(f + 1) * P], k.y[:, f * P:(f + 1) * P], ident)
        ins.then_inc(k.zt_ready, 1)
        pe.wait_ge(k.zT_done, i + 1)
        for b in range(BINS):
            if b >= 2:
                pe.wait_ge(k.e_used, i * BINS + b - 1)
            else:
                pe.wait_ge(k.e_used, i * BINS)
            for f in range(FT):
                ins = pe.matmul(k.tr[b % 2][:, :], k.yT[:, f * P:(f + 1) * P], k.we[b][:, f * D:(f + 1) * D],
                                start=(f == 0), stop=(f == FT - 1))
            ins.then_inc(k.e_ready, 1)


def kernel(**inputs):
    import concourse.bacc as _bacc
    from concourse.bass_utils import run_bass_kernel_spmd as _run

    a = {n: np.asarray(v) for n, v in inputs.items()}

    def cols(v):
        return v.reshape(-1, P).T

    arrays = {
        "in_x": a["x"], "in_src": a["src"], "in_dst": a["dst"],
        "in_w0t": a["L0_gnn_W"].T,
        "in_par": np.concatenate([cols(a["L0_gnn_b"]), cols(a["L0_gnn_gamma"]), cols(a["L0_gnn_beta"]),
                                  cols(a["L0_gnn_beta"]), cols(a["L0_ffn_bq"])], axis=1),
        "in_wq": a["L0_ffn_Wq"],
        "in_keys": a["L0_ffn_keys"].transpose(1, 3, 0, 2).reshape(P, H * NK),
        "in_wdu": np.concatenate([a["L0_ffn_w_down"], a["L0_ffn_w_up"]], axis=1),
        "in_w1": a["L1_gnn_W"], "in_b1": a["L1_gnn_b"], "in_we": a["L1_ffn_W"],
    }
    arrays = {n: np.ascontiguousarray(v) for n, v in arrays.items()}
    nc = _bacc.Bacc("TRN2", target_bir_lowering=False, num_devices=1)
    args = [nc.dram_tensor(n, v.shape, mybir.dt.from_np(v.dtype), kind="ExternalInput").ap()
            for n, v in arrays.items()]
    args.append(nc.dram_tensor("out", (N, D), F32, kind="ExternalOutput").ap())
    program(nc, *args)
    r = _run(nc, [arrays], core_ids=[0])
    return r.results[0]["out"]
```

```python
from contextlib import ExitStack

import numpy as np
import concourse.bass as bass
from concourse import mybir

F32 = mybir.dt.float32
F16 = mybir.dt.float16
I32 = mybir.dt.int32
U32 = mybir.dt.uint32
ALU = mybir.AluOpType
ACT = mybir.ActivationFunctionType
AX = mybir.AxisListType

P = 128
N = 1250
D = 512
E = 21250
NT = -(-N // P)
NPAD = NT * P
LAST = N - (NT - 1) * P
FT = D // P
H = 8
NK = 256
HK = H * 8
EPS = 1e-5
BPS = 4
SPAN = BPS * P
NS = -(-E // SPAN)
TAIL = E - (NS - 1) * SPAN
NO_NODE = 4096
FAR = 1000.0
CHUNKS = [(0, 512), (512, 512), (1024, N - 1024)]
GS = 4
NG = HK // GS
RING = 4
BINS = 8
SLOTS = (NPAD + BINS * (P - 1)) // P
ROW = 2 * D + 1
ID0 = 2000.0
XR = 4


class Net:
    pass


def lay_out(nc, ctx, k):
    def sb(name, cols, dt=F32, rows=P):
        return ctx.enter_context(nc.sbuf_tensor(name, [rows, cols], dt))

    k.AT = sb("AT", NT * NPAD)
    k.x = sb("x", NT * D)
    k.big = sb("big", 16 * 1024)
    k.qk = sb("qk", 4096 + 2048)
    k.outT = sb("outT", FT * NPAD)
    k.y = sb("y", 2 * D)
    k.yT = sb("yT", D)
    k.qT = sb("qT", H * P)
    k.gt = sb("gt", D)
    k.diag = sb("diag", 2 * GS * P)
    k.b1 = k.gt
    k.h0 = k.big[:, 0:5120]
    k.ei = k.big[0:NS, 0:2 * SPAN].bitcast(I32)
    k.ef = k.big[0:NS, 2 * SPAN:4 * SPAN]
    k.aggT = k.big[:, 5120:10240]
    k.stage = k.big[:, 10240:12800]
    k.w0 = k.big[:, 12800:14848]
    k.dinvB = k.big[:, 14848:16128]
    k.zero = k.big[:, 2048:2304].bitcast(F16)
    k.dstp = k.big[:, 4096:4096 + BPS * NS]
    k.srcp = k.big[:, 4096 + BPS * NS:4096 + 2 * BPS * NS]
    k.iota = k.big[:, 4440:4440 + NPAD // 2].bitcast(F16)
    k.ones = k.big[:, 16128:16256]
    k.iotai = k.big[:, 5120:5120 + NPAD].bitcast(I32)
    oh = k.outT[:, 0:BPS * (NPAD + P) // 2].bitcast(F16)
    k.ohs = [oh[:, b * NPAD:(b + 1) * NPAD] for b in range(BPS)]
    k.ohd = [oh[:, BPS * NPAD + b * P:BPS * NPAD + (b + 1) * P] for b in range(BPS)]
    k.dg = k.outT[:, 0:NT * P]
    k.wq = k.qk[:, 0:4096]
    k.keys = k.qk[:, 4096:6144]
    k.h1 = k.outT[:, 0:NT * D]
    k.agg1 = k.qk[:, 0:FT * NPAD]
    k.w1 = [k.qT[:, 0:D], k.qT[:, D:2 * D], k.diag[:, 0:D], k.diag[:, D:2 * D]]
    k.zx = [k.AT[:, t * ROW:(t + 1) * ROW] for t in range(NT)]
    k.zxv = k.AT[:, 0:NT * ROW].rearrange("p (t c) -> p t c", c=ROW)
    k.upper = k.y[:, 0:P]
    k.ones1 = k.y[:, P:2 * P]
    k.xb = [k.x[:, r * NPAD:r * NPAD + ROW] for r in range(XR)]
    k.zT = [k.yT, k.gt]
    k.ident = sb("ident", P)
    k.eps = sb("eps", 1)
    k.thr = sb("thr", NT)
    k.thri = sb("thri", NT, I32)
    k.qcol = sb("qcol", 2, rows=NS)
    k.qcoli = sb("qcoli", 1, I32, rows=NS)
    k.lt = sb("lt", 2 * NT, rows=NT)
    k.iota8 = sb("iota8", 8)
    k.iota8i = sb("iota8i", 8, I32)
    k.bins = sb("bins", BINS - 1)
    k.par = sb("par", 4 * FT + H)
    k.mm = sb("mm", 2, rows=NS)
    k.ov = k.big[0:NS, 2304:2304 + 4 * NT]
    k.lh = sb("lh", 4, rows=NT)
    k.row = sb("row", 3 * NT, rows=1)
    k.bnd = sb("bnd", 3 * NT, I32, rows=1)
    k.st = sb("st", 6 * NT)
    k.mv = sb("mv", 2 * NT)
    k.rs = sb("rs", 2 * NT)
    k.pq = sb("pq", 2 * NT)
    k.degin = sb("degin", NT)
    k.deg = sb("deg", 3 * NT)
    k.dsq = sb("dsq", 3 * NT)
    k.dri = sb("dri", 3 * NT)
    k.comb = sb("comb", NT)
    k.bst = sb("bst", FT * 3 * 6)
    k.bmv = sb("bmv", 2 * FT)
    k.bsd = sb("bsd", FT)
    k.bsc = sb("bsc", 2 * FT)
    k.tst = sb("tst", 6)
    k.tmv = sb("tmv", 2)
    k.tsd = sb("tsd", 2)
    k.top = sb("top", 2 * HK)
    k.topi = sb("topi", 2 * HK, U32)
    k.topf = sb("topf", 2 * HK)
    k.best = sb("best", HK)
    k.pos = sb("pos", HK, U32)
    k.posab = sb("posab", 2 * HK, U32)
    k.posf = sb("posf", 2 * HK)
    k.pick = sb("pick", 2 * H * 64)
    k.all = k.pick[:, 0:H * 64]
    k.iab = k.posf
    k.idx = [sb(f"idx{b}", HK, I32) for b in range(2)]
    k.sm = sb("sm", HK)
    k.ex = k.sm
    k.ssum = sb("ssum", 2 * H)
    k.prob = sb("prob", 2 * HK)
    k.inner = sb("inner", HK)
    k.val = sb("val", HK)
    def piece(at, n):
        return k.pick[:, at:at + n]
    k.gtb = piece(0, NT * (BINS - 1))
    k.mem = piece(80, NT)
    k.sel = piece(96, NT * BINS)
    k.rank = piece(176, NT * BINS)
    k.cnt = piece(256, (NT + 1) * BINS)
    k.cmp = piece(344, BINS * NT)
    k.tiles = piece(424, BINS)
    k.base = piece(432, BINS)
    k.lt8 = piece(440, BINS * BINS)
    k.posn = piece(504, NT)
    k.binf = piece(520, SLOTS)
    k.cmps = piece(544, SLOTS * BINS)
    k.iotas = piece(680, SLOTS)
    k.iotasi = piece(700, SLOTS).bitcast(I32)
    k.bini = piece(720, SLOTS).bitcast(I32)
    k.posi = piece(740, NT).bitcast(I32)
    k.ids = piece(752, NT).bitcast(I32)
    k.oid = [piece(764 + r, 1).bitcast(I32) for r in range(XR)]

    def ps(name, cols, dt=F32):
        return ctx.enter_context(nc.psum_tensor(name, [P, cols], dt))

    k.acc = [ps(f"acc{s}", 3 * 512) for s in range(2)]
    k.tr = [ps(f"tr{s}", 512) for s in range(2)]
    banks = [k.acc[s][:, b * 512:(b + 1) * 512] for s in range(2) for b in range(3)]
    k.TK = k.YT = banks[0]
    k.ZB = banks[0:2]
    k.RK = banks[4:6]
    k.Q = banks[1]
    k.S = [banks[2:4], banks[4:6]]
    k.O = [k.tr[0][:, :], k.tr[1][:, :]]




def program(nc, x_d, src_d, dst_d, w0t_d, par_d, wq_d, keys_d, wdu_d, w1_d, b1_d, we_d, out_d):
    k = Net()
    with ExitStack() as ctx:
        k.nc = nc
        lay_out(nc, ctx, k)

        def sem(name):
            return ctx.enter_context(nc.semaphore(name))

        k.ring_free = sem("ring_free")
        k.s_seen = sem("s_seen")
        k.consts = sem("consts")
        k.edges_pre = sem("edges_pre")
        k.xpad = sem("xpad")
        k.edges_in = sem("edges_in")
        k.x_in = sem("x_in")
        k.w_in = sem("w_in")
        k.par_in = sem("par_in")
        k.wq_in = sem("wq_in")
        k.keys_in = sem("keys_in")
        k.b1_in = sem("b1_in")
        k.edge_f = sem("edge_f")
        k.ov_done = sem("ov_done")
        k.stats0 = sem("stats0")
        k.sd0_ready = sem("sd0_ready")
        k.edgeT_ready = sem("edgeT_ready")
        k.edgeT_done = sem("edgeT_done")
        k.lowT_ready = sem("lowT_ready")
        k.lh_ready = sem("lh_ready")
        k.row_ready = sem("row_ready")
        k.bounds_ready = sem("bounds_ready")
        k.oh_ready = sem("oh_ready")
        k.oh_used = sem("oh_used")
        k.acc_ready = sem("acc_ready")
        k.stage_ready = sem("stage_ready")
        k.trp_ready = sem("trp_ready")
        k.at_done = sem("at_done")
        k.degs_ready = sem("degs_ready")
        k.degsq_ready = sem("degsq_ready")
        k.dego_ready = sem("dego_ready")
        k.degosq_ready = sem("degosq_ready")
        k.h0_ready = sem("h0_ready")
        k.dg_ready = sem("dg_ready")
        k.dinvB_psum = sem("dinvB_psum")
        k.dinvB_ready = sem("dinvB_ready")
        k.agg_ready = sem("agg_ready")
        k.aggT_done = sem("aggT_done")
        k.out_ready = sem("out_ready")
        k.outT_done = sem("outT_done")
        k.bnvar_ready = sem("bnvar_ready")
        k.bnsd_ready = sem("bnsd_ready")
        k.bn_ready = sem("bn_ready")
        k.gelu_done = sem("gelu_done")
        k.tk_ready = sem("tk_ready")
        k.x1_done = sem("x1_done")
        k.var_ready = sem("var_ready")
        k.sd_ready = sem("sd_ready")
        k.y_ready = sem("y_ready")
        k.yt_ready = sem("yt_ready")
        k.yT_done = sem("yT_done")
        k.q_ready = sem("q_ready")
        k.qT_done = sem("qT_done")
        k.s_ready = sem("s_ready")
        k.topk_done = sem("topk_done")
        k.idx_ready = sem("idx_ready")
        k.exp_in = sem("exp_in")
        k.exp_done = sem("exp_done")
        k.prob_ready = sem("prob_ready")
        k.val_ready = sem("val_ready")
        k.diag_ready = sem("diag_ready")
        k.grp_done = sem("grp_done")
        k.x2_done = sem("x2_done")
        k.stats1 = sem("stats1")
        k.sd1_ready = sem("sd1_ready")
        k.h1_ready = sem("h1_ready")
        k.agg1_ready = sem("agg1_ready")
        k.agg1_done = sem("agg1_done")
        k.g1_ready = sem("g1_ready")
        k.x3_done = sem("x3_done")
        k.var4_ready = sem("var4_ready")
        k.sd4_ready = sem("sd4_ready")
        k.z_ready = sem("z_ready")
        k.zt_ready = sem("zt_ready")
        k.zT_done = sem("zT_done")
        k.e_ready = sem("e_ready")
        k.w1_in = sem("w1_in")
        k.we_in = sem("we_in")
        k.cleared = sem("cleared")
        k.e_consts = sem("e_consts")
        k.ids_ready = sem("ids_ready")
        k.sel_ready = sem("sel_ready")
        k.rank_psum = sem("rank_psum")
        k.pos_ready = sem("pos_ready")
        k.sorted = sem("sorted")
        k.x4_done = sem("x4_done")
        k.x4_seen = sem("x4_seen")
        k.loaded = [sem(f"loaded{r}") for r in range(XR)]
        k.stored = [sem(f"stored{r}") for r in range(XR)]
        k.landed = [ctx.enter_context(nc.semaphore(f"landed{r}")) for r in range(RING)]
        k.x_d, k.src_d, k.dst_d, k.w0t_d, k.par_d, k.wq_d = x_d, src_d, dst_d, w0t_d, par_d, wq_d
        k.zs_d = nc.dram_tensor("sorted_rows", (SLOTS * P, ROW), F32).ap()
        k.keys_d, k.wdu_d, k.w1_d, k.b1_d, k.we_d, k.out_d = keys_d, wdu_d, w1_d, b1_d, we_d, out_d
        block = ctx.enter_context(nc.Block())

        @block.sync
        def _(sp):
            sync_program(sp, k)

        @block.gpsimd
        def _(pool):
            pool_program(pool, k)

        @block.scalar
        def _(act):
            act_program(act, k)

        @block.vector
        def _(dve):
            dve_program(dve, k)

        @block.tensor
        def _(pe):
            pe_program(pe, k)


def sync_program(sp, k):
    sp.wait_ge(k.edges_pre, 1)
    full = (NS - 1) * SPAN
    for c, d in enumerate((k.dst_d, k.src_d)):
        cols = slice(c * SPAN, (c + 1) * SPAN)
        sp.dma_start(k.ei[0:NS - 1, cols], d[0:full].rearrange("(q n) -> q n", n=SPAN)).then_inc(k.edges_in, 16)
        sp.dma_start(k.ei[NS - 1:NS, c * SPAN:c * SPAN + TAIL],
                     d[full:E].rearrange("(q n) -> q n", q=1)).then_inc(k.edges_in, 16)
    sp.wait_ge(k.xpad, 1)
    sp.dma_start(k.x[:, 0:(NT - 1) * D].rearrange("p (t d) -> p t d", d=D),
                 k.x_d[0:(NT - 1) * P, :].rearrange("(t p) d -> p t d", p=P)).then_inc(k.x_in, 16)
    sp.dma_start(k.x[0:LAST, (NT - 1) * D:NT * D], k.x_d[(NT - 1) * P:N, :]).then_inc(k.x_in, 16)
    sp.wait_ge(k.consts, 1)
    zeros = k.zs_d.rearrange("(p t) c -> p (t c)", p=P)
    for c0 in range(0, SLOTS * ROW, 2 * NPAD):
        n = min(2 * NPAD, SLOTS * ROW - c0)
        sp.dma_start(zeros[:, c0:c0 + n], k.stage[:, 0:n]).then_inc(k.cleared, 16)
    sp.dma_start(k.w0.rearrange("p (f n) -> p f n", n=D),
                 k.w0t_d.rearrange("(f p) n -> p f n", p=P)).then_inc(k.w_in, 16)
    sp.dma_start(k.par[:, :], k.par_d).then_inc(k.par_in, 16)
    sp.dma_start(k.wq.rearrange("p (f n) -> p f n", n=H * P),
                 k.wq_d.rearrange("(f p) n -> p f n", p=P)).then_inc(k.wq_in, 16)
    sp.dma_start(k.keys, k.keys_d).then_inc(k.keys_in, 16)
    sp.wait_ge(k.grp_done, NT * NG + RING)
    sp.wait_ge(k.x2_done, NT)
    sp.dma_start(k.b1[:, :], k.b1_d.partition_broadcast(P)).then_inc(k.b1_in, 16)
    for f in range(FT):
        sp.dma_start(k.w1[f], k.w1_d[f * P:(f + 1) * P, :]).then_inc(k.w1_in, 16)
    for b in range(BINS):
        sp.dma_start(k.big[:, b * 2048:(b + 1) * 2048].rearrange("p (f n) -> p f n", n=D),
                     k.we_d[b].rearrange("(f p) n -> p f n", p=P)).then_inc(k.we_in, 16)
    sp.wait_ge(k.sorted, 16 * NT)
    for r in range(XR):
        sp.dma_start(k.xb[r], k.zs_d[r * P:(r + 1) * P, :]).then_inc(k.loaded[r], 16)
    with sp.Fori(1, SLOTS // XR) as q:
        for r in range(XR):
            sp.wait_ge(k.stored[r], q * 16)
            sp.dma_start(k.xb[r], k.zs_d[bass.ds(q * (XR * P) + r * P, P), :]).then_inc(k.loaded[r], 16)
    for m in range(SLOTS // XR * XR, SLOTS):
        sp.wait_ge(k.stored[m % XR], 16 * (m // XR))
        sp.dma_start(k.xb[m % XR], k.zs_d[m * P:(m + 1) * P, :]).then_inc(k.loaded[m % XR], 16)
    for r in range(XR):
        sp.wait_ge(k.stored[r], 16 * len(range(r, SLOTS, XR)))


def pool_program(pool, k):
    pool.memset(k.ei, NO_NODE).then_inc(k.edges_pre, 1)
    pool.memset(k.x[:, (NT - 1) * D:NT * D], 0.0).then_inc(k.xpad, 1)
    pool.memset(k.ident[:, :], 0.0)
    pool.memset(k.lt[:, :], 0.0)
    pool.memset(k.ones, 1.0)
    pool.memset(k.zero, 0.0)
    pool.memset(k.eps[:, :], EPS)
    pool.memset(k.stage, 0.0)
    pool.iota(k.iotai, pattern=[[1, NPAD]], base=0, channel_multiplier=0)
    pool.iota(k.thri[:, :], pattern=[[P, NT]], base=0, channel_multiplier=0)
    pool.iota(k.qcoli[:, :], pattern=[[0, 1]], base=0, channel_multiplier=1)
    pool.iota(k.iota8i[:, :], pattern=[[1, 8]], base=0, channel_multiplier=0)
    pool.drain()
    pool.affine_select(out=k.ident[:, :], in_=k.ident[:, :], compare_op=ALU.not_equal, fill=1.0, base=0,
                       pattern=[[-1, P]], channel_multiplier=1)
    pool.affine_select(out=k.lt[:, 0:NT], in_=k.lt[:, 0:NT], compare_op=ALU.is_ge, fill=1.0, base=0,
                       pattern=[[-1, NT]], channel_multiplier=1)
    pool.affine_select(out=k.lt[:, NT:2 * NT], in_=k.lt[:, NT:2 * NT], compare_op=ALU.is_gt, fill=1.0, base=0,
                       pattern=[[-1, NT]], channel_multiplier=1)
    pool.tensor_copy(k.iota, k.iotai)
    pool.tensor_copy(k.thr[:, :], k.thri[:, :])
    pool.tensor_copy(k.iota8[:, :], k.iota8i[:, :])
    pool.drain()
    pool.tensor_scalar(k.qcol[:, 0:1], k.qcoli[:, :], -FAR, None, ALU.add)
    pool.tensor_scalar(k.qcol[:, 1:2], k.qcoli[:, :], 1.0, None, ALU.add)
    pool.tensor_scalar(k.bins[:, :], k.iota8[:, 0:BINS - 1], 0.5, -1.5, ALU.mult, ALU.add)
    pool.drain().then_inc(k.consts, 1)

    def gather_tile(i, par):
        pool.wait_ge(k.idx_ready, i + 1)
        for g in range(NG):
            r = g % RING
            pool.wait_ge(k.val_ready, i * NG + g + 1)
            pool.wait_ge(k.grp_done, i * NG + g + 1)
            pool.sem_inc(k.ring_free, 1)
            for s in range(GS):
                j = g * GS + s
                slot = r * GS + s
                pool.indirect_dma_start(
                    out=k.big[:, slot * 2 * D:(slot + 1) * 2 * D], out_offset=None, in_=k.wdu_d,
                    in_offset=bass.IndirectOffsetOnAxis(ap=k.idx[par][:, j:j + 1], axis=0),
                ).then_inc(k.landed[r], 16)

    with pool.Fori(0, NT // 2) as pair:
        gather_tile(pair * 2, 0)
        gather_tile(pair * 2 + 1, 1)

    pool.wait_ge(k.x2_done, NT)
    pool.memset(k.upper, 0.0)
    pool.memset(k.ones1, 1.0)
    pool.iota(k.iotasi, pattern=[[1, SLOTS]], base=0, channel_multiplier=0)
    pool.iota(k.ids, pattern=[[P, NT]], base=0, channel_multiplier=1)
    pool.drain()
    pool.affine_select(out=k.upper, in_=k.upper, compare_op=ALU.is_ge, fill=1.0, base=0,
                       pattern=[[-1, P]], channel_multiplier=1)
    pool.tensor_copy(k.iotas, k.iotasi)
    pool.drain().then_inc(k.e_consts, 1)
    pool.wait_ge(k.agg1_ready, FT)
    pool.tensor_scalar(k.zxv[:, :, 2 * D:ROW], k.ids.unsqueeze(2), -1.0, ID0, ALU.mult, ALU.add)
    pool.drain().then_inc(k.ids_ready, 1)
    pool.wait_ge(k.cleared, 16 * -(-SLOTS * ROW // (2 * NPAD)))
    pool.wait_ge(k.pos_ready, 1)
    for t in range(NT):
        pool.indirect_dma_start(out=k.zs_d, out_offset=bass.IndirectOffsetOnAxis(ap=k.posi[:, t:t + 1], axis=0),
                                in_=k.zx[t], in_offset=None).then_inc(k.sorted, 16)

    def store(m, r):
        pool.wait_ge(k.x4_done, m + 3)
        pool.sem_inc(k.x4_seen, 1)
        pool.indirect_dma_start(out=k.out_d, out_offset=bass.IndirectOffsetOnAxis(ap=k.oid[r], axis=0),
                                in_=k.xb[r][:, D:2 * D], in_offset=None, bounds_check=N - 1,
                                oob_is_err=False).then_inc(k.stored[r], 16)

    with pool.Fori(0, SLOTS // XR) as q:
        for r in range(XR):
            store(q * XR + r, r)
    for m in range(SLOTS // XR * XR, SLOTS):
        store(m, m % XR)


def act_program(act, k):
    copy = ACT.Copy
    act.wait_ge(k.consts, 1)
    act.wait_ge(k.edgeT_ready, 1)
    act.activation(k.dstp, k.tr[0][:, 0:BPS * NS], copy)
    act.activation(k.srcp, k.tr[1][:, 0:BPS * NS], copy).then_inc(k.edgeT_done, 1)
    act.wait_ge(k.row_ready, 1)
    act.activation(k.row[:, :], k.tr[0][0:1, 0:3 * NT], copy).then_inc(k.lh_ready, 1)
    act.wait_ge(k.stats0, 1)
    act.activation(k.rs[:, 0:NT], k.mv[:, NT:2 * NT], ACT.Sqrt, bias=k.eps[:, :]).then_inc(k.sd0_ready, 1)

    def count_rows(t, s):
        act.wait_ge(k.acc_ready, t + 1)
        act.wait_ge(k.trp_ready, t * 3 - 3)
        act.activation(k.stage[:, s * NPAD:s * NPAD + N], k.acc[s][:, 0:N], copy,
                       accum_out=k.degin[:, bass.ds(t, 1)]).then_inc(k.stage_ready, 1)

    def count_cols(t, s):
        at = k.AT[:, :].rearrange("p (j c) -> p j c", c=NPAD)
        for b, j0 in enumerate((0, 4, 8)):
            n = min(4, NT - j0)
            act.wait_ge(k.trp_ready, t * 3 + b + 1)
            act.activation(at[:, j0:j0 + n, bass.ds(t * P, P)],
                           k.tr[(s + b) % 2][:, 0:n * P].rearrange("p (j c) -> p j c", c=P),
                           copy).then_inc(k.at_done, 1)

    act.wait_ge(k.acc_ready, 1)
    act.wait_ge(k.cleared, 16 * -(-SLOTS * ROW // (2 * NPAD)))
    act.activation(k.stage[:, 0:N], k.acc[0][:, 0:N], copy, accum_out=k.degin[:, 0:1]).then_inc(k.stage_ready, 1)
    act.wait_ge(k.acc_ready, 2)
    act.activation(k.stage[:, NPAD:NPAD + N], k.acc[1][:, 0:N], copy,
                   accum_out=k.degin[:, 1:2]).then_inc(k.stage_ready, 1)
    count_cols(0, 0)
    with act.Fori(1, NT // 2) as h:
        count_rows(2 * h, 0)
        count_cols(2 * h - 1, 1)
        count_rows(2 * h + 1, 1)
        count_cols(2 * h, 0)
    count_cols(NT - 1, 1)

    act.wait_ge(k.degs_ready, 1)
    act.activation(k.dsq[:, 0:2 * NT], k.deg[:, 0:2 * NT], ACT.Sqrt).then_inc(k.degsq_ready, 1)
    act.wait_ge(k.dinvB_psum, 1)
    act.activation(k.dinvB[:, 0:512], k.tr[0][:, :], copy)
    act.activation(k.dinvB[:, 512:1024], k.tr[1][:, :], copy).then_inc(k.dinvB_ready, 1)
    act.wait_ge(k.dinvB_psum, 2)
    act.activation(k.dinvB[:, 1024:NPAD], k.tr[0][:, 0:NPAD - 1024], copy).then_inc(k.dinvB_ready, 1)
    act.wait_ge(k.dego_ready, 1)
    act.activation(k.dsq[:, 2 * NT:3 * NT], k.deg[:, 2 * NT:3 * NT], ACT.Sqrt).then_inc(k.degosq_ready, 1)
    act.wait_ge(k.par_in, 16)
    for o in range(FT):
        act.wait_ge(k.out_ready, o + 1)
        act.activation(k.outT[:, o * NPAD:o * NPAD + N], k.acc[o % 2][:, 0:N], ACT.Identity,
                       bias=k.par[:, o:o + 1]).then_inc(k.outT_done, 1)
    act.wait_ge(k.bnvar_ready, 1)
    act.activation(k.bsd[:, :], k.bmv[:, FT:2 * FT], ACT.Sqrt, bias=k.eps[:, :]).then_inc(k.bnsd_ready, 1)
    act.wait_ge(k.bn_ready, 1)

    def gelu(i):
        act.wait_ge(k.tk_ready, i)
        for o in range(FT):
            ins = act.activation(k.gt[:, o * P:(o + 1) * P], k.outT[:, bass.ds(i * P + o * NPAD, P)], ACT.Gelu,
                                 bias=k.bsc[:, FT + o:FT + o + 1], scale=k.bsc[:, o:o + 1])
        ins.then_inc(k.gelu_done, 1)

    def root(i):
        act.wait_ge(k.var_ready, i + 1)
        act.activation(k.tsd[:, 0:1], k.tmv[:, 1:2], ACT.Sqrt, bias=k.eps[:, :]).then_inc(k.sd_ready, 1)

    def copy_yT(i):
        act.wait_ge(k.yt_ready, i + 1)
        act.activation(k.yT[:, :], k.YT, copy).then_inc(k.yT_done, 1)

    def copy_q(i, half):
        act.wait_ge(k.q_ready, 2 * i + half + 1)
        if half == 0:
            act.wait_ge(k.s_ready, i * H)
        for b in range(4):
            h = 4 * half + b
            act.activation(k.qT[:, h * P:(h + 1) * P], k.Q[:, b * P:(b + 1) * P], ACT.Identity,
                           bias=k.par[:, 4 * FT + h:4 * FT + h + 1]).then_inc(k.qT_done, 1)

    def exps(i):
        act.wait_ge(k.exp_in, i + 1)
        act.activation(k.ex[:, :], k.sm[:, :], ACT.Exp).then_inc(k.exp_done, 1)

    pieces = {0: gelu, 3: root, 5: copy_yT, 6: lambda i: copy_q(i, 0), 7: lambda i: copy_q(i, 1), 13: exps}

    def search(i):
        for g in sorted(pieces):
            pieces[g](i)

    def tile(i, par, ahead):
        for g in range(NG):
            if ahead and g in pieces:
                pieces[g](i + 1)
            act.wait_ge(k.val_ready, i * NG + g + 1 + RING)
            act.wait_ge(k.grp_done, i * NG + g - 1 + RING)
            for s in range(GS):
                j = g * GS + s
                ins = act.activation(k.diag[:, ((g % 2) * GS + s) * P:((g % 2) * GS + s + 1) * P], k.ident[:, :],
                                     copy, scale=k.val[:, j:j + 1])
            ins.then_inc(k.diag_ready, 1)

    search(0)
    with act.Fori(0, NT // 2 - 1) as pair:
        tile(pair * 2, 0, True)
        tile(pair * 2 + 1, 1, True)
    tile(NT - 2, 0, True)
    tile(NT - 1, 1, False)

    act.wait_ge(k.stats1, 1)
    act.activation(k.rs[:, 0:NT], k.mv[:, NT:2 * NT], ACT.Sqrt, bias=k.eps[:, :]).then_inc(k.sd1_ready, 1)
    for f in range(FT):
        act.wait_ge(k.agg1_ready, f + 1)
        act.activation(k.agg1[:, f * NPAD:f * NPAD + N], k.acc[f % 2][:, 0:N], copy).then_inc(k.agg1_done, 1)
    with act.Fori(0, NT) as t:
        act.wait_ge(k.var4_ready, t + 1)
        act.activation(k.rs[:, bass.ds(t, 1)], k.mv[:, bass.ds(t + NT, 1)], ACT.Sqrt,
                       bias=k.eps[:, :]).then_inc(k.sd4_ready, 1)

    def copy_zT(m, par):
        act.wait_ge(k.zt_ready, m + 1)
        act.activation(k.zT[par][:, :], k.ZB[par], copy).then_inc(k.zT_done, 1)

    with act.Fori(0, SLOTS // 2) as h:
        copy_zT(2 * h, 0)
        copy_zT(2 * h + 1, 1)
    copy_zT(SLOTS - 1, 0)


def dve_program(dve, k):
    def stats(tile, t):
        dve.bn_stats(k.st[:, 6 * t:6 * t + 6], tile)

    dve.wait_ge(k.edges_in, 64)
    dve.tensor_copy(k.ef, k.ei).then_inc(k.edge_f, 1)
    dve.drain()
    dve.tensor_reduce(k.mm[:, 0:1], k.ef[:, 0:SPAN], AX.X, ALU.min)
    dve.tensor_reduce(k.mm[:, 1:2], k.ef[:, 0:SPAN], AX.X, ALU.max)
    dve.wait_ge(k.consts, 1)
    dve.drain()
    a, b = k.ov[:, 0:NT], k.ov[:, NT:2 * NT]
    low, high = k.ov[:, 2 * NT:3 * NT], k.ov[:, 3 * NT:4 * NT]
    dve.tensor_scalar(a, k.thr[0:NS, :], k.mm[:, 1:2], None, ALU.is_le)
    dve.tensor_scalar(b, k.thr[0:NS, :], float(P), k.mm[:, 0:1], ALU.add, ALU.is_gt)
    dve.drain()
    dve.tensor_tensor(a, a, b, ALU.mult)
    dve.drain()
    dve.tensor_scalar(low, a, k.qcol[:, 0:1], FAR, ALU.mult, ALU.add)
    dve.tensor_scalar(high, a, k.qcol[:, 1:2], None, ALU.mult)
    dve.drain().then_inc(k.ov_done, 1)
    dve.wait_ge(k.lowT_ready, 1)
    lo, hi, ln, pos = (k.lh[:, c:c + 1] for c in range(4))
    dve.tensor_reduce(lo, k.acc[0][0:NT, 0:NS], AX.X, ALU.min)
    dve.tensor_reduce(hi, k.acc[0][0:NT, NS:2 * NS], AX.X, ALU.max)
    dve.drain()
    dve.tensor_scalar(pos, hi, 0.0, None, ALU.is_gt)
    dve.tensor_scalar(hi, hi, 1.0, None, ALU.max)
    dve.drain()
    dve.tensor_tensor(lo, lo, pos, ALU.mult)
    dve.drain()
    dve.tensor_tensor(ln, hi, lo, ALU.subtract)
    dve.drain().then_inc(k.bounds_ready, 1)
    dve.wait_ge(k.lh_ready, 1)
    dve.tensor_copy(k.bnd[:, 0:2 * NT], k.row[:, NT:3 * NT])
    dve.tensor_tensor(k.bnd[:, 2 * NT:3 * NT], k.row[:, 0:NT], k.row[:, NT:2 * NT], ALU.subtract)
    dve.drain().then_inc(k.bounds_ready, 1)
    dve.wait_ge(k.x_in, 32)
    for t in range(NT):
        stats(k.x[:, t * D:(t + 1) * D], t)
    dve.drain()
    mv = k.mv[:, :].rearrange("p (c t) -> p t c", c=2)
    for t in range(NT):
        dve.bn_aggr(mv[:, t, :], k.st[:, 6 * t:6 * t + 6])
    dve.drain().then_inc(k.stats0, 1)
    dve.wait_ge(k.edgeT_done, 1)
    with dve.Fori(0, NT) as t:
        first = dve.value_load(k.bnd[0:1, bass.ds(t, 1)], min_val=0, max_val=NS * NT)
        end = dve.value_load(k.bnd[0:1, bass.ds(t + NT, 1)], min_val=1, max_val=NS * NT + 1)
        shift = dve.value_load(k.bnd[0:1, bass.ds(t + 2 * NT, 1)], min_val=-NS * NT, max_val=NS)
        with dve.Fori(first, end) as n:
            q = k.nc.s_assert_within(dve.snap(n + shift), 0, NS - 1,
                                       skip_runtime_bounds_check_because="first <= n < end, so lo <= q < hi <= NS")
            for c in range(BPS):
                dve.wait_ge(k.oh_used, n * BPS + c + 1)
                dve.tensor_scalar(k.ohs[c][:, 0:N], k.iota[:, 0:N], k.srcp[:, bass.ds(q + c * NS, 1)], None,
                                  ALU.is_equal).then_inc(k.oh_ready, 1)
                dve.tensor_scalar(k.ohd[c], k.iota[:, bass.ds(t * P, P)], k.dstp[:, bass.ds(q + c * NS, 1)], None,
                                  ALU.is_equal).then_inc(k.oh_ready, 1)

    dve.wait_ge(k.stage_ready, NT)
    dve.tensor_scalar(k.deg[:, 0:NT], k.degin[:, :], 1.0, None, ALU.add)
    dve.tensor_scalar(k.deg[:, NT:2 * NT], k.degin[:, :], 1.0, None, ALU.max)
    dve.drain().then_inc(k.degs_ready, 1)
    dve.wait_ge(k.sd0_ready, 1)
    dve.reciprocal(k.rs[:, NT:2 * NT], k.rs[:, 0:NT])
    dve.wait_ge(k.degsq_ready, 1)
    dve.reciprocal(k.dri[:, 0:2 * NT], k.dsq[:, 0:2 * NT])
    dve.drain()
    dve.tensor_tensor(k.comb[:, :], k.rs[:, NT:2 * NT], k.dri[:, 0:NT], ALU.mult)
    dve.tensor_scalar(k.pq[:, 0:NT], k.rs[:, NT:2 * NT], 1.0, None, ALU.add)
    dve.tensor_tensor(k.pq[:, NT:2 * NT], k.rs[:, NT:2 * NT], k.mv[:, 0:NT], ALU.mult)
    dve.wait_ge(k.at_done, 3 * NT)
    dve.drain()
    for t in range(NT):
        diag = k.AT[:, t * NPAD + t * P:t * NPAD + (t + 1) * P]
        dve.tensor_tensor(diag, diag, k.ident[:, :], ALU.add)
        dve.tensor_scalar(k.h0[:, t * D:(t + 1) * D], k.x[:, t * D:(t + 1) * D], k.mv[:, t:t + 1],
                          k.comb[:, t:t + 1], ALU.subtract, ALU.mult)
        dve.drain().then_inc(k.h0_ready, 1)
    for t in range(NT):
        dve.tensor_scalar(k.dg[:, t * P:(t + 1) * P], k.ident[:, :], k.dri[:, t:t + 1], None, ALU.mult)
    dve.drain().then_inc(k.dg_ready, 1)
    dve.tensor_reduce(k.degin[:, :], k.AT[:, :].rearrange("p (j c) -> p j c", c=NPAD), AX.X, ALU.add)
    dve.drain()
    dve.tensor_scalar(k.deg[:, 2 * NT:3 * NT], k.degin[:, :], -1.0, 1.0, ALU.add, ALU.max)
    dve.drain().then_inc(k.dego_ready, 1)
    for t in range(NT):
        tile = k.x[:, t * D:(t + 1) * D]
        dve.tensor_scalar(tile, tile, k.pq[:, t:t + 1], k.pq[:, NT + t:NT + t + 1], ALU.mult, ALU.subtract)
    dve.wait_ge(k.degosq_ready, 1)
    dve.reciprocal(k.dri[:, 2 * NT:3 * NT], k.dsq[:, 2 * NT:3 * NT])
    dve.wait_ge(k.dinvB_ready, 2)
    for f in range(FT):
        dve.wait_ge(k.agg_ready, f + 1)
        dve.tensor_tensor(k.aggT[:, f * NPAD:f * NPAD + N], k.acc[f % 2][:, 0:N], k.dinvB[:, 0:N],
                          ALU.mult).then_inc(k.aggT_done, 1)
    dve.memset(k.outT[:, :].rearrange("p (o c) -> p o c", c=NPAD)[:, :, N:NPAD], 0.0)
    bmv = k.bmv[:, :].rearrange("p (c o) -> p o c", c=2)
    for o in range(FT):
        dve.wait_ge(k.outT_done, o + 1)
        for c, (c0, n) in enumerate(CHUNKS):
            dve.bn_stats(k.bst[:, (o * 3 + c) * 6:(o * 3 + c + 1) * 6], k.outT[:, o * NPAD + c0:o * NPAD + c0 + n])
        dve.drain()
        dve.bn_aggr(bmv[:, o, :], k.bst[:, o * 18:(o + 1) * 18])
    dve.drain().then_inc(k.bnvar_ready, 1)
    dve.wait_ge(k.bnsd_ready, 1)
    dve.reciprocal(k.bsd[:, :], k.bsd[:, :])
    dve.wait_ge(k.par_in, 16)
    dve.drain()
    dve.tensor_tensor(k.bsc[:, 0:FT], k.bsd[:, :], k.par[:, FT:2 * FT], ALU.mult)
    dve.drain()
    dve.tensor_tensor(k.bsc[:, FT:2 * FT], k.bsc[:, 0:FT], k.bmv[:, 0:FT], ALU.mult)
    dve.drain()
    dve.tensor_tensor(k.bsc[:, FT:2 * FT], k.par[:, 2 * FT:3 * FT], k.bsc[:, FT:2 * FT], ALU.subtract)
    dve.drain().then_inc(k.bn_ready, 1)

    def first_norm(i, par):
        dve.wait_ge(k.tk_ready, i + 1)
        tile = k.x[:, bass.ds(i * D, D)]
        dve.tensor_tensor(tile, tile, k.TK, ALU.add).then_inc(k.x1_done, 1)
        dve.drain()
        dve.bn_stats(k.tst[:, :], tile)
        dve.drain()
        dve.bn_aggr(k.tmv[:, :], k.tst[:, :]).then_inc(k.var_ready, 1)

    def normed(i, par):
        dve.wait_ge(k.sd_ready, i + 1)
        dve.reciprocal(k.tsd[:, 1:2], k.tsd[:, 0:1])
        dve.drain()
        dve.tensor_scalar(k.y[:, par * D:(par + 1) * D], k.x[:, bass.ds(i * D, D)], k.tmv[:, 0:1], k.tsd[:, 1:2],
                          ALU.subtract, ALU.mult).then_inc(k.y_ready, 1)

    def top_heads(i, h0):
        for h in (h0, h0 + 1):
            dve.wait_ge(k.s_ready, i * H + h + 1)
            dve.sem_inc(k.s_seen, 1)
            for c in range(2):
                dve.max(k.top[:, c * HK + h * 8:c * HK + h * 8 + 8], k.S[h % 2][c][:, 0:NK])
            dve.drain()
            for c in range(2):
                ins = dve.max_index(k.topi[:, c * HK + h * 8:c * HK + h * 8 + 8],
                                    k.top[:, c * HK + h * 8:c * HK + h * 8 + 8], k.S[h % 2][c][:, 0:NK])
            dve.drain().then_inc(k.topk_done, 1)

    def pairs(i, par):
        shape = [P, H, 8, 8]
        t1 = k.top[:, 0:HK].rearrange("p (h a) -> p h a", h=H).unsqueeze(3).to_broadcast(shape)
        t2 = k.top[:, HK:2 * HK].rearrange("p (h b) -> p h b", h=H).unsqueeze(2).to_broadcast(shape)
        dve.tensor_tensor(k.all.rearrange("p (h a b) -> p h a b", h=H, a=8), t1, t2, ALU.add)
        dve.tensor_copy(k.topf[:, :], k.topi[:, :])
        dve.drain()
        for h in range(H):
            dve.max(k.best[:, h * 8:h * 8 + 8], k.all[:, h * 64:(h + 1) * 64])
        dve.drain()
        for h in range(H):
            dve.max_index(k.pos[:, h * 8:h * 8 + 8], k.best[:, h * 8:h * 8 + 8], k.all[:, h * 64:(h + 1) * 64])
        dve.drain()
        dve.tensor_scalar(k.posab[:, 0:HK], k.pos[:, :], 3, None, ALU.logical_shift_right)
        dve.tensor_scalar(k.posab[:, HK:2 * HK], k.pos[:, :], 7, None, ALU.bitwise_and)
        dve.drain()
        dve.tensor_copy(k.posf[:, :], k.posab[:, :])
        dve.drain()
        pick3 = k.pick[:, :].rearrange("p (j a) -> p j a", a=8)
        dve.tensor_tensor(pick3, k.posf[:, :].unsqueeze(2).to_broadcast([P, 2 * HK, 8]),
                          k.iota8[:, :].unsqueeze(1).to_broadcast([P, 2 * HK, 8]), ALU.is_equal)
        dve.drain()
        pick4 = k.pick[:, :].rearrange("p (h j a) -> p h j a", h=2 * H, a=8)
        dve.tensor_tensor(pick4, pick4, k.topf[:, :].rearrange("p (h a) -> p h a", a=8).unsqueeze(2)
                          .to_broadcast([P, 2 * H, 8, 8]), ALU.mult)
        dve.drain()
        dve.tensor_reduce(k.iab[:, :], pick3, AX.X, ALU.add)
        dve.drain()
        dve.scalar_tensor_tensor(k.idx[par][:, :], k.iab[:, 0:HK], float(NK), k.iab[:, HK:2 * HK],
                                 ALU.mult, ALU.add).then_inc(k.idx_ready, 1)
        best = k.best[:, :].rearrange("p (h a) -> p h a", a=8)
        dve.tensor_tensor(k.sm[:, :].rearrange("p (h a) -> p h a", a=8), best,
                          best[:, :, 0:1].to_broadcast([P, H, 8]), ALU.subtract).then_inc(k.exp_in, 1)

    def softmax(i, par):
        dve.wait_ge(k.exp_done, i + 1)
        ex = k.ex[:, :].rearrange("p (h a) -> p h a", a=8)
        dve.tensor_reduce(k.ssum[:, 0:H], ex, AX.X, ALU.add)
        dve.drain()
        dve.reciprocal(k.ssum[:, H:2 * H], k.ssum[:, 0:H])
        dve.drain()
        dve.tensor_tensor(k.prob[:, par * HK:(par + 1) * HK].rearrange("p (h a) -> p h a", a=8), ex,
                          k.ssum[:, H:2 * H].unsqueeze(2).to_broadcast([P, H, 8]), ALU.mult)

    pieces = {2: first_norm, 4: normed, 8: lambda i, p: top_heads(i, 0), 9: lambda i, p: top_heads(i, 2),
              10: lambda i, p: top_heads(i, 4), 11: lambda i, p: top_heads(i, 6), 12: pairs, 15: softmax}

    def search(i, par):
        for g in sorted(pieces):
            pieces[g](i, par)

    def tile(i, par, ahead):
        for g in range(NG):
            if ahead and g in pieces:
                pieces[g](i + 1, 1 - par)
            r = g % RING
            use = i * (NG // RING) + g // RING
            dve.wait_ge(k.landed[r], use * (16 * GS) + 16 * GS)
            for s in range(GS):
                slot = (r * GS + s) * 2 * D
                dve.tensor_tensor_reduce(out=k.big[:, slot:slot + D], in0=k.big[:, slot:slot + D],
                                         in1=k.y[:, par * D:(par + 1) * D], scale=1.0, scalar=0.0,
                                         op0=ALU.mult, op1=ALU.add,
                                         accum_out=k.inner[:, g * GS + s:g * GS + s + 1])
            dve.drain()
            dve.scalar_tensor_tensor(k.val[:, g * GS:(g + 1) * GS], k.inner[:, g * GS:(g + 1) * GS], 0.0,
                                     k.prob[:, par * HK + g * GS:par * HK + (g + 1) * GS],
                                     ALU.max, ALU.mult).then_inc(k.val_ready, 1)
        dve.wait_ge(k.grp_done, i * NG + NG + RING)
        t = k.x[:, bass.ds(i * D, D)]
        dve.tensor_tensor(t, t, k.O[par], ALU.add).then_inc(k.x2_done, 1)

    dve.sem_inc(k.val_ready, RING)
    search(0, 0)
    dve.drain()
    with dve.Fori(0, NT // 2 - 1) as pair:
        tile(pair * 2, 0, True)
        tile(pair * 2 + 1, 1, True)
    tile(NT - 2, 0, True)
    tile(NT - 1, 1, False)

    dve.drain()
    for t in range(NT):
        stats(k.x[:, t * D:(t + 1) * D], t)
    dve.drain()
    for t in range(NT):
        dve.bn_aggr(mv[:, t, :], k.st[:, 6 * t:6 * t + 6])
    dve.drain().then_inc(k.stats1, 1)
    for t in range(NT):
        diag = k.AT[:, t * NPAD + t * P:t * NPAD + (t + 1) * P]
        dve.tensor_tensor(diag, diag, k.ident[:, :], ALU.subtract)
    dve.wait_ge(k.sd1_ready, 1)
    dve.reciprocal(k.rs[:, NT:2 * NT], k.rs[:, 0:NT])
    dve.drain()
    dve.tensor_tensor(k.comb[:, :], k.rs[:, NT:2 * NT], k.dri[:, 2 * NT:3 * NT], ALU.mult)
    dve.drain()
    for t in range(NT):
        dve.tensor_scalar(k.h1[:, t * D:(t + 1) * D], k.x[:, t * D:(t + 1) * D], k.mv[:, t:t + 1],
                          k.comb[:, t:t + 1], ALU.subtract, ALU.mult).then_inc(k.h1_ready, 1)
    dve.memset(k.agg1.rearrange("p (o c) -> p o c", c=NPAD)[:, :, N:NPAD], 0.0).then_inc(k.h1_ready, 1)
    dve.wait_ge(k.b1_in, 16)
    for t in range(NT):
        tile_ = k.x[:, t * D:(t + 1) * D]
        dve.tensor_tensor(tile_, tile_, k.b1[:, :], ALU.add)
    dve.drain()

    def normed_row(t):
        dve.wait_ge(k.sd4_ready, t + 1)
        dve.reciprocal(k.rs[:, NT + t:NT + t + 1], k.rs[:, t:t + 1])
        dve.drain()
        dve.tensor_scalar(k.zx[t][:, 0:D], k.zx[t][:, D:2 * D], k.mv[:, t:t + 1], k.rs[:, NT + t:NT + t + 1],
                          ALU.subtract, ALU.mult)

    for t in range(NT):
        dve.wait_ge(k.g1_ready, t + 1)
        dve.scalar_tensor_tensor(k.zx[t][:, D:2 * D], k.tr[t % 2][:, :], k.dri[:, NT + t:NT + t + 1],
                                 k.x[:, t * D:(t + 1) * D], ALU.mult, ALU.add).then_inc(k.x3_done, 1)
        dve.drain()
        stats(k.zx[t][:, D:2 * D], t)
        if t:
            normed_row(t - 1)
        else:
            dve.wait_ge(k.e_consts, 1)
            dve.tensor_tensor(k.lt8.rearrange("p (a b) -> p a b", a=BINS),
                              k.iota8[:, :].unsqueeze(1).to_broadcast([P, BINS, BINS]),
                              k.iota8[:, :].unsqueeze(2).to_broadcast([P, BINS, BINS]), ALU.is_lt)
        dve.drain()
        dve.bn_aggr(mv[:, t, :], k.st[:, 6 * t:6 * t + 6]).then_inc(k.var4_ready, 1)
    normed_row(NT - 1)
    dve.drain()
    gtb = k.gtb.rearrange("p (t b) -> p t b", t=NT)
    dve.tensor_tensor(gtb, k.bins[:, :].unsqueeze(1).to_broadcast([P, NT, BINS - 1]),
                      k.zxv[:, :, 0:1].to_broadcast([P, NT, BINS - 1]), ALU.is_lt)
    dve.drain()
    dve.tensor_reduce(k.mem, gtb, AX.X, ALU.add)
    dve.drain()
    sel = k.sel.rearrange("p (t b) -> p t b", t=NT)
    dve.tensor_tensor(sel, k.iota8[:, :].unsqueeze(1).to_broadcast([P, NT, BINS]),
                      k.mem.unsqueeze(2).to_broadcast([P, NT, BINS]), ALU.is_equal).then_inc(k.sel_ready, 1)
    dve.memset(k.cnt[:, 0:BINS], 0.0)
    dve.drain()
    dve.wait_ge(k.rank_psum, 1)
    for t in range(NT):
        dve.tensor_tensor(k.cnt[:, (t + 1) * BINS:(t + 2) * BINS], k.cnt[:, t * BINS:(t + 1) * BINS],
                          k.RK[1][:, t * BINS:(t + 1) * BINS], ALU.add)
        dve.drain()
    dve.tensor_tensor(k.rank, k.RK[0][:, 0:NT * BINS], k.cnt[:, 0:NT * BINS], ALU.add)
    cmp_ = k.cmp.rearrange("p (b m) -> p b m", b=BINS)
    dve.tensor_tensor(cmp_, k.cnt[:, NT * BINS:].unsqueeze(2).to_broadcast([P, BINS, NT]),
                      k.thr[:, :].unsqueeze(1).to_broadcast([P, BINS, NT]), ALU.is_gt)
    dve.drain()
    dve.tensor_reduce(k.tiles, cmp_, AX.X, ALU.add)
    dve.drain()
    lt8 = k.lt8.rearrange("p (a b) -> p a b", a=BINS)
    dve.tensor_tensor(lt8, lt8, k.tiles.unsqueeze(1).to_broadcast([P, BINS, BINS]), ALU.mult)
    dve.drain()
    dve.tensor_reduce(k.base, lt8, AX.X, ALU.add)
    dve.drain()
    dve.scalar_tensor_tensor(k.rank.rearrange("p (t b) -> p t b", t=NT),
                             k.base.unsqueeze(1).to_broadcast([P, NT, BINS]), float(P),
                             k.rank.rearrange("p (t b) -> p t b", t=NT), ALU.mult, ALU.add)
    cmps = k.cmps.rearrange("p (m b) -> p m b", m=SLOTS)
    dve.tensor_tensor(cmps, k.base.unsqueeze(1).to_broadcast([P, SLOTS, BINS]),
                      k.iotas.unsqueeze(2).to_broadcast([P, SLOTS, BINS]), ALU.is_le)
    dve.drain()
    dve.tensor_tensor(k.rank, k.rank, k.sel, ALU.mult)
    dve.tensor_reduce(k.binf, cmps, AX.X, ALU.add)
    dve.drain()
    dve.tensor_reduce(k.posn, k.rank.rearrange("p (t b) -> p t b", t=NT), AX.X, ALU.add)
    dve.tensor_scalar(k.bini, k.binf, -1.0, None, ALU.add)
    dve.drain()
    dve.wait_ge(k.ids_ready, 1)
    dve.tensor_copy(k.posi, k.posn)
    dve.drain().then_inc(k.pos_ready, 1)

    def finish(m, r):
        dve.wait_ge(k.e_ready, m + 1)
        dve.tensor_scalar(k.oid[r], k.xb[r][:, 2 * D:ROW], -1.0, ID0, ALU.mult, ALU.add)
        dve.tensor_tensor(k.xb[r][:, D:2 * D], k.xb[r][:, D:2 * D], k.tr[r % 2][:, :], ALU.add)
        dve.drain().then_inc(k.x4_done, 1)

    dve.sem_inc(k.x4_done, 2)
    with dve.Fori(0, SLOTS // XR) as q:
        for r in range(XR):
            finish(q * XR + r, r)
    for m in range(SLOTS // XR * XR, SLOTS):
        finish(m, m % XR)


def pe_program(pe, k):
    ident = k.ident[:, :]
    pe.wait_ge(k.consts, 1)
    pe.wait_ge(k.edge_f, 1)
    for c in range(2):
        for b in range(BPS):
            ins = pe.transpose(k.tr[c][:, b * NS:(b + 1) * NS], k.ef[:, c * SPAN + b * P:c * SPAN + (b + 1) * P],
                               k.ident[0:NS, 0:NS])
    ins.then_inc(k.edgeT_ready, 1)
    pe.wait_ge(k.ov_done, 1)
    for c in range(2):
        ins = pe.transpose(k.acc[0][0:NT, c * NS:(c + 1) * NS], k.ov[:, (2 + c) * NT:(3 + c) * NT],
                           k.ident[0:NS, 0:NS])
    ins.then_inc(k.lowT_ready, 1)
    pe.wait_ge(k.bounds_ready, 1)
    pe.wait_ge(k.edgeT_done, 1)
    pe.matmul(k.tr[0][0:1, 0:NT], k.lh[:, 0:1], k.ident[0:NT, 0:NT], start=True, stop=True)
    pe.matmul(k.tr[0][0:1, NT:3 * NT], k.lh[:, 2:3], k.lt[:, :], start=True, stop=True).then_inc(k.row_ready, 1)
    pe.wait_ge(k.bounds_ready, 2)
    pe.sem_inc(k.oh_used, BPS)

    def counts(t, s):
        first = pe.value_load(k.bnd[0:1, bass.ds(t, 1)], min_val=0, max_val=NS * NT)
        end = pe.value_load(k.bnd[0:1, bass.ds(t + NT, 1)], min_val=1, max_val=NS * NT + 1)
        for c0, n in CHUNKS:
            pe.matmul(k.acc[s][:, c0:c0 + n], k.zero[:, 0:P], k.zero[:, 0:n], start=True, stop=False)
        with pe.Fori(first, end) as n_step:
            for b in range(BPS):
                pe.wait_ge(k.oh_ready, n_step * (2 * BPS) + 2 * b + 2)
                for c0, n in CHUNKS:
                    ins = pe.matmul(k.acc[s][:, c0:c0 + n], k.ohd[b], k.ohs[b][:, c0:c0 + n], start=False, stop=False)
                ins.then_inc(k.oh_used, 1)
        for c0, n in CHUNKS:
            ins = pe.matmul(k.acc[s][:, c0:c0 + n], k.zero[:, 0:P], k.zero[:, 0:n], start=False, stop=True)
        ins.then_inc(k.acc_ready, 1)

    def flip(t, s):
        pe.wait_ge(k.stage_ready, t + 1)
        for b, j0 in enumerate((0, 4, 8)):
            pe.wait_ge(k.at_done, t * 3 + b - 1 if not isinstance(t, int) else max(t * 3 + b - 1, 0))
            for j in range(j0, min(j0 + 4, NT)):
                ins = pe.transpose(k.tr[(s + b) % 2][:, (j - j0) * P:(j - j0 + 1) * P],
                                   k.stage[:, s * NPAD + j * P:s * NPAD + (j + 1) * P], ident)
            ins.then_inc(k.trp_ready, 1)

    counts(0, 0)
    counts(1, 1)
    flip(0, 0)
    with pe.Fori(1, NT // 2) as h:
        pe.wait_ge(k.stage_ready, 2 * h - 1)
        counts(2 * h, 0)
        flip(2 * h - 1, 1)
        counts(2 * h + 1, 1)
        flip(2 * h, 0)
    flip(NT - 1, 1)

    def aggregate(h, f, s, ready, at=None):
        for t in range(NT):
            if f == 0:
                pe.wait_ge(ready, t + 1)
            for c0, n in CHUNKS:
                ins = pe.matmul(k.acc[s][:, c0:c0 + n], h[:, t * D + f * P:t * D + (f + 1) * P],
                                k.AT[:, t * NPAD + c0:t * NPAD + c0 + n], start=(t == 0), stop=(t == NT - 1))
        return ins

    aggregate(k.h0, 0, 0, k.h0_ready).then_inc(k.agg_ready, 1)
    pe.wait_ge(k.dg_ready, 1)
    for t in range(8):
        ins = pe.matmul(k.tr[t // 4][:, (t % 4) * P:(t % 4 + 1) * P], k.ones, k.dg[:, t * P:(t + 1) * P],
                        start=True, stop=True)
    ins.then_inc(k.dinvB_psum, 1)
    pe.wait_ge(k.dinvB_ready, 1)
    for t in range(8, NT):
        ins = pe.matmul(k.tr[0][:, (t - 8) * P:(t - 7) * P], k.ones, k.dg[:, t * P:(t + 1) * P],
                        start=True, stop=True)
    ins.then_inc(k.dinvB_psum, 1)
    for f in range(1, FT):
        if f >= 2:
            pe.wait_ge(k.aggT_done, f - 1)
        aggregate(k.h0, f, f % 2, k.h0_ready).then_inc(k.agg_ready, 1)
    pe.wait_ge(k.w_in, 16)
    for o in range(FT):
        pe.wait_ge(k.aggT_done, FT - 1 if o == 0 else FT)
        if o >= 2:
            pe.wait_ge(k.outT_done, o - 1)
        for f in range(FT):
            if f == FT - 1:
                pe.wait_ge(k.aggT_done, FT)
            for c0, n in CHUNKS:
                ins = pe.matmul(k.acc[o % 2][:, c0:c0 + n], k.w0[:, f * D + o * P:f * D + (o + 1) * P],
                                k.aggT[:, f * NPAD + c0:f * NPAD + c0 + n], start=(f == 0), stop=(f == FT - 1))
        ins.then_inc(k.out_ready, 1)

    def flip_gelu(i):
        pe.wait_ge(k.gelu_done, i + 1)
        pe.wait_ge(k.yT_done, i)
        for o in range(FT):
            ins = pe.transpose(k.TK[:, o * P:(o + 1) * P], k.gt[:, o * P:(o + 1) * P], ident)
        ins.then_inc(k.tk_ready, 1)

    def flip_y(i, par):
        pe.wait_ge(k.y_ready, i + 1)
        for f in range(FT):
            c = par * D + f * P
            ins = pe.transpose(k.YT[:, f * P:(f + 1) * P], k.y[:, c:c + P], ident)
        ins.then_inc(k.yt_ready, 1)

    def queries(i, half):
        pe.wait_ge(k.yT_done, i + 1)
        pe.wait_ge(k.qT_done, i * H + 4 * half)
        for b in range(4):
            h = 4 * half + b
            for f in range(FT):
                ins = pe.matmul(k.Q[:, b * P:(b + 1) * P], k.wq[:, f * H * P + h * P:f * H * P + (h + 1) * P],
                                k.yT[:, f * P:(f + 1) * P], start=(f == 0), stop=(f == FT - 1))
        ins.then_inc(k.q_ready, 1)

    def scores(i, h0):
        for h in (h0, h0 + 1):
            pe.wait_ge(k.qT_done, i * H + h + 1)
            if h >= 2:
                pe.wait_ge(k.topk_done, i * H + h - 1)
            else:
                pe.wait_ge(k.topk_done, i * H)
            for c in range(2):
                half = slice(64 * c, 64 * c + 64)
                ins = pe.matmul(k.S[h % 2][c][:, 0:NK], k.qT[half, h * P:(h + 1) * P],
                                k.keys[half, h * NK:(h + 1) * NK], start=True, stop=True)
            ins.then_inc(k.s_ready, 1)

    pieces = {1: lambda i, p: flip_gelu(i), 4: flip_y, 5: lambda i, p: queries(i, 0), 6: lambda i, p: queries(i, 1),
              7: lambda i, p: scores(i, 0), 8: lambda i, p: scores(i, 2), 9: lambda i, p: scores(i, 4),
              10: lambda i, p: scores(i, 6)}

    def search(i, par):
        for g in sorted(pieces):
            pieces[g](i, par)

    def tile(i, par, ahead):
        for g in range(NG):
            if ahead and g in pieces:
                pieces[g](i + 1, 1 - par)
            pe.wait_ge(k.diag_ready, i * NG + g + 1)
            for s in range(GS):
                slot = ((g % RING) * GS + s) * 2 * D + D
                c = ((g % 2) * GS + s) * P
                ins = pe.matmul(k.O[par], k.diag[:, c:c + P], k.big[:, slot:slot + D],
                                start=(g == 0 and s == 0), stop=(g == NG - 1 and s == GS - 1))
            ins.then_inc(k.grp_done, 1)

    pe.wait_ge(k.wq_in, 16)
    pe.wait_ge(k.keys_in, 16)
    pe.sem_inc(k.grp_done, RING)
    search(0, 0)
    with pe.Fori(0, NT // 2 - 1) as pair:
        tile(pair * 2, 0, True)
        tile(pair * 2 + 1, 1, True)
    tile(NT - 2, 0, True)
    tile(NT - 1, 1, False)

    for f in range(FT):
        if f >= 2:
            pe.wait_ge(k.agg1_done, f - 1)
        aggregate(k.h1, f, f % 2, k.h1_ready).then_inc(k.agg1_ready, 1)
    pe.wait_ge(k.h1_ready, NT + 1)
    pe.wait_ge(k.agg1_done, FT)
    pe.wait_ge(k.x2_done, NT)
    pe.wait_ge(k.w1_in, 16 * FT)
    for t in range(NT):
        if t >= 2:
            pe.wait_ge(k.x3_done, t - 1)
        for f in range(FT):
            ins = pe.matmul(k.tr[t % 2][:, :], k.agg1[:, f * NPAD + t * P:f * NPAD + (t + 1) * P],
                            k.w1[f], start=(f == 0), stop=(f == FT - 1))
        ins.then_inc(k.g1_ready, 1)
    pe.wait_ge(k.sel_ready, 1)
    pe.wait_ge(k.e_consts, 1)
    pe.matmul(k.RK[0][:, 0:NT * BINS], k.upper, k.sel, start=True, stop=True)
    pe.matmul(k.RK[1][:, 0:NT * BINS], k.ones1, k.sel, start=True, stop=True).then_inc(k.rank_psum, 1)
    pe.wait_ge(k.pos_ready, 1)
    pe.wait_ge(k.we_in, 16 * BINS)

    def flip_z(m, r, use):
        pe.wait_ge(k.loaded[r], use * 16 + 16)
        for f in range(FT):
            ins = pe.transpose(k.ZB[r % 2][:, f * P:(f + 1) * P], k.xb[r][:, f * P:(f + 1) * P], ident)
        ins.then_inc(k.zt_ready, 1)

    def expert(m, r):
        pe.wait_ge(k.zT_done, m + 1)
        pe.wait_ge(k.x4_done, m + 1)
        b = pe.value_load(k.bini[0:1, bass.ds(m, 1)], min_val=0, max_val=BINS - 1)
        for f in range(FT):
            ins = pe.matmul(k.tr[r % 2][:, :], k.zT[r % 2][:, f * P:(f + 1) * P],
                            k.big[:, bass.ds(b * (FT * D) + f * D, D)], start=(f == 0), stop=(f == FT - 1))
        ins.then_inc(k.e_ready, 1)

    flip_z(0, 0, 0)
    with pe.Fori(0, SLOTS // XR) as q:
        for r in range(XR):
            nxt = (r + 1) % XR
            flip_z(q * XR + r + 1, nxt, q + (r + 1) // XR)
            expert(q * XR + r, r)
    for m in range(SLOTS // XR * XR, SLOTS):
        if m + 1 < SLOTS:
            flip_z(m + 1, (m + 1) % XR, (m + 1) // XR)
        expert(m, m % XR)


def kernel(**inputs):
    import concourse.bacc as _bacc
    from concourse.bass_utils import run_bass_kernel_spmd as _run

    a = {n: np.asarray(v) for n, v in inputs.items()}

    def cols(v):
        return v.reshape(-1, P).T

    arrays = {
        "in_x": a["x"], "in_src": a["src"], "in_dst": a["dst"],
        "in_w0t": a["L0_gnn_W"].T,
        "in_par": np.concatenate([cols(a["L0_gnn_b"]), cols(a["L0_gnn_gamma"]), cols(a["L0_gnn_beta"]),
                                  cols(a["L0_gnn_beta"]), cols(a["L0_ffn_bq"])], axis=1),
        "in_wq": a["L0_ffn_Wq"],
        "in_keys": a["L0_ffn_keys"].transpose(1, 3, 0, 2).reshape(P, H * NK),
        "in_wdu": np.concatenate([a["L0_ffn_w_down"], a["L0_ffn_w_up"]], axis=1),
        "in_w1": a["L1_gnn_W"], "in_b1": a["L1_gnn_b"], "in_we": a["L1_ffn_W"],
    }
    arrays = {n: np.ascontiguousarray(v) for n, v in arrays.items()}
    nc = _bacc.Bacc("TRN2", target_bir_lowering=False, num_devices=1)
    args = [nc.dram_tensor(n, v.shape, mybir.dt.from_np(v.dtype), kind="ExternalInput").ap()
            for n, v in arrays.items()]
    args.append(nc.dram_tensor("out", (N, D), F32, kind="ExternalOutput").ap())
    program(nc, *args)
    r = _run(nc, [arrays], core_ids=[0])
    return r.results[0]["out"]
```

```python
from contextlib import ExitStack

import numpy as np
import concourse.bass as bass
from concourse import mybir

F32 = mybir.dt.float32
F16 = mybir.dt.float16
I32 = mybir.dt.int32
U32 = mybir.dt.uint32
ALU = mybir.AluOpType
ACT = mybir.ActivationFunctionType
AX = mybir.AxisListType

P = 128
N = 1250
D = 512
E = 21250
NT = -(-N // P)
NPAD = NT * P
LAST = N - (NT - 1) * P
FT = D // P
H = 8
NK = 256
HK = H * 8
EPS = 1e-5
BPS = 4
SPAN = BPS * P
NS = -(-E // SPAN)
TAIL = E - (NS - 1) * SPAN
NO_NODE = 4096
FAR = 1000.0
CHUNKS = [(0, 512), (512, 512), (1024, N - 1024)]
GS = 4
NG = HK // GS
RING = 4
BINS = 8
ROW = 2 * D + 1
ID0 = 2000.0
XR = 4
MOST = (NPAD + BINS * (P - 1)) // P
ROUNDS = -(-(MOST - XR // 2) // XR) + 1
FEWEST = -(-(NT - XR // 2) // XR) + 1
SLOTS = ROUNDS * XR


UNITS = [(f, c0, n) for f in range(FT) for c0, n in CHUNKS]
UPP = 2
FIRST_UNIT = NG * UPP - len(UNITS)


class Net:
    pass


def lay_out(nc, ctx, k):
    def sb(name, cols, dt=F32, rows=P):
        return ctx.enter_context(nc.sbuf_tensor(name, [rows, cols], dt))

    k.AT = sb("AT", NT * NPAD)
    k.x = sb("x", NT * D)
    k.big = sb("big", 16 * 1024)
    k.qk = sb("qk", 4096 + 2048)
    k.outT = sb("outT", FT * NPAD)
    k.y = sb("y", 2 * D)
    k.yT = sb("yT", D)
    k.qT = sb("qT", H * P)
    k.gt = sb("gt", D)
    k.diag = sb("diag", 2 * GS * P)
    k.b1 = k.qk[:, 0:D]
    k.h0 = k.big[:, 0:5120]
    k.ei = k.big[0:NS, 0:2 * SPAN].bitcast(I32)
    k.ef = k.big[0:NS, 2 * SPAN:4 * SPAN]
    k.aggT = k.big[:, 5120:10240]
    k.stage = k.big[:, 10240:12800]
    k.w0 = k.big[:, 12800:14848]
    k.dinvB = k.big[:, 14848:16128]
    k.zero = k.big[:, 2048:2304].bitcast(F16)
    k.tab = k.big[:, 3584:3584 + (BPS + 1) * NS]
    k.tabv = k.tab.rearrange("p (q c) -> p q c", c=BPS + 1)
    k.dstp = k.big[:, 4096:4096 + BPS * NS]
    k.now = k.big[:, 4096 + BPS * NS:4096 + BPS * NS + BPS + 1]
    k.dnow = k.big[:, 4096 + BPS * NS + 8:4096 + BPS * NS + 8 + BPS - 1]
    k.tile_iota = k.gt[:, 0:P // 2].bitcast(F16)
    k.iota = k.big[:, 4440:4440 + NPAD // 2].bitcast(F16)
    k.ones = k.big[:, 16128:16256]
    k.iotai = k.big[:, 5120:5120 + NPAD].bitcast(I32)
    oh = k.outT[:, 0:BPS * (NPAD + P) // 2].bitcast(F16)
    k.ohs = [oh[:, b * NPAD:(b + 1) * NPAD] for b in range(BPS)]
    k.ohd = [oh[:, BPS * NPAD + b * P:BPS * NPAD + (b + 1) * P] for b in range(BPS)]
    k.dg = k.outT[:, 0:NT * P]
    k.wq = k.qk[:, 0:4096]
    k.keys = k.qk[:, 4096:6144]
    k.h1 = k.gt
    k.agg1 = k.outT
    k.gtt = [k.gt, k.diag]
    k.w1 = [k.qT[:, 0:D], k.qT[:, D:2 * D], k.diag[:, 0:D], k.diag[:, D:2 * D]]
    k.zx = [k.AT[:, t * ROW:(t + 1) * ROW] for t in range(NT)]
    k.zxv = k.AT[:, 0:NT * ROW].rearrange("p (t c) -> p t c", c=ROW)
    k.upper = k.y[:, 0:P]
    k.ones1 = k.y[:, P:2 * P]
    k.xb = [k.x[:, r * NPAD:r * NPAD + ROW] for r in range(XR)]
    k.zT = [k.yT, k.gt]
    k.ident = sb("ident", P)
    k.eps = sb("eps", 1)
    k.thr = sb("thr", NT)
    k.thri = sb("thri", NT, I32)
    k.qcol = sb("qcol", 2, rows=NS)
    k.qcoli = sb("qcoli", 1, I32, rows=NS)
    k.lt = sb("lt", 2 * NT, rows=NT)
    k.iota8 = sb("iota8", 8)
    k.iota8h = sb("iota8h", 8, F16)
    k.iota8i = sb("iota8i", 8, I32)
    k.bins = sb("bins", BINS - 1)
    k.par = sb("par", 4 * FT + H)
    k.mm = sb("mm", 2, rows=NS)
    k.ov = k.big[0:NS, 2304:2304 + 4 * NT]
    k.lh = sb("lh", 4, rows=NT)
    k.row = sb("row", 3 * NT, rows=1)
    k.bnd = sb("bnd", 3 * NT, I32, rows=1)
    k.st = sb("st", 6 * NT)
    k.mv = sb("mv", 2 * NT)
    k.rs = sb("rs", 2 * NT)
    k.pq = sb("pq", 2 * NT)
    k.degin = sb("degin", NT)
    k.deg = sb("deg", 3 * NT)
    k.dsq = sb("dsq", 3 * NT)
    k.dri = sb("dri", 3 * NT)
    k.comb = sb("comb", NT)
    k.bst = sb("bst", FT * 3 * 6)
    k.bmv = sb("bmv", 2 * FT)
    k.bsd = sb("bsd", FT)
    k.bsc = sb("bsc", 2 * FT)
    k.tst = sb("tst", 12)
    k.tmv = sb("tmv", 4)
    k.tsd = sb("tsd", 4)
    k.hco = sb("hco", 1)
    k.top = sb("top", 2 * HK)
    k.topi = sb("topi", 2 * HK, U32)
    k.topf = sb("topf", 2 * HK, F16)
    k.best = sb("best", HK)
    k.pos = sb("pos", HK, U32)
    k.posab = sb("posab", 2 * HK, U32)
    k.posf = sb("posf", 2 * HK, F16)
    k.iab = sb("iab", 2 * HK)
    k.pick = sb("pick", 2 * H * 64)
    k.all = k.pick[:, 0:H * 64]
    k.pickh = k.pick[:, 0:H * 64].bitcast(F16)
    k.idx = [sb(f"idx{b}", HK, I32) for b in range(2)]
    k.sm = sb("sm", HK)
    k.ex = k.sm
    k.ssum = sb("ssum", 2 * H)
    k.prob = sb("prob", 2 * HK)
    k.inner = sb("inner", HK)
    k.val = sb("val", HK)
    def piece(at, n):
        return k.pick[:, at:at + n]
    k.gtb = piece(0, NT * (BINS - 1))
    k.mem = piece(80, NT)
    k.sel = piece(96, NT * BINS)
    k.rank = piece(176, NT * BINS)
    k.cnt = piece(256, (NT + 1) * BINS)
    k.cmp = piece(344, BINS * NT)
    k.tiles = piece(424, BINS)
    k.base = piece(432, BINS)
    k.lt8 = piece(440, BINS * BINS)
    k.posn = piece(504, NT)
    k.binf = piece(520, SLOTS)
    k.cmps = piece(544, SLOTS * BINS)
    k.iotas = piece(704, SLOTS)
    k.iotasi = piece(724, SLOTS).bitcast(I32)
    k.bini = piece(744, SLOTS).bitcast(I32)
    k.posi = piece(764, NT).bitcast(I32)
    k.ids = piece(774, NT).bitcast(I32)
    k.oid = [piece(784 + r, 1).bitcast(I32) for r in range(XR)]
    k.used = piece(790, 1)
    k.less = piece(791, 1)
    k.begun = piece(792, ROUNDS)
    k.fullf = piece(802, 1)
    k.rounds = piece(804, 2).bitcast(I32)
    k.last_full = piece(806, 1).bitcast(I32)

    def ps(name, cols, dt=F32):
        return ctx.enter_context(nc.psum_tensor(name, [P, cols], dt))

    k.acc = [ps(f"acc{s}", 3 * 512) for s in range(2)]
    k.tr = [ps(f"tr{s}", 512) for s in range(2)]
    banks = [k.acc[s][:, b * 512:(b + 1) * 512] for s in range(2) for b in range(3)]
    k.TK = [k.tr[0][:, :], k.tr[1][:, :]]
    k.YT = banks[0]
    k.G = [banks[0], banks[1]]
    k.ZB = banks[0:2]
    k.RK = banks[4:6]
    k.Q = banks[1]
    k.S = [banks[2:4], banks[4:6]]
    k.O = [k.tr[0][:, :], k.tr[1][:, :]]




def program(nc, x_d, src_d, dst_d, w0t_d, par_d, wq_d, keys_d, wdu_d, w1_d, b1_d, we_d, out_d):
    k = Net()
    with ExitStack() as ctx:
        k.nc = nc
        lay_out(nc, ctx, k)

        def sem(name):
            return ctx.enter_context(nc.semaphore(name))

        k.ring_free = sem("ring_free")
        k.s_seen = sem("s_seen")
        k.consts = sem("consts")
        k.stage_zero = sem("stage_zero")
        k.edges_pre = sem("edges_pre")
        k.xpad = sem("xpad")
        k.edges_in = sem("edges_in")
        k.x_in = sem("x_in")
        k.w_in = sem("w_in")
        k.par_in = sem("par_in")
        k.wq_in = sem("wq_in")
        k.keys_in = sem("keys_in")
        k.b1_in = sem("b1_in")
        k.finished = sem("finished")
        k.rounds_ready = sem("rounds_ready")
        k.xb_ready = sem("xb_ready")
        k.edge_f = sem("edge_f")
        k.ov_done = sem("ov_done")
        k.stats0 = sem("stats0")
        k.sd0_ready = sem("sd0_ready")
        k.edgeT_ready = sem("edgeT_ready")
        k.edgeT_done = sem("edgeT_done")
        k.lowT_ready = sem("lowT_ready")
        k.lh_ready = sem("lh_ready")
        k.row_ready = sem("row_ready")
        k.bounds_ready = sem("bounds_ready")
        k.oh_ready = sem("oh_ready")
        k.oh_used = sem("oh_used")
        k.ohd_ready = sem("ohd_ready")
        k.ohd_free = sem("ohd_free")
        k.acc_ready = sem("acc_ready")
        k.stage_ready = sem("stage_ready")
        k.trp_ready = sem("trp_ready")
        k.at_done = sem("at_done")
        k.degs_ready = sem("degs_ready")
        k.degsq_ready = sem("degsq_ready")
        k.dego_ready = sem("dego_ready")
        k.degosq_ready = sem("degosq_ready")
        k.h0_ready = sem("h0_ready")
        k.dg_ready = sem("dg_ready")
        k.dinvB_psum = sem("dinvB_psum")
        k.dinvB_ready = sem("dinvB_ready")
        k.agg_ready = sem("agg_ready")
        k.aggT_done = sem("aggT_done")
        k.out_ready = sem("out_ready")
        k.outT_done = sem("outT_done")
        k.bnvar_ready = sem("bnvar_ready")
        k.bnsd_ready = sem("bnsd_ready")
        k.bn_ready = sem("bn_ready")
        k.gelu_done = sem("gelu_done")
        k.ht_ready = sem("ht_ready")
        k.g_ready = sem("g_ready")
        k.g_used = sem("g_used")
        k.tk_ready = sem("tk_ready")
        k.x1_done = sem("x1_done")
        k.var_ready = sem("var_ready")
        k.sd_ready = sem("sd_ready")
        k.y_ready = sem("y_ready")
        k.yt_ready = sem("yt_ready")
        k.yT_done = sem("yT_done")
        k.q_ready = sem("q_ready")
        k.qT_done = sem("qT_done")
        k.s_ready = sem("s_ready")
        k.topk_done = sem("topk_done")
        k.idx_ready = sem("idx_ready")
        k.exp_in = sem("exp_in")
        k.exp_done = sem("exp_done")
        k.prob_ready = sem("prob_ready")
        k.val_ready = sem("val_ready")
        k.diag_ready = sem("diag_ready")
        k.grp_done = sem("grp_done")
        k.x2_done = sem("x2_done")
        k.g1_ready = sem("g1_ready")
        k.x3_done = sem("x3_done")
        k.var4_ready = sem("var4_ready")
        k.sd4_ready = sem("sd4_ready")
        k.z_ready = sem("z_ready")
        k.zt_ready = sem("zt_ready")
        k.zT_done = sem("zT_done")
        k.e_ready = sem("e_ready")
        k.w1_in = sem("w1_in")
        k.we_in = sem("we_in")
        k.cleared = sem("cleared")
        k.e_consts = sem("e_consts")
        k.ids_ready = sem("ids_ready")
        k.sel_ready = sem("sel_ready")
        k.rank_psum = sem("rank_psum")
        k.pos_ready = sem("pos_ready")
        k.sorted = sem("sorted")
        k.x4_done = sem("x4_done")
        k.x4_seen = sem("x4_seen")
        k.loaded = [sem(f"loaded{r}") for r in range(XR)]
        k.stored = [sem(f"stored{r}") for r in range(XR)]
        k.landed = [ctx.enter_context(nc.semaphore(f"landed{r}")) for r in range(RING)]
        k.x_d, k.src_d, k.dst_d, k.w0t_d, k.par_d, k.wq_d = x_d, src_d, dst_d, w0t_d, par_d, wq_d
        k.zs_d = nc.dram_tensor("sorted_rows", (SLOTS * P, ROW), F32).ap()
        k.keys_d, k.wdu_d, k.w1_d, k.b1_d, k.we_d, k.out_d = keys_d, wdu_d, w1_d, b1_d, we_d, out_d
        block = ctx.enter_context(nc.Block())

        @block.sync
        def _(sp):
            sync_program(sp, k)

        @block.gpsimd
        def _(pool):
            pool_program(pool, k)

        @block.scalar
        def _(act):
            act_program(act, k)

        @block.vector
        def _(dve):
            dve_program(dve, k)

        @block.tensor
        def _(pe):
            pe_program(pe, k)


def sync_program(sp, k):
    sp.wait_ge(k.edges_pre, 1)
    full = (NS - 1) * SPAN
    for c, d in enumerate((k.dst_d, k.src_d)):
        cols = slice(c * SPAN, (c + 1) * SPAN)
        sp.dma_start(k.ei[0:NS - 1, cols], d[0:full].rearrange("(q n) -> q n", n=SPAN)).then_inc(k.edges_in, 16)
        sp.dma_start(k.ei[NS - 1:NS, c * SPAN:c * SPAN + TAIL],
                     d[full:E].rearrange("(q n) -> q n", q=1)).then_inc(k.edges_in, 16)
    sp.wait_ge(k.xpad, 1)
    sp.dma_start(k.x[:, 0:(NT - 1) * D].rearrange("p (t d) -> p t d", d=D),
                 k.x_d[0:(NT - 1) * P, :].rearrange("(t p) d -> p t d", p=P)).then_inc(k.x_in, 16)
    sp.dma_start(k.x[0:LAST, (NT - 1) * D:NT * D], k.x_d[(NT - 1) * P:N, :]).then_inc(k.x_in, 16)
    sp.wait_ge(k.stage_zero, 1)
    zeros = k.zs_d.rearrange("(p t) c -> p (t c)", p=P)
    for c0 in range(0, SLOTS * ROW, 2 * NPAD):
        n = min(2 * NPAD, SLOTS * ROW - c0)
        sp.dma_start(zeros[:, c0:c0 + n], k.stage[:, 0:n]).then_inc(k.cleared, 16)
    sp.dma_start(k.w0.rearrange("p (f n) -> p f n", n=D),
                 k.w0t_d.rearrange("(f p) n -> p f n", p=P)).then_inc(k.w_in, 16)
    sp.dma_start(k.par[:, :], k.par_d).then_inc(k.par_in, 16)
    sp.dma_start(k.wq.rearrange("p (f n) -> p f n", n=H * P),
                 k.wq_d.rearrange("(f p) n -> p f n", p=P)).then_inc(k.wq_in, 16)
    sp.dma_start(k.keys, k.keys_d).then_inc(k.keys_in, 16)
    sp.wait_ge(k.grp_done, NT * NG + RING)
    sp.wait_ge(k.x2_done, NT)
    sp.dma_start(k.b1, k.b1_d.partition_broadcast(P)).then_inc(k.b1_in, 16)
    for f in range(FT):
        sp.dma_start(k.w1[f], k.w1_d[f * P:(f + 1) * P, :]).then_inc(k.w1_in, 16)
    for b in range(BINS):
        sp.dma_start(k.big[:, b * 2048:(b + 1) * 2048].rearrange("p (f n) -> p f n", n=D),
                     k.we_d[b].rearrange("(f p) n -> p f n", p=P)).then_inc(k.we_in, 16)
    sp.wait_ge(k.sorted, 16 * NT)
    for r in range(XR):
        sp.dma_start(k.xb[r], k.zs_d[r * P:(r + 1) * P, :]).then_inc(k.loaded[r], 16)
    sp.wait_ge(k.rounds_ready, 1)
    rounds = sp.value_load(k.rounds[0:1, 0:1], min_val=FEWEST, max_val=ROUNDS)
    full = sp.value_load(k.rounds[0:1, 1:2], min_val=FEWEST - 1, max_val=ROUNDS - 1)
    landed = sp.snap(rounds * 16), sp.snap(full * 16)

    def load(q, tiles):
        for r in range(tiles):
            sp.wait_ge(k.stored[r], q * 16)
            sp.dma_start(k.xb[r], k.zs_d[bass.ds(q * (XR * P) + r * P, P), :]).then_inc(k.loaded[r], 16)

    with sp.Fori(1, full) as q:
        load(q, XR)
    with sp.Fori(full, rounds) as q:
        load(q, XR // 2)
    for r in range(XR):
        sp.wait_ge(k.stored[r], landed[0 if r < XR // 2 else 1])
        sp.sem_inc(k.finished, 1)


def pool_program(pool, k):
    pool.memset(k.ei, NO_NODE).then_inc(k.edges_pre, 1)
    pool.memset(k.x[:, (NT - 1) * D:NT * D], 0.0).then_inc(k.xpad, 1)
    pool.memset(k.ident[:, :], 0.0)
    pool.memset(k.lt[:, :], 0.0)
    pool.memset(k.ones, 1.0)
    pool.memset(k.zero, 0.0)
    pool.memset(k.eps[:, :], EPS)
    pool.iota(k.iotai, pattern=[[1, NPAD]], base=0, channel_multiplier=0)
    pool.iota(k.thri[:, :], pattern=[[P, NT]], base=0, channel_multiplier=0)
    pool.iota(k.qcoli[:, :], pattern=[[0, 1]], base=0, channel_multiplier=1)
    pool.iota(k.iota8i[:, :], pattern=[[1, 8]], base=0, channel_multiplier=0)
    pool.drain()
    pool.affine_select(out=k.ident[:, :], in_=k.ident[:, :], compare_op=ALU.not_equal, fill=1.0, base=0,
                       pattern=[[-1, P]], channel_multiplier=1)
    pool.affine_select(out=k.lt[:, 0:NT], in_=k.lt[:, 0:NT], compare_op=ALU.is_ge, fill=1.0, base=0,
                       pattern=[[-1, NT]], channel_multiplier=1)
    pool.affine_select(out=k.lt[:, NT:2 * NT], in_=k.lt[:, NT:2 * NT], compare_op=ALU.is_gt, fill=1.0, base=0,
                       pattern=[[-1, NT]], channel_multiplier=1)
    pool.tensor_copy(k.thr[:, :], k.thri[:, :])
    pool.tensor_copy(k.iota8[:, :], k.iota8i[:, :])
    pool.tensor_copy(k.iota8h[:, :], k.iota8i[:, :])
    pool.drain()
    pool.tensor_scalar(k.qcol[:, 0:1], k.qcoli[:, :], -FAR, None, ALU.add)
    pool.tensor_scalar(k.qcol[:, 1:2], k.qcoli[:, :], 1.0, None, ALU.add)
    pool.tensor_scalar(k.bins[:, :], k.iota8[:, 0:BINS - 1], 0.5, -1.5, ALU.mult, ALU.add)
    pool.drain().then_inc(k.consts, 1)
    pool.memset(k.stage, 0.0).then_inc(k.stage_zero, 1)

    pool.wait_ge(k.bounds_ready, 2)
    pool.wait_ge(k.edgeT_done, 1)
    with pool.Fori(0, NT) as t:
        first = pool.value_load(k.bnd[0:1, bass.ds(t, 1)], min_val=0, max_val=NS * NT)
        end = pool.value_load(k.bnd[0:1, bass.ds(t + NT, 1)], min_val=1, max_val=NS * NT + 1)
        shift = pool.value_load(k.bnd[0:1, bass.ds(t + 2 * NT, 1)], min_val=-NS * NT, max_val=NS)
        pool.drain()
        pool.tensor_copy(k.tile_iota, k.iota[:, bass.ds(t * P, P)])
        with pool.Fori(first, end) as n:
            q = k.nc.s_assert_within(pool.snap(n + shift), 0, NS - 1,
                                     skip_runtime_bounds_check_because="first <= n < end, so lo <= q < hi <= NS")
            pool.drain()
            pool.tensor_copy(k.dnow, k.dstp[:, bass.ds(q * BPS, BPS - 1)])
            pool.drain()
            for c in range(BPS - 1):
                pool.wait_ge(k.oh_used, n * BPS + c + 1)
                pool.sem_inc(k.ohd_free, 1)
                pool.tensor_scalar(k.ohd[c], k.tile_iota, k.dnow[:, c:c + 1], None,
                                   ALU.is_equal).then_inc(k.ohd_ready, 1)

    def gather_tile(i, par):
        pool.wait_ge(k.idx_ready, i + 1)
        for g in range(NG):
            r = g % RING
            pool.wait_ge(k.val_ready, i * NG + g + 1)
            pool.wait_ge(k.grp_done, i * NG + g + 1)
            pool.sem_inc(k.ring_free, 1)
            for s in range(GS):
                j = g * GS + s
                slot = r * GS + s
                pool.indirect_dma_start(
                    out=k.big[:, slot * 2 * D:(slot + 1) * 2 * D], out_offset=None, in_=k.wdu_d,
                    in_offset=bass.IndirectOffsetOnAxis(ap=k.idx[par][:, j:j + 1], axis=0),
                ).then_inc(k.landed[r], 16)

    with pool.Fori(0, NT // 2) as pair:
        gather_tile(pair * 2, 0)
        gather_tile(pair * 2 + 1, 1)

    pool.wait_ge(k.x2_done, NT)
    pool.memset(k.upper, 0.0)
    pool.memset(k.ones1, 1.0)
    pool.iota(k.iotasi, pattern=[[1, SLOTS]], base=0, channel_multiplier=0)
    pool.iota(k.ids, pattern=[[P, NT]], base=0, channel_multiplier=1)
    pool.drain()
    pool.affine_select(out=k.upper, in_=k.upper, compare_op=ALU.is_ge, fill=1.0, base=0,
                       pattern=[[-1, P]], channel_multiplier=1)
    pool.tensor_copy(k.iotas, k.iotasi)
    pool.drain().then_inc(k.e_consts, 1)
    pool.wait_ge(k.b1_in, 16)
    pool.wait_ge(k.ht_ready, NT)
    for t in range(NT):
        tile_ = k.x[:, t * D:(t + 1) * D]
        pool.tensor_tensor(tile_, tile_, k.b1, ALU.add).then_inc(k.xb_ready, 1)
    pool.wait_ge(k.g_ready, NT * len(UNITS))
    pool.tensor_scalar(k.zxv[:, :, 2 * D:ROW], k.ids.unsqueeze(2), -1.0, ID0, ALU.mult, ALU.add)
    pool.drain().then_inc(k.ids_ready, 1)
    pool.wait_ge(k.cleared, 16 * -(-SLOTS * ROW // (2 * NPAD)))
    pool.wait_ge(k.pos_ready, 1)
    for t in range(NT):
        pool.indirect_dma_start(out=k.zs_d, out_offset=bass.IndirectOffsetOnAxis(ap=k.posi[:, t:t + 1], axis=0),
                                in_=k.zx[t], in_offset=None).then_inc(k.sorted, 16)

    def store(m, r):
        pool.wait_ge(k.x4_done, m + 3)
        pool.sem_inc(k.x4_seen, 1)
        pool.indirect_dma_start(out=k.out_d, out_offset=bass.IndirectOffsetOnAxis(ap=k.oid[r], axis=0),
                                in_=k.xb[r][:, D:2 * D], in_offset=None, bounds_check=N - 1,
                                oob_is_err=False).then_inc(k.stored[r], 16)

    pool.wait_ge(k.rounds_ready, 1)
    rounds = pool.value_load(k.rounds[0:1, 0:1], min_val=FEWEST, max_val=ROUNDS)
    full = pool.value_load(k.rounds[0:1, 1:2], min_val=FEWEST - 1, max_val=ROUNDS - 1)
    with pool.Fori(0, full) as q:
        for r in range(XR):
            store(q * XR + r, r)
    with pool.Fori(full, rounds) as q:
        for r in range(XR // 2):
            store(q * XR + r, r)


def act_program(act, k):
    copy = ACT.Copy
    act.wait_ge(k.consts, 1)
    act.wait_ge(k.edgeT_ready, 1)
    by_step = "p (c q) -> p q c"
    act.activation(k.dstp.rearrange("p (q c) -> p q c", c=BPS),
                   k.tr[0][:, 0:BPS * NS].rearrange(by_step, c=BPS), copy)
    act.activation(k.tabv[:, :, BPS:BPS + 1],
                   k.tr[0][:, (BPS - 1) * NS:BPS * NS].unsqueeze(2), copy)
    act.activation(k.tabv[:, :, 0:BPS],
                   k.tr[1][:, 0:BPS * NS].rearrange(by_step, c=BPS), copy).then_inc(k.edgeT_done, 1)
    act.wait_ge(k.row_ready, 1)
    act.activation(k.row[:, :], k.tr[0][0:1, 0:3 * NT], copy).then_inc(k.lh_ready, 1)

    def count_rows(t, s):
        act.wait_ge(k.acc_ready, t + 1)
        act.wait_ge(k.trp_ready, t * 3 - 3)
        act.activation(k.stage[:, s * NPAD:s * NPAD + N], k.acc[s][:, 0:N], copy,
                       accum_out=k.degin[:, bass.ds(t, 1)]).then_inc(k.stage_ready, 1)

    def count_cols(t, s):
        at = k.AT[:, :].rearrange("p (j c) -> p j c", c=NPAD)
        for b, j0 in enumerate((0, 4, 8)):
            n = min(4, NT - j0)
            act.wait_ge(k.trp_ready, t * 3 + b + 1)
            act.activation(at[:, j0:j0 + n, bass.ds(t * P, P)],
                           k.tr[(s + b) % 2][:, 0:n * P].rearrange("p (j c) -> p j c", c=P),
                           copy).then_inc(k.at_done, 1)

    act.wait_ge(k.acc_ready, 1)
    act.wait_ge(k.cleared, 16 * -(-SLOTS * ROW // (2 * NPAD)))
    act.activation(k.stage[:, 0:N], k.acc[0][:, 0:N], copy, accum_out=k.degin[:, 0:1]).then_inc(k.stage_ready, 1)
    act.wait_ge(k.acc_ready, 2)
    act.activation(k.stage[:, NPAD:NPAD + N], k.acc[1][:, 0:N], copy,
                   accum_out=k.degin[:, 1:2]).then_inc(k.stage_ready, 1)
    count_cols(0, 0)
    with act.Fori(1, NT // 2) as h:
        count_rows(2 * h, 0)
        count_cols(2 * h - 1, 1)
        count_rows(2 * h + 1, 1)
        count_cols(2 * h, 0)
    count_cols(NT - 1, 1)

    act.wait_ge(k.stats0, 1)
    act.activation(k.rs[:, 0:NT], k.mv[:, NT:2 * NT], ACT.Sqrt, bias=k.eps[:, :]).then_inc(k.sd0_ready, 1)
    act.wait_ge(k.degs_ready, 1)
    act.activation(k.dsq[:, 0:2 * NT], k.deg[:, 0:2 * NT], ACT.Sqrt).then_inc(k.degsq_ready, 1)
    act.wait_ge(k.dinvB_psum, 1)
    act.activation(k.dinvB[:, 0:512], k.tr[0][:, :], copy)
    act.activation(k.dinvB[:, 512:1024], k.tr[1][:, :], copy).then_inc(k.dinvB_ready, 1)
    act.wait_ge(k.dinvB_psum, 2)
    act.activation(k.dinvB[:, 1024:NPAD], k.tr[0][:, 0:NPAD - 1024], copy).then_inc(k.dinvB_ready, 1)
    act.wait_ge(k.dego_ready, 1)
    act.activation(k.dsq[:, 2 * NT:3 * NT], k.deg[:, 2 * NT:3 * NT], ACT.Sqrt).then_inc(k.degosq_ready, 1)
    act.wait_ge(k.par_in, 16)
    for o in range(FT):
        act.wait_ge(k.out_ready, o + 1)
        act.activation(k.outT[:, o * NPAD:o * NPAD + N], k.acc[o % 2][:, 0:N], ACT.Identity,
                       bias=k.par[:, o:o + 1]).then_inc(k.outT_done, 1)
    act.wait_ge(k.bnvar_ready, 1)
    act.activation(k.bsd[:, :], k.bmv[:, FT:2 * FT], ACT.Sqrt, bias=k.eps[:, :]).then_inc(k.bnsd_ready, 1)
    act.wait_ge(k.bn_ready, 1)

    def gelu(i, par):
        if i > 1:
            act.wait_ge(k.tk_ready, i - 1)
        for o in range(FT):
            ins = act.activation(k.gtt[par][:, o * P:(o + 1) * P], k.outT[:, o * NPAD + i * P:o * NPAD + (i + 1) * P],
                                 ACT.Gelu, bias=k.bsc[:, FT + o:FT + o + 1], scale=k.bsc[:, o:o + 1])
        ins.then_inc(k.gelu_done, 1)

    def root(i):
        act.wait_ge(k.var_ready, i + 1)
        act.activation(k.tsd[:, 0:2], k.tmv[:, 2:4], ACT.Sqrt, bias=k.eps[:, :]).then_inc(k.sd_ready, 1)

    def copy_yT(i):
        act.wait_ge(k.yt_ready, i + 1)
        act.activation(k.yT[:, :], k.YT, copy).then_inc(k.yT_done, 1)

    def copy_q(i, half):
        act.wait_ge(k.q_ready, 2 * i + half + 1)
        if half == 0:
            act.wait_ge(k.s_ready, i * H)
        for b in range(4):
            h = 4 * half + b
            act.activation(k.qT[:, h * P:(h + 1) * P], k.Q[:, b * P:(b + 1) * P], ACT.Identity,
                           bias=k.par[:, 4 * FT + h:4 * FT + h + 1]).then_inc(k.qT_done, 1)

    def exps(i):
        act.wait_ge(k.exp_in, i + 1)
        act.activation(k.ex[:, :], k.sm[:, :], ACT.Exp).then_inc(k.exp_done, 1)

    pieces = {1: root, 3: copy_yT, 4: lambda i: copy_q(i, 0), 5: lambda i: copy_q(i, 1), 12: exps}

    def search(i):
        for g in sorted(pieces):
            pieces[g](i)

    def tile(i, par, ahead):
        for g in range(NG):
            if g in pieces and (ahead or g == 1):
                pieces[g](i + 1)
            act.wait_ge(k.val_ready, i * NG + g + 1 + RING)
            act.wait_ge(k.grp_done, i * NG + g - 1 + RING)
            for s in range(GS):
                j = g * GS + s
                ins = act.activation(k.diag[:, ((g % 2) * GS + s) * P:((g % 2) * GS + s + 1) * P], k.ident[:, :],
                                     copy, scale=k.val[:, j:j + 1])
            ins.then_inc(k.diag_ready, 1)

    gelu(0, 0)
    search(0)
    for i in range(1, NT):
        gelu(i, i % 2)
    with act.Fori(0, NT // 2 - 1) as pair:
        tile(pair * 2, 0, True)
        tile(pair * 2 + 1, 1, True)
    tile(NT - 2, 0, True)
    tile(NT - 1, 1, False)

    root(NT + 1)
    with act.Fori(0, NT) as t:
        act.wait_ge(k.var4_ready, t + 1)
        act.activation(k.rs[:, bass.ds(t, 1)], k.mv[:, bass.ds(t + NT, 1)], ACT.Sqrt,
                       bias=k.eps[:, :]).then_inc(k.sd4_ready, 1)

    def copy_zT(m, par):
        act.wait_ge(k.zt_ready, m + 1)
        act.activation(k.zT[par][:, :], k.ZB[par], copy).then_inc(k.zT_done, 1)

    act.wait_ge(k.rounds_ready, 1)
    rounds = act.value_load(k.rounds[0:1, 0:1], min_val=FEWEST, max_val=ROUNDS)
    full = act.value_load(k.rounds[0:1, 1:2], min_val=FEWEST - 1, max_val=ROUNDS - 1)
    with act.Fori(0, full) as q:
        for r in range(XR):
            copy_zT(q * XR + r, r % 2)
    with act.Fori(full, rounds) as q:
        for r in range(XR // 2):
            copy_zT(q * XR + r, r % 2)


def dve_program(dve, k):
    def stats(tile, t):
        dve.bn_stats(k.st[:, 6 * t:6 * t + 6], tile)

    dve.wait_ge(k.edges_in, 64)
    dve.tensor_copy(k.ef, k.ei).then_inc(k.edge_f, 1)
    dve.drain()
    dve.tensor_reduce(k.mm[:, 0:1], k.ef[:, 0:SPAN], AX.X, ALU.min)
    dve.tensor_reduce(k.mm[:, 1:2], k.ef[:, 0:SPAN], AX.X, ALU.max)
    dve.wait_ge(k.consts, 1)
    dve.tensor_copy(k.iota, k.iotai)
    dve.drain()
    a, b = k.ov[:, 0:NT], k.ov[:, NT:2 * NT]
    low, high = k.ov[:, 2 * NT:3 * NT], k.ov[:, 3 * NT:4 * NT]
    dve.tensor_scalar(a, k.thr[0:NS, :], k.mm[:, 1:2], None, ALU.is_le)
    dve.tensor_scalar(b, k.thr[0:NS, :], float(P), k.mm[:, 0:1], ALU.add, ALU.is_gt)
    dve.drain()
    dve.tensor_tensor(a, a, b, ALU.mult)
    dve.drain()
    dve.tensor_scalar(low, a, k.qcol[:, 0:1], FAR, ALU.mult, ALU.add)
    dve.tensor_scalar(high, a, k.qcol[:, 1:2], None, ALU.mult)
    dve.drain().then_inc(k.ov_done, 1)
    dve.wait_ge(k.lowT_ready, 1)
    lo, hi, ln, pos = (k.lh[:, c:c + 1] for c in range(4))
    dve.tensor_reduce(lo, k.acc[0][0:NT, 0:NS], AX.X, ALU.min)
    dve.tensor_reduce(hi, k.acc[0][0:NT, NS:2 * NS], AX.X, ALU.max)
    dve.drain()
    dve.tensor_scalar(pos, hi, 0.0, None, ALU.is_gt)
    dve.tensor_scalar(hi, hi, 1.0, None, ALU.max)
    dve.drain()
    dve.tensor_tensor(lo, lo, pos, ALU.mult)
    dve.drain()
    dve.tensor_tensor(ln, hi, lo, ALU.subtract)
    dve.drain().then_inc(k.bounds_ready, 1)
    dve.wait_ge(k.lh_ready, 1)
    dve.tensor_copy(k.bnd[:, 0:2 * NT], k.row[:, NT:3 * NT])
    dve.tensor_tensor(k.bnd[:, 2 * NT:3 * NT], k.row[:, 0:NT], k.row[:, NT:2 * NT], ALU.subtract)
    dve.drain().then_inc(k.bounds_ready, 1)
    dve.wait_ge(k.x_in, 32)
    dve.wait_ge(k.edgeT_done, 1)
    with dve.Fori(0, NT) as t:
        first = dve.value_load(k.bnd[0:1, bass.ds(t, 1)], min_val=0, max_val=NS * NT)
        end = dve.value_load(k.bnd[0:1, bass.ds(t + NT, 1)], min_val=1, max_val=NS * NT + 1)
        shift = dve.value_load(k.bnd[0:1, bass.ds(t + 2 * NT, 1)], min_val=-NS * NT, max_val=NS)
        dve.bn_stats(k.st[:, bass.ds(t * 6, 6)], k.x[:, bass.ds(t * D, D)])
        with dve.Fori(first, end) as n:
            q = k.nc.s_assert_within(dve.snap(n + shift), 0, NS - 1,
                                     skip_runtime_bounds_check_because="first <= n < end, so lo <= q < hi <= NS")
            dve.drain()
            dve.tensor_copy(k.now, k.tab[:, bass.ds(q * (BPS + 1), BPS + 1)])
            dve.drain()
            for c in range(BPS):
                if c % 2 == 0:
                    dve.wait_ge(k.oh_used, n * BPS + c + 2)
                dve.tensor_scalar(k.ohs[c][:, 0:N], k.iota[:, 0:N], k.now[:, c:c + 1], None,
                                  ALU.is_equal).then_inc(k.oh_ready, 1)
            dve.tensor_scalar(k.ohd[BPS - 1], k.iota[:, bass.ds(t * P, P)], k.now[:, BPS:BPS + 1], None,
                              ALU.is_equal).then_inc(k.oh_ready, 1)

    dve.drain()
    mv = k.mv[:, :].rearrange("p (c t) -> p t c", c=2)
    for t in range(NT):
        dve.bn_aggr(mv[:, t, :], k.st[:, 6 * t:6 * t + 6])
    dve.drain().then_inc(k.stats0, 1)
    dve.wait_ge(k.stage_ready, NT)
    dve.tensor_scalar(k.deg[:, 0:NT], k.degin[:, :], 1.0, None, ALU.add)
    dve.tensor_scalar(k.deg[:, NT:2 * NT], k.degin[:, :], 1.0, None, ALU.max)
    dve.drain().then_inc(k.degs_ready, 1)
    dve.wait_ge(k.sd0_ready, 1)
    dve.reciprocal(k.rs[:, NT:2 * NT], k.rs[:, 0:NT])
    dve.wait_ge(k.degsq_ready, 1)
    dve.reciprocal(k.dri[:, 0:2 * NT], k.dsq[:, 0:2 * NT])
    dve.drain()
    dve.tensor_tensor(k.comb[:, :], k.rs[:, NT:2 * NT], k.dri[:, 0:NT], ALU.mult)
    dve.tensor_scalar(k.pq[:, 0:NT], k.rs[:, NT:2 * NT], 1.0, None, ALU.add)
    dve.tensor_tensor(k.pq[:, NT:2 * NT], k.rs[:, NT:2 * NT], k.mv[:, 0:NT], ALU.mult)
    dve.wait_ge(k.at_done, 3 * NT)
    dve.drain()
    for t in range(NT):
        diag = k.AT[:, t * NPAD + t * P:t * NPAD + (t + 1) * P]
        dve.tensor_tensor(diag, diag, k.ident[:, :], ALU.add)
        dve.tensor_scalar(k.h0[:, t * D:(t + 1) * D], k.x[:, t * D:(t + 1) * D], k.mv[:, t:t + 1],
                          k.comb[:, t:t + 1], ALU.subtract, ALU.mult)
        dve.drain().then_inc(k.h0_ready, 1)
    for t in range(NT):
        dve.tensor_scalar(k.dg[:, t * P:(t + 1) * P], k.ident[:, :], k.dri[:, t:t + 1], None, ALU.mult)
    dve.drain().then_inc(k.dg_ready, 1)
    dve.tensor_reduce(k.degin[:, :], k.AT[:, :].rearrange("p (j c) -> p j c", c=NPAD), AX.X, ALU.add)
    dve.drain()
    dve.tensor_scalar(k.deg[:, 2 * NT:3 * NT], k.degin[:, :], -1.0, 1.0, ALU.add, ALU.max)
    dve.drain().then_inc(k.dego_ready, 1)
    for t in range(NT):
        tile = k.x[:, t * D:(t + 1) * D]
        dve.tensor_scalar(tile, tile, k.pq[:, t:t + 1], k.pq[:, NT + t:NT + t + 1], ALU.mult, ALU.subtract)
    dve.wait_ge(k.degosq_ready, 1)
    dve.reciprocal(k.dri[:, 2 * NT:3 * NT], k.dsq[:, 2 * NT:3 * NT])
    dve.wait_ge(k.dinvB_ready, 2)
    for f in range(FT):
        dve.wait_ge(k.agg_ready, f + 1)
        dve.tensor_tensor(k.aggT[:, f * NPAD:f * NPAD + N], k.acc[f % 2][:, 0:N], k.dinvB[:, 0:N],
                          ALU.mult).then_inc(k.aggT_done, 1)
    dve.memset(k.outT[:, :].rearrange("p (o c) -> p o c", c=NPAD)[:, :, N:NPAD], 0.0)
    bmv = k.bmv[:, :].rearrange("p (c o) -> p o c", c=2)
    for o in range(FT):
        dve.wait_ge(k.outT_done, o + 1)
        for c, (c0, n) in enumerate(CHUNKS):
            dve.bn_stats(k.bst[:, (o * 3 + c) * 6:(o * 3 + c + 1) * 6], k.outT[:, o * NPAD + c0:o * NPAD + c0 + n])
        dve.drain()
        dve.bn_aggr(bmv[:, o, :], k.bst[:, o * 18:(o + 1) * 18])
    dve.drain().then_inc(k.bnvar_ready, 1)
    dve.wait_ge(k.bnsd_ready, 1)
    dve.reciprocal(k.bsd[:, :], k.bsd[:, :])
    dve.wait_ge(k.par_in, 16)
    dve.drain()
    dve.tensor_tensor(k.bsc[:, 0:FT], k.bsd[:, :], k.par[:, FT:2 * FT], ALU.mult)
    dve.drain()
    dve.tensor_tensor(k.bsc[:, FT:2 * FT], k.bsc[:, 0:FT], k.bmv[:, 0:FT], ALU.mult)
    dve.drain()
    dve.tensor_tensor(k.bsc[:, FT:2 * FT], k.par[:, 2 * FT:3 * FT], k.bsc[:, FT:2 * FT], ALU.subtract)
    dve.drain().then_inc(k.bn_ready, 1)

    def add_gelu(i, par):
        dve.wait_ge(k.tk_ready, i + 1)
        tile = k.x[:, i * D:(i + 1) * D]
        dve.tensor_tensor(tile, tile, k.TK[par], ALU.add).then_inc(k.x1_done, 1)

    add_gelu(0, 0)
    dve.memset(k.tmv[:, :], 1.0)
    dve.drain()

    def norms(i, search, done):
        for c, (on, j) in enumerate(((search, i), (done, i - 2))):
            if on:
                dve.bn_stats(k.tst[:, 6 * c:6 * c + 6], k.x[:, bass.ds(j * D, D)])
        dve.drain()
        tmv = k.tmv[:, :].rearrange("p (v c) -> p c v", c=2)
        for c, on in enumerate((search, done)):
            if on:
                dve.bn_aggr(tmv[:, c, :], k.tst[:, 6 * c:6 * c + 6])
        dve.drain().then_inc(k.var_ready, 1)

    def normed(i, par, search, done):
        dve.wait_ge(k.sd_ready, i + 1)
        dve.reciprocal(k.tsd[:, 2:4], k.tsd[:, 0:2])
        dve.drain()
        if search:
            dve.tensor_scalar(k.y[:, par * D:(par + 1) * D], k.x[:, bass.ds(i * D, D)], k.tmv[:, 0:1], k.tsd[:, 2:3],
                              ALU.subtract, ALU.mult).then_inc(k.y_ready, 1)
        if done:
            dve.tensor_tensor(k.hco[:, :], k.tsd[:, 3:4], k.dri[:, bass.ds(i - 2 + 2 * NT, 1)], ALU.mult)
            dve.drain()
            dve.tensor_scalar(k.h1[:, :], k.x[:, bass.ds((i - 2) * D, D)], k.tmv[:, 1:2], k.hco[:, :],
                              ALU.subtract, ALU.mult).then_inc(k.ht_ready, 1)

    def add_units(j, u0, n_units):
        for u in range(u0, u0 + n_units):
            f, c0, n = UNITS[u]
            piece = k.agg1[:, f * NPAD + c0:f * NPAD + c0 + n]
            dve.wait_ge(k.g_ready, j * len(UNITS) + u + 1)
            dve.tensor_tensor(piece, piece, k.G[u % 2][:, 0:n], ALU.add).then_inc(k.g_used, 1)

    def top_heads(i, h0):
        for h in (h0, h0 + 1):
            dve.wait_ge(k.s_ready, i * H + h + 1)
            dve.sem_inc(k.s_seen, 1)
            for c in range(2):
                dve.max(k.top[:, c * HK + h * 8:c * HK + h * 8 + 8], k.S[h % 2][c][:, 0:NK])
            dve.drain()
            for c in range(2):
                ins = dve.max_index(k.topi[:, c * HK + h * 8:c * HK + h * 8 + 8],
                                    k.top[:, c * HK + h * 8:c * HK + h * 8 + 8], k.S[h % 2][c][:, 0:NK])
            dve.drain().then_inc(k.topk_done, 1)

    def pairs(i, par):
        shape = [P, H, 8, 8]
        t1 = k.top[:, 0:HK].rearrange("p (h a) -> p h a", h=H).unsqueeze(3).to_broadcast(shape)
        t2 = k.top[:, HK:2 * HK].rearrange("p (h b) -> p h b", h=H).unsqueeze(2).to_broadcast(shape)
        dve.tensor_tensor(k.all.rearrange("p (h a b) -> p h a b", h=H, a=8), t1, t2, ALU.add)
        dve.tensor_copy(k.topf[:, :], k.topi[:, :])
        dve.drain()
        for h in range(H):
            dve.max(k.best[:, h * 8:h * 8 + 8], k.all[:, h * 64:(h + 1) * 64])
        dve.drain()
        for h in range(H):
            dve.max_index(k.pos[:, h * 8:h * 8 + 8], k.best[:, h * 8:h * 8 + 8], k.all[:, h * 64:(h + 1) * 64])
        dve.drain()

    def halves(i, par):
        best = k.best[:, :].rearrange("p (h a) -> p h a", a=8)
        dve.tensor_scalar(k.posab[:, 0:HK], k.pos[:, :], 3, None, ALU.logical_shift_right)
        dve.tensor_scalar(k.posab[:, HK:2 * HK], k.pos[:, :], 7, None, ALU.bitwise_and)
        dve.tensor_tensor(k.sm[:, :].rearrange("p (h a) -> p h a", a=8), best,
                          best[:, :, 0:1].to_broadcast([P, H, 8]), ALU.subtract).then_inc(k.exp_in, 1)
        dve.drain()
        dve.tensor_copy(k.posf[:, :], k.posab[:, :])
        dve.drain()
        dve.tensor_tensor(k.pickh.rearrange("p (j a) -> p j a", a=8),
                          k.posf[:, :].unsqueeze(2).to_broadcast([P, 2 * HK, 8]),
                          k.iota8h[:, :].unsqueeze(1).to_broadcast([P, 2 * HK, 8]), ALU.is_equal)
        dve.drain()

    def rows(i, par):
        pick4 = k.pickh.rearrange("p (h j a) -> p h j a", h=2 * H, a=8)
        dve.tensor_tensor(pick4, pick4, k.topf[:, :].rearrange("p (h a) -> p h a", a=8).unsqueeze(2)
                          .to_broadcast([P, 2 * H, 8, 8]), ALU.mult)
        dve.drain()
        dve.tensor_reduce(k.iab[:, :], k.pickh.rearrange("p (j a) -> p j a", a=8), AX.X, ALU.add)
        dve.drain()
        dve.scalar_tensor_tensor(k.idx[par][:, :], k.iab[:, 0:HK], float(NK), k.iab[:, HK:2 * HK],
                                 ALU.mult, ALU.add).then_inc(k.idx_ready, 1)

    def softmax(i, par):
        dve.wait_ge(k.exp_done, i + 1)
        ex = k.ex[:, :].rearrange("p (h a) -> p h a", a=8)
        dve.tensor_reduce(k.ssum[:, 0:H], ex, AX.X, ALU.add)
        dve.drain()
        dve.reciprocal(k.ssum[:, H:2 * H], k.ssum[:, 0:H])
        dve.drain()
        dve.tensor_tensor(k.prob[:, par * HK:(par + 1) * HK].rearrange("p (h a) -> p h a", a=8), ex,
                          k.ssum[:, H:2 * H].unsqueeze(2).to_broadcast([P, H, 8]), ALU.mult)

    pieces = {6: lambda i, p: top_heads(i, 0), 7: lambda i, p: top_heads(i, 2),
              8: lambda i, p: top_heads(i, 4), 9: lambda i, p: top_heads(i, 6), 10: pairs, 11: halves, 12: rows, 14: softmax}

    def add_rows(i, par):
        dve.wait_ge(k.grp_done, i * NG + NG + RING)
        t = k.x[:, bass.ds(i * D, D)]
        dve.tensor_tensor(t, t, k.O[par], ALU.add).then_inc(k.x2_done, 1)
        dve.drain()

    def search(i, par):
        norms(i, True, False)
        normed(i, par, True, False)
        for g in sorted(pieces):
            pieces[g](i, par)

    def tile(i, par, ahead, behind):
        first_tile = not behind
        for g in range(NG):
            if g == 1:
                if behind:
                    add_rows(i - 1, 1 - par)
                norms(i + 1, ahead, behind)
            if g == 2:
                normed(i + 1, 1 - par, ahead, behind)
            if ahead and g in pieces:
                pieces[g](i + 1, 1 - par)
            if behind and g > NG - len(UNITS) // UPP:
                add_units(i - 1, (g - 1) * UPP - FIRST_UNIT, UPP)
            if first_tile and g in (3, 4):
                for t in range((g - 3) * (NT // 2), (g - 2) * (NT // 2)):
                    loops = k.AT[:, t * NPAD + t * P:t * NPAD + (t + 1) * P]
                    dve.tensor_tensor(loops, loops, k.ident[:, :], ALU.subtract)
            if first_tile and g >= NG - FT:
                dve.memset(k.agg1[:, (g - NG + FT) * NPAD:(g - NG + FT + 1) * NPAD], 0.0)
            r = g % RING
            use = i * (NG // RING) + g // RING
            dve.wait_ge(k.landed[r], use * (16 * GS) + 16 * GS)
            for s in range(GS):
                slot = (r * GS + s) * 2 * D
                dve.tensor_tensor_reduce(out=k.big[:, slot:slot + D], in0=k.big[:, slot:slot + D],
                                         in1=k.y[:, par * D:(par + 1) * D], scale=1.0, scalar=0.0,
                                         op0=ALU.mult, op1=ALU.add,
                                         accum_out=k.inner[:, g * GS + s:g * GS + s + 1])
            dve.drain()
            dve.scalar_tensor_tensor(k.val[:, g * GS:(g + 1) * GS], k.inner[:, g * GS:(g + 1) * GS], 0.0,
                                     k.prob[:, par * HK + g * GS:par * HK + (g + 1) * GS],
                                     ALU.max, ALU.mult).then_inc(k.val_ready, 1)
        if behind:
            add_units(i - 1, len(UNITS) - UPP, UPP)

    dve.sem_inc(k.val_ready, RING)
    dve.sem_inc(k.g_used, 2)
    search(0, 0)
    for i in range(1, NT):
        add_gelu(i, i % 2)
    tile(0, 0, True, False)
    tile(1, 1, True, True)
    with dve.Fori(1, NT // 2 - 1) as pair:
        tile(pair * 2, 0, True, True)
        tile(pair * 2 + 1, 1, True, True)
    tile(NT - 2, 0, True, True)
    tile(NT - 1, 1, False, True)

    add_rows(NT - 1, (NT - 1) % 2)
    norms(NT + 1, False, True)
    normed(NT + 1, 1, False, True)
    add_units(NT - 1, 0, len(UNITS))
    dve.drain()

    def normed_row(t):
        dve.wait_ge(k.sd4_ready, t + 1)
        dve.reciprocal(k.rs[:, NT + t:NT + t + 1], k.rs[:, t:t + 1])
        dve.drain()
        dve.tensor_scalar(k.zx[t][:, 0:D], k.zx[t][:, D:2 * D], k.mv[:, t:t + 1], k.rs[:, NT + t:NT + t + 1],
                          ALU.subtract, ALU.mult)

    for t in range(NT):
        dve.wait_ge(k.g1_ready, t + 1)
        dve.wait_ge(k.xb_ready, t + 1)
        dve.scalar_tensor_tensor(k.zx[t][:, D:2 * D], k.tr[t % 2][:, :], k.dri[:, NT + t:NT + t + 1],
                                 k.x[:, t * D:(t + 1) * D], ALU.mult, ALU.add).then_inc(k.x3_done, 1)
        dve.drain()
        stats(k.zx[t][:, D:2 * D], t)
        if t:
            normed_row(t - 1)
        else:
            dve.wait_ge(k.e_consts, 1)
            dve.tensor_tensor(k.lt8.rearrange("p (a b) -> p a b", a=BINS),
                              k.iota8[:, :].unsqueeze(1).to_broadcast([P, BINS, BINS]),
                              k.iota8[:, :].unsqueeze(2).to_broadcast([P, BINS, BINS]), ALU.is_lt)
        dve.drain()
        dve.bn_aggr(mv[:, t, :], k.st[:, 6 * t:6 * t + 6]).then_inc(k.var4_ready, 1)
    normed_row(NT - 1)
    dve.drain()
    gtb = k.gtb.rearrange("p (t b) -> p t b", t=NT)
    dve.tensor_tensor(gtb, k.bins[:, :].unsqueeze(1).to_broadcast([P, NT, BINS - 1]),
                      k.zxv[:, :, 0:1].to_broadcast([P, NT, BINS - 1]), ALU.is_lt)
    dve.drain()
    dve.tensor_reduce(k.mem, gtb, AX.X, ALU.add)
    dve.drain()
    sel = k.sel.rearrange("p (t b) -> p t b", t=NT)
    dve.tensor_tensor(sel, k.iota8[:, :].unsqueeze(1).to_broadcast([P, NT, BINS]),
                      k.mem.unsqueeze(2).to_broadcast([P, NT, BINS]), ALU.is_equal).then_inc(k.sel_ready, 1)
    dve.memset(k.cnt[:, 0:BINS], 0.0)
    dve.drain()
    dve.wait_ge(k.rank_psum, 1)
    for t in range(NT):
        dve.tensor_tensor(k.cnt[:, (t + 1) * BINS:(t + 2) * BINS], k.cnt[:, t * BINS:(t + 1) * BINS],
                          k.RK[1][:, t * BINS:(t + 1) * BINS], ALU.add)
        dve.drain()
    dve.tensor_tensor(k.rank, k.RK[0][:, 0:NT * BINS], k.cnt[:, 0:NT * BINS], ALU.add)
    cmp_ = k.cmp.rearrange("p (b m) -> p b m", b=BINS)
    dve.tensor_tensor(cmp_, k.cnt[:, NT * BINS:].unsqueeze(2).to_broadcast([P, BINS, NT]),
                      k.thr[:, :].unsqueeze(1).to_broadcast([P, BINS, NT]), ALU.is_gt)
    dve.drain()
    dve.tensor_reduce(k.tiles, cmp_, AX.X, ALU.add)
    dve.drain()
    lt8 = k.lt8.rearrange("p (a b) -> p a b", a=BINS)
    dve.tensor_tensor(lt8, lt8, k.tiles.unsqueeze(1).to_broadcast([P, BINS, BINS]), ALU.mult)
    dve.drain()
    dve.tensor_reduce(k.base, lt8, AX.X, ALU.add)
    dve.drain()
    dve.scalar_tensor_tensor(k.rank.rearrange("p (t b) -> p t b", t=NT),
                             k.base.unsqueeze(1).to_broadcast([P, NT, BINS]), float(P),
                             k.rank.rearrange("p (t b) -> p t b", t=NT), ALU.mult, ALU.add)
    cmps = k.cmps.rearrange("p (m b) -> p m b", m=SLOTS)
    dve.tensor_tensor(cmps, k.base.unsqueeze(1).to_broadcast([P, SLOTS, BINS]),
                      k.iotas.unsqueeze(2).to_broadcast([P, SLOTS, BINS]), ALU.is_le)
    dve.drain()
    dve.tensor_tensor(k.rank, k.rank, k.sel, ALU.mult)
    dve.tensor_reduce(k.binf, cmps, AX.X, ALU.add)
    dve.drain()
    dve.tensor_reduce(k.posn, k.rank.rearrange("p (t b) -> p t b", t=NT), AX.X, ALU.add)
    dve.tensor_scalar(k.bini, k.binf, -1.0, None, ALU.add)
    dve.drain()
    dve.wait_ge(k.ids_ready, 1)
    dve.tensor_copy(k.posi, k.posn)
    dve.drain().then_inc(k.pos_ready, 1)
    dve.tensor_tensor(k.used, k.base[:, BINS - 1:BINS], k.tiles[:, BINS - 1:BINS], ALU.add)
    dve.drain()
    dve.tensor_scalar(k.less, k.used, -float(XR // 2), None, ALU.add)
    dve.drain()
    dve.tensor_scalar(k.begun, k.iota8[:, 0:ROUNDS], float(XR), k.less, ALU.mult, ALU.is_lt)
    dve.drain()
    dve.tensor_reduce(k.fullf, k.begun, AX.X, ALU.add)
    dve.drain()
    dve.tensor_scalar(k.rounds[:, 0:1], k.fullf, 1.0, None, ALU.add)
    dve.tensor_copy(k.rounds[:, 1:2], k.fullf)
    dve.tensor_scalar(k.last_full, k.fullf, -1.0, None, ALU.add)
    dve.drain().then_inc(k.rounds_ready, 1)

    def finish(m, r):
        dve.wait_ge(k.e_ready, m + 1)
        dve.tensor_scalar(k.oid[r], k.xb[r][:, 2 * D:ROW], -1.0, ID0, ALU.mult, ALU.add)
        dve.tensor_tensor(k.xb[r][:, D:2 * D], k.xb[r][:, D:2 * D], k.tr[r % 2][:, :], ALU.add)
        dve.drain().then_inc(k.x4_done, 1)

    dve.sem_inc(k.x4_done, 2)
    rounds = dve.value_load(k.rounds[0:1, 0:1], min_val=FEWEST, max_val=ROUNDS)
    full = dve.value_load(k.rounds[0:1, 1:2], min_val=FEWEST - 1, max_val=ROUNDS - 1)
    with dve.Fori(0, full) as q:
        for r in range(XR):
            finish(q * XR + r, r)
    with dve.Fori(full, rounds) as q:
        for r in range(XR // 2):
            finish(q * XR + r, r)


def pe_program(pe, k):
    ident = k.ident[:, :]
    pe.wait_ge(k.consts, 1)
    pe.wait_ge(k.edge_f, 1)
    for c in range(2):
        for b in range(BPS):
            ins = pe.transpose(k.tr[c][:, b * NS:(b + 1) * NS], k.ef[:, c * SPAN + b * P:c * SPAN + (b + 1) * P],
                               k.ident[0:NS, 0:NS])
    ins.then_inc(k.edgeT_ready, 1)
    pe.wait_ge(k.ov_done, 1)
    for c in range(2):
        ins = pe.transpose(k.acc[0][0:NT, c * NS:(c + 1) * NS], k.ov[:, (2 + c) * NT:(3 + c) * NT],
                           k.ident[0:NS, 0:NS])
    ins.then_inc(k.lowT_ready, 1)
    pe.wait_ge(k.bounds_ready, 1)
    pe.wait_ge(k.edgeT_done, 1)
    pe.matmul(k.tr[0][0:1, 0:NT], k.lh[:, 0:1], k.ident[0:NT, 0:NT], start=True, stop=True)
    pe.matmul(k.tr[0][0:1, NT:3 * NT], k.lh[:, 2:3], k.lt[:, :], start=True, stop=True).then_inc(k.row_ready, 1)
    pe.wait_ge(k.bounds_ready, 2)
    pe.sem_inc(k.oh_used, BPS)

    def counts(t, s, between=None):
        first = pe.value_load(k.bnd[0:1, bass.ds(t, 1)], min_val=0, max_val=NS * NT)
        end = pe.value_load(k.bnd[0:1, bass.ds(t + NT, 1)], min_val=1, max_val=NS * NT + 1)
        for c0, n in CHUNKS:
            pe.matmul(k.acc[s][:, c0:c0 + n], k.zero[:, 0:P], k.zero[:, 0:n], start=True, stop=False)
        if between is not None:
            flip(*between, 2)
        with pe.Fori(first, end) as n_step:
            for b in range(BPS):
                if b < BPS - 1:
                    pe.wait_ge(k.ohd_ready, n_step * (BPS - 1) + b + 1)
                pe.wait_ge(k.oh_ready, n_step * (BPS + 1) + b + (2 if b == BPS - 1 else 1))
                for c0, n in CHUNKS:
                    ins = pe.matmul(k.acc[s][:, c0:c0 + n], k.ohd[b], k.ohs[b][:, c0:c0 + n], start=False, stop=False)
                ins.then_inc(k.oh_used, 1)
        for c0, n in CHUNKS:
            ins = pe.matmul(k.acc[s][:, c0:c0 + n], k.zero[:, 0:P], k.zero[:, 0:n], start=False, stop=True)
        ins.then_inc(k.acc_ready, 1)

    def flip(t, s, b):
        if b == 0:
            pe.wait_ge(k.stage_ready, t + 1)
        pe.wait_ge(k.at_done, t * 3 + b - 1 if not isinstance(t, int) else max(t * 3 + b - 1, 0))
        for j in range(4 * b, min(4 * b + 4, NT)):
            ins = pe.transpose(k.tr[(s + b) % 2][:, (j - 4 * b) * P:(j - 4 * b + 1) * P],
                               k.stage[:, s * NPAD + j * P:s * NPAD + (j + 1) * P], ident)
        ins.then_inc(k.trp_ready, 1)

    counts(0, 0)
    counts(1, 1)
    flip(0, 0, 0)
    flip(0, 0, 1)
    with pe.Fori(1, NT // 2) as h:
        pe.wait_ge(k.stage_ready, 2 * h - 1)
        counts(2 * h, 0, between=(2 * h - 2, 0))
        flip(2 * h - 1, 1, 0)
        flip(2 * h - 1, 1, 1)
        pe.wait_ge(k.stage_ready, 2 * h)
        counts(2 * h + 1, 1, between=(2 * h - 1, 1))
        flip(2 * h, 0, 0)
        flip(2 * h, 0, 1)
    flip(NT - 2, 0, 2)
    for b in range(3):
        flip(NT - 1, 1, b)

    def aggregate(h, f, s, ready, at=None):
        for t in range(NT):
            if f == 0:
                pe.wait_ge(ready, t + 1)
            for c0, n in CHUNKS:
                ins = pe.matmul(k.acc[s][:, c0:c0 + n], h[:, t * D + f * P:t * D + (f + 1) * P],
                                k.AT[:, t * NPAD + c0:t * NPAD + c0 + n], start=(t == 0), stop=(t == NT - 1))
        return ins

    aggregate(k.h0, 0, 0, k.h0_ready).then_inc(k.agg_ready, 1)
    pe.wait_ge(k.dg_ready, 1)
    for t in range(8):
        ins = pe.matmul(k.tr[t // 4][:, (t % 4) * P:(t % 4 + 1) * P], k.ones, k.dg[:, t * P:(t + 1) * P],
                        start=True, stop=True)
    ins.then_inc(k.dinvB_psum, 1)
    pe.wait_ge(k.dinvB_ready, 1)
    for t in range(8, NT):
        ins = pe.matmul(k.tr[0][:, (t - 8) * P:(t - 7) * P], k.ones, k.dg[:, t * P:(t + 1) * P],
                        start=True, stop=True)
    ins.then_inc(k.dinvB_psum, 1)
    for f in range(1, FT):
        if f >= 2:
            pe.wait_ge(k.aggT_done, f - 1)
        aggregate(k.h0, f, f % 2, k.h0_ready).then_inc(k.agg_ready, 1)
    pe.wait_ge(k.w_in, 16)
    for o in range(FT):
        pe.wait_ge(k.aggT_done, FT - 1 if o == 0 else FT)
        if o >= 2:
            pe.wait_ge(k.outT_done, o - 1)
        for f in range(FT):
            if f == FT - 1:
                pe.wait_ge(k.aggT_done, FT)
            for c0, n in CHUNKS:
                ins = pe.matmul(k.acc[o % 2][:, c0:c0 + n], k.w0[:, f * D + o * P:f * D + (o + 1) * P],
                                k.aggT[:, f * NPAD + c0:f * NPAD + c0 + n], start=(f == 0), stop=(f == FT - 1))
        ins.then_inc(k.out_ready, 1)

    def flip_gelu(i, par):
        pe.wait_ge(k.gelu_done, i + 1)
        if i > 1:
            pe.wait_ge(k.x1_done, i - 1)
        for o in range(FT):
            ins = pe.transpose(k.TK[par][:, o * P:(o + 1) * P], k.gtt[par][:, o * P:(o + 1) * P], ident)
        ins.then_inc(k.tk_ready, 1)

    flip_gelu(0, 0)

    def flip_y(i, par):
        pe.wait_ge(k.y_ready, i + 1)
        for f in range(FT):
            c = par * D + f * P
            ins = pe.transpose(k.YT[:, f * P:(f + 1) * P], k.y[:, c:c + P], ident)
        ins.then_inc(k.yt_ready, 1)

    def queries(i, half):
        pe.wait_ge(k.yT_done, i + 1)
        pe.wait_ge(k.qT_done, i * H + 4 * half)
        for b in range(4):
            h = 4 * half + b
            for f in range(FT):
                ins = pe.matmul(k.Q[:, b * P:(b + 1) * P], k.wq[:, f * H * P + h * P:f * H * P + (h + 1) * P],
                                k.yT[:, f * P:(f + 1) * P], start=(f == 0), stop=(f == FT - 1))
        ins.then_inc(k.q_ready, 1)

    def scores(i, h0):
        for h in (h0, h0 + 1):
            pe.wait_ge(k.qT_done, i * H + h + 1)
            if h >= 2:
                pe.wait_ge(k.topk_done, i * H + h - 1)
            else:
                pe.wait_ge(k.topk_done, i * H)
            for c in range(2):
                half = slice(64 * c, 64 * c + 64)
                ins = pe.matmul(k.S[h % 2][c][:, 0:NK], k.qT[half, h * P:(h + 1) * P],
                                k.keys[half, h * NK:(h + 1) * NK], start=True, stop=True)
            ins.then_inc(k.s_ready, 1)

    def units(j, u0, n_units):
        pe.wait_ge(k.ht_ready, j + 1)
        for u in range(u0, u0 + n_units):
            f, c0, n = UNITS[u]
            pe.wait_ge(k.g_used, j * len(UNITS) + u + 1)
            pe.matmul(k.G[u % 2][:, 0:n], k.h1[:, f * P:(f + 1) * P], k.AT[:, bass.ds(j * NPAD + c0, n)],
                      start=True, stop=True).then_inc(k.g_ready, 1)

    pieces = {2: flip_y, 3: lambda i, p: queries(i, 0), 4: lambda i, p: queries(i, 1),
              5: lambda i, p: scores(i, 0), 6: lambda i, p: scores(i, 2), 7: lambda i, p: scores(i, 4),
              8: lambda i, p: scores(i, 6)}

    def search(i, par):
        for g in (2, 3, 5, 4, 6, 7, 8):
            pieces[g](i, par)

    def tile(i, par, ahead, behind):
        for g in range(NG):
            if ahead and g in pieces:
                pieces[g](i + 1, 1 - par)
            if behind and g >= NG - len(UNITS) // UPP:
                units(i - 1, g * UPP - FIRST_UNIT, UPP)
            pe.wait_ge(k.diag_ready, i * NG + g + 1)
            for s in range(GS):
                slot = ((g % RING) * GS + s) * 2 * D + D
                c = ((g % 2) * GS + s) * P
                ins = pe.matmul(k.O[par], k.diag[:, c:c + P], k.big[:, slot:slot + D],
                                start=(g == 0 and s == 0), stop=(g == NG - 1 and s == GS - 1))
            ins.then_inc(k.grp_done, 1)

    pe.wait_ge(k.wq_in, 16)
    pe.wait_ge(k.keys_in, 16)
    pe.sem_inc(k.grp_done, RING)
    search(0, 0)
    for i in range(1, NT):
        flip_gelu(i, i % 2)
    pe.wait_ge(k.x1_done, NT)
    tile(0, 0, True, False)
    tile(1, 1, True, True)
    with pe.Fori(1, NT // 2 - 1) as pair:
        tile(pair * 2, 0, True, True)
        tile(pair * 2 + 1, 1, True, True)
    tile(NT - 2, 0, True, True)
    tile(NT - 1, 1, False, True)

    units(NT - 1, 0, len(UNITS))
    pe.wait_ge(k.g_used, NT * len(UNITS) + 2)
    pe.wait_ge(k.x2_done, NT)
    pe.wait_ge(k.w1_in, 16 * FT)
    for t in range(NT):
        if t >= 2:
            pe.wait_ge(k.x3_done, t - 1)
        for f in range(FT):
            ins = pe.matmul(k.tr[t % 2][:, :], k.agg1[:, f * NPAD + t * P:f * NPAD + (t + 1) * P],
                            k.w1[f], start=(f == 0), stop=(f == FT - 1))
        ins.then_inc(k.g1_ready, 1)
    pe.wait_ge(k.sel_ready, 1)
    pe.wait_ge(k.e_consts, 1)
    pe.matmul(k.RK[0][:, 0:NT * BINS], k.upper, k.sel, start=True, stop=True)
    pe.matmul(k.RK[1][:, 0:NT * BINS], k.ones1, k.sel, start=True, stop=True).then_inc(k.rank_psum, 1)
    pe.wait_ge(k.pos_ready, 1)
    pe.wait_ge(k.we_in, 16 * BINS)

    def flip_z(m, r, use):
        pe.wait_ge(k.loaded[r], use * 16 + 16)
        for f in range(FT):
            ins = pe.transpose(k.ZB[r % 2][:, f * P:(f + 1) * P], k.xb[r][:, f * P:(f + 1) * P], ident)
        ins.then_inc(k.zt_ready, 1)

    def expert(m, r):
        pe.wait_ge(k.zT_done, m + 1)
        pe.wait_ge(k.x4_done, m + 1)
        b = pe.value_load(k.bini[0:1, bass.ds(m, 1)], min_val=0, max_val=BINS - 1)
        for f in range(FT):
            ins = pe.matmul(k.tr[r % 2][:, :], k.zT[r % 2][:, f * P:(f + 1) * P],
                            k.big[:, bass.ds(b * (FT * D) + f * D, D)], start=(f == 0), stop=(f == FT - 1))
        ins.then_inc(k.e_ready, 1)

    pe.wait_ge(k.rounds_ready, 1)
    rounds = pe.value_load(k.rounds[0:1, 0:1], min_val=FEWEST, max_val=ROUNDS)
    full = pe.value_load(k.rounds[0:1, 1:2], min_val=FEWEST - 1, max_val=ROUNDS - 1)
    last = pe.value_load(k.last_full[0:1, 0:1], min_val=FEWEST - 2, max_val=ROUNDS - 2)
    flip_z(0, 0, 0)
    with pe.Fori(0, last) as q:
        for r in range(XR):
            flip_z(q * XR + r + 1, (r + 1) % XR, q + (r + 1) // XR)
            expert(q * XR + r, r)
    with pe.Fori(last, full) as q:
        for r in range(XR):
            if r + 1 < XR:
                flip_z(q * XR + r + 1, r + 1, q)
            expert(q * XR + r, r)
    with pe.Fori(full, rounds) as q:
        for r in range(XR // 2):
            flip_z(q * XR + r, r, q)
        for r in range(XR // 2):
            expert(q * XR + r, r)


def kernel(**inputs):
    import concourse.bacc as _bacc
    from concourse.bass_utils import run_bass_kernel_spmd as _run

    a = {n: np.asarray(v) for n, v in inputs.items()}

    def cols(v):
        return v.reshape(-1, P).T

    arrays = {
        "in_x": a["x"], "in_src": a["src"], "in_dst": a["dst"],
        "in_w0t": a["L0_gnn_W"].T,
        "in_par": np.concatenate([cols(a["L0_gnn_b"]), cols(a["L0_gnn_gamma"]), cols(a["L0_gnn_beta"]),
                                  cols(a["L0_gnn_beta"]), cols(a["L0_ffn_bq"])], axis=1),
        "in_wq": a["L0_ffn_Wq"],
        "in_keys": a["L0_ffn_keys"].transpose(1, 3, 0, 2).reshape(P, H * NK),
        "in_wdu": np.concatenate([a["L0_ffn_w_down"], a["L0_ffn_w_up"]], axis=1),
        "in_w1": a["L1_gnn_W"], "in_b1": a["L1_gnn_b"], "in_we": a["L1_ffn_W"],
    }
    arrays = {n: np.ascontiguousarray(v) for n, v in arrays.items()}
    nc = _bacc.Bacc("TRN2", target_bir_lowering=False, num_devices=1)
    args = [nc.dram_tensor(n, v.shape, mybir.dt.from_np(v.dtype), kind="ExternalInput").ap()
            for n, v in arrays.items()]
    args.append(nc.dram_tensor("out", (N, D), F32, kind="ExternalOutput").ap())
    program(nc, *args)
    r = _run(nc, [arrays], core_ids=[0])
    return r.results[0]["out"]
```
